# Optimizing a Trainium2 kernel written in Bass

```python
import numpy as np
import jax
import jax.numpy as jnp

def _softmax(x, axis=-1):
    return jax.nn.softmax(x, axis=axis)

def _gelu(x):
    return jax.nn.gelu(x, approximate=True)

def _silu(x):
    return jax.nn.silu(x)

def _sigmoid(x):
    return jax.nn.sigmoid(x)

def _layernorm(x, axis=-1, eps=1e-05):
    m = jnp.mean(x, axis=axis, keepdims=True)
    v = jnp.var(x, axis=axis, keepdims=True)
    return (x - m) / jnp.sqrt(v + eps)

def _scatter_add(tgt, idx, src, axis=0):
    return tgt.at[idx].add(src)

def _segment_sum(src, seg, n):
    return jax.ops.segment_sum(src, seg, n)
kernel_name = 'mk_lm_tower_d2_tok_ids512_r4_6d4ae1'

def setup_inputs(seed: int=0):
    np.random.seed(seed)
    _w = jnp.asarray

    def _rec_inputs():
        import jax
        import jax.numpy as jnp
        _rk = jax.random.key(seed)
        x = jax.random.randint(jax.random.fold_in(_rk, 1), (32, 256), 0, 125, jnp.int32)
        return x
    x = _rec_inputs()

    def _L0_tok_setup():
        import jax, jax.numpy as jnp
        import numpy as np
        QMAX = 127.0
        CTX = 2

        def fake_quant(w):
            scale = jnp.max(jnp.abs(w)) / QMAX
            wq = jnp.round(w / scale) * scale
            return w + jax.lax.stop_gradient(wq - w)
        key = jax.random.key(seed)
        k1, k2, k3 = jax.random.split(key, 3)
        y = jax.random.randint(k1, (64, 512), 0, 125, dtype=jnp.int64)
        emb_weight = jax.random.normal(k2, (125, 128), dtype=jnp.float32)
        conv_weight = jax.random.normal(k3, (128, 1, 2), dtype=jnp.float32)
        return {'y': y, 'emb_weight': emb_weight, 'conv_weight': conv_weight}
    _L0_tok_all = _L0_tok_setup()
    _L0_tok_in = {k: v for k, v in _L0_tok_all.items() if k in ('emb_weight', 'conv_weight')}
    del _L0_tok_all

    def _L0_attn_setup():
        import jax, jax.numpy as jnp
        import numpy as np
        import math
        D_MODEL = 128
        NUM_HEADS = 8
        HEAD_DIM = D_MODEL // NUM_HEADS
        B, L = (2, 512)
        LN_EPS = 1e-05
        DEN_EPS = 1e-05
        key = jax.random.key(seed)
        ks = jax.random.split(key, 6)
        s = 1.0 / math.sqrt(D_MODEL)
        return {'x': jax.random.normal(ks[0], (B, L, D_MODEL), dtype=jnp.float32), 'Wqkv': jax.random.normal(ks[1], (D_MODEL, 3 * D_MODEL), dtype=jnp.float32) * s, 'bqkv': jnp.zeros((3 * D_MODEL,), dtype=jnp.float32), 'Wout': jax.random.normal(ks[2], (D_MODEL, D_MODEL), dtype=jnp.float32) * s, 'bout': jnp.zeros((D_MODEL,), dtype=jnp.float32), 'ln_gamma': jnp.ones((D_MODEL,), dtype=jnp.float32), 'ln_beta': jnp.zeros((D_MODEL,), dtype=jnp.float32), 'decay_logits': jnp.full((NUM_HEADS,), 5.0, dtype=jnp.float32)}
    _L0_attn_all = _L0_attn_setup()
    _L0_attn_in = {k: v for k, v in _L0_attn_all.items() if k in ('Wqkv', 'bqkv', 'Wout', 'bout', 'ln_gamma', 'ln_beta', 'decay_logits')}
    del _L0_attn_all

    def _L0_ffn_setup():
        import jax, jax.numpy as jnp
        import numpy as np
        G = 4
        EPG = 4
        E = 16
        KG = 2
        K = 2
        GTP = 0.9
        TP = 0.9
        SCALE = 1.0 / float(np.sqrt(G))

        def _routing_weights(xf, Wr, br, Wgate, bgate):
            N = xf.shape[0]
            gp = jax.nn.softmax(xf @ Wr + br, axis=-1)
            order = jnp.argsort(-gp, axis=-1)
            sp_k = jnp.take_along_axis(gp, order, axis=-1)[:, :KG]
            idx_k = order[:, :KG]
            act = jnp.cumsum(sp_k, axis=-1) <= GTP
            act = act.at[:, 0].set(True)
            mp = sp_k * act
            rn = mp / (jnp.sum(mp, axis=-1, keepdims=True) + 1e-09)
            w_group = jnp.zeros((N, G), xf.dtype).at[jnp.arange(N)[:, None], idx_k].set(rn)
            ep = jax.nn.softmax(jnp.einsum('nd,gde->nge', xf, Wgate) + bgate, axis=-1)
            eorder = jnp.argsort(-ep, axis=-1)
            esp = jnp.take_along_axis(ep, eorder, axis=-1)[:, :, :K]
            eidx = eorder[:, :, :K]
            eact = jnp.cumsum(esp, axis=-1) <= TP
            eact = eact.at[:, :, 0].set(True)
            emp = esp * eact
            ern = emp / (jnp.sum(emp, axis=-1, keepdims=True) + 1e-09)
            w_exp = jnp.zeros((N, G, EPG), xf.dtype).at[jnp.arange(N)[:, None, None], jnp.arange(G)[None, :, None], eidx].set(ern)
            return (w_group[:, :, None] * w_exp * SCALE).reshape(N, E)
        key = jax.random.key(seed)
        ks = jax.random.split(key, 6)
        B, T, D, H = (2, 256, 128, 512)
        x = jax.random.normal(ks[0], (B, T, D), jnp.float32)
        Wr = jax.random.normal(ks[1], (D, G), jnp.float32) * 0.02
        br = jnp.zeros((G,), jnp.float32)
        Wgate = jax.random.normal(ks[2], (G, D, EPG), jnp.float32) * 0.02
        bgate = jnp.zeros((G, EPG), jnp.float32)
        W1 = jax.random.normal(ks[3], (E, D, H), jnp.float32) * 0.02
        W3 = jax.random.normal(ks[4], (E, D, H), jnp.float32) * 0.02
        W2 = jax.random.normal(ks[5], (E, H, D), jnp.float32) * 0.02
        return {'x': x, 'Wr': Wr, 'br': br, 'Wgate': Wgate, 'bgate': bgate, 'W1': W1, 'W3': W3, 'W2': W2}
    _L0_ffn_all = _L0_ffn_setup()
    _L0_ffn_in = {k: v for k, v in _L0_ffn_all.items() if k in ('Wr', 'br', 'Wgate', 'bgate', 'W1', 'W3', 'W2')}
    del _L0_ffn_all

    def _L1_attn_setup():
        import jax, jax.numpy as jnp
        import numpy as np
        H, DH, M, DIN = (8, 64, 32, 128)
        INNER = H * DH
        key = jax.random.key(seed)
        ks = jax.random.split(key, 12)
        s = 0.02
        B, N = (4, 4096)
        return {'x': jax.random.normal(ks[0], (B, N, DIN), jnp.float32), 'Wx': jax.random.normal(ks[1], (INNER, DIN), jnp.float32) * s, 'bx': jnp.zeros((INNER,), jnp.float32), 'Wfx': jax.random.normal(ks[2], (INNER, DIN), jnp.float32) * s, 'bfx': jnp.zeros((INNER,), jnp.float32), 'Wslice': jax.random.normal(ks[3], (M, DH), jnp.float32) * s, 'bslice': jnp.zeros((M,), jnp.float32), 'Wq': jax.random.normal(ks[4], (DH, DH), jnp.float32) * s, 'Wk': jax.random.normal(ks[5], (DH, DH), jnp.float32) * s, 'Wv': jax.random.normal(ks[6], (DH, DH), jnp.float32) * s, 'Wout': jax.random.normal(ks[7], (DIN, INNER), jnp.float32) * s, 'bout': jnp.zeros((DIN,), jnp.float32), 'temperature': jnp.full((1, H, 1, 1), 0.5, jnp.float32)}
    _L1_attn_all = _L1_attn_setup()
    _L1_attn_in = {k: v for k, v in _L1_attn_all.items() if k in ('Wx', 'bx', 'Wfx', 'bfx', 'Wslice', 'bslice', 'Wq', 'Wk', 'Wv', 'Wout', 'bout', 'temperature')}
    del _L1_attn_all

    def _L1_ffn_setup():
        import jax, jax.numpy as jnp
        import numpy as np
        EPS = 1e-06
        SINKHORN_ITERS = 8
        TEMPERATURE = 1.0
        B, N, D = (4, 2048, 128)
        E, OUT = (8, 128)
        H = 1

        def _sinkhorn(logits):
            t = jnp.log(jnp.clip(logits, EPS)) / TEMPERATURE
            for _ in range(SINKHORN_ITERS):
                t = t - jax.nn.logsumexp(t, axis=-2, keepdims=True)
                t = t - jax.nn.logsumexp(t, axis=-1, keepdims=True)
            return jnp.exp(t)
        key = jax.random.key(seed)
        k1, k2, k3 = jax.random.split(key, 3)
        x = jax.random.normal(k1, (B, N, D), dtype=jnp.float32)
        gate_weight = jax.random.normal(k2, (H, D, E), dtype=jnp.float32)
        experts = jax.random.normal(k3, (E, D, OUT), dtype=jnp.float32) * 0.02
        return {'x': x, 'gate_weight': gate_weight, 'experts': experts}
    _L1_ffn_all = _L1_ffn_setup()
    _L1_ffn_in = {k: v for k, v in _L1_ffn_all.items() if k in ('gate_weight', 'experts')}
    del _L1_ffn_all
    return {'x': x, 'L0_tok_emb_weight': _L0_tok_in['emb_weight'], 'L0_tok_conv_weight': _L0_tok_in['conv_weight'], 'L0_attn_Wqkv': _L0_attn_in['Wqkv'], 'L0_attn_bqkv': _L0_attn_in['bqkv'], 'L0_attn_Wout': _L0_attn_in['Wout'], 'L0_attn_bout': _L0_attn_in['bout'], 'L0_attn_ln_gamma': _L0_attn_in['ln_gamma'], 'L0_attn_ln_beta': _L0_attn_in['ln_beta'], 'L0_attn_decay_logits': _L0_attn_in['decay_logits'], 'L0_ffn_Wr': _L0_ffn_in['Wr'], 'L0_ffn_br': _L0_ffn_in['br'], 'L0_ffn_Wgate': _L0_ffn_in['Wgate'], 'L0_ffn_bgate': _L0_ffn_in['bgate'], 'L0_ffn_W1': _L0_ffn_in['W1'], 'L0_ffn_W3': _L0_ffn_in['W3'], 'L0_ffn_W2': _L0_ffn_in['W2'], 'L1_attn_Wx': _L1_attn_in['Wx'], 'L1_attn_bx': _L1_attn_in['bx'], 'L1_attn_Wfx': _L1_attn_in['Wfx'], 'L1_attn_bfx': _L1_attn_in['bfx'], 'L1_attn_Wslice': _L1_attn_in['Wslice'], 'L1_attn_bslice': _L1_attn_in['bslice'], 'L1_attn_Wq': _L1_attn_in['Wq'], 'L1_attn_Wk': _L1_attn_in['Wk'], 'L1_attn_Wv': _L1_attn_in['Wv'], 'L1_attn_Wout': _L1_attn_in['Wout'], 'L1_attn_bout': _L1_attn_in['bout'], 'L1_attn_temperature': _L1_attn_in['temperature'], 'L1_ffn_gate_weight': _L1_ffn_in['gate_weight'], 'L1_ffn_experts': _L1_ffn_in['experts']}

def reference(x, L0_tok_emb_weight, L0_tok_conv_weight, L0_attn_Wqkv, L0_attn_bqkv, L0_attn_Wout, L0_attn_bout, L0_attn_ln_gamma, L0_attn_ln_beta, L0_attn_decay_logits, L0_ffn_Wr, L0_ffn_br, L0_ffn_Wgate, L0_ffn_bgate, L0_ffn_W1, L0_ffn_W3, L0_ffn_W2, L1_attn_Wx, L1_attn_bx, L1_attn_Wfx, L1_attn_bfx, L1_attn_Wslice, L1_attn_bslice, L1_attn_Wq, L1_attn_Wk, L1_attn_Wv, L1_attn_Wout, L1_attn_bout, L1_attn_temperature, L1_ffn_gate_weight, L1_ffn_experts):
    import jax
    import jax.numpy as jnp

    def _L0_tok_ref(y, emb_weight, conv_weight):
        import jax, jax.numpy as jnp
        import numpy as np
        QMAX = 127.0
        CTX = 2

        def fake_quant(w):
            scale = jnp.max(jnp.abs(w)) / QMAX
            wq = jnp.round(w / scale) * scale
            return w + jax.lax.stop_gradient(wq - w)
        w_emb = fake_quant(emb_weight)
        e = w_emb[jnp.clip(y, 0)]
        e = e * (y >= 0)[..., None].astype(e.dtype)
        x = jnp.pad(e, ((0, 0), (CTX - 1, 0), (0, 0)))
        D = conv_weight.shape[0]
        w = fake_quant(conv_weight).transpose(2, 1, 0)
        out = jax.lax.conv_general_dilated(x, w, window_strides=(1,), padding='VALID', feature_group_count=D, dimension_numbers=('NWC', 'WIO', 'NWC'))
        return jax.nn.relu(out)

    def _L0_attn_ref(x, Wqkv, bqkv, Wout, bout, ln_gamma, ln_beta, decay_logits):
        import jax, jax.numpy as jnp
        import numpy as np
        import math
        D_MODEL = 128
        NUM_HEADS = 8
        HEAD_DIM = D_MODEL // NUM_HEADS
        B, L = (2, 512)
        LN_EPS = 1e-05
        DEN_EPS = 1e-05
        Bv, Lv, D = x.shape
        H = decay_logits.shape[0]
        E = D // H
        qkv = x @ Wqkv + bqkv
        q, k, v = jnp.split(qkv, 3, axis=-1)
        q = q.reshape(Bv, Lv, H, E)
        k = k.reshape(Bv, Lv, H, E)
        v = v.reshape(Bv, Lv, H, E)
        q = (jax.nn.elu(q) + 1.0) / jnp.sqrt(jnp.asarray(E, x.dtype))
        k = jax.nn.elu(k) + 1.0
        lambdas = jax.nn.sigmoid(decay_logits).reshape(1, 1, H, 1)
        t = jnp.arange(Lv, dtype=x.dtype).reshape(1, Lv, 1, 1)
        decay_k = jnp.power(lambdas, -t)
        decay_q = jnp.power(lambdas, t)
        k_dec = k * decay_k
        kv = jnp.einsum('blhe,blhf->blhef', k_dec, v)
        memory = jnp.cumsum(kv, axis=1)
        k_sum = jnp.cumsum(k_dec, axis=1)
        q_dec = q * decay_q
        num = jnp.einsum('blhe,blhef->blhf', q_dec, memory)
        den = jnp.einsum('blhe,blhe->blh', q_dec, k_sum)[..., None] + DEN_EPS
        out = (num / den).reshape(Bv, Lv, D)
        out = out @ Wout + bout
        mu = jnp.mean(out, axis=-1, keepdims=True)
        var = jnp.var(out, axis=-1, keepdims=True)
        out = (out - mu) / jnp.sqrt(var + LN_EPS) * ln_gamma + ln_beta
        return out

    def _L0_ffn_ref(x, Wr, br, Wgate, bgate, W1, W3, W2):
        import jax, jax.numpy as jnp
        import numpy as np
        G = 4
        EPG = 4
        E = 16
        KG = 2
        K = 2
        GTP = 0.9
        TP = 0.9
        SCALE = 1.0 / float(np.sqrt(G))

        def _routing_weights(xf, Wr, br, Wgate, bgate):
            N = xf.shape[0]
            gp = jax.nn.softmax(xf @ Wr + br, axis=-1)
            order = jnp.argsort(-gp, axis=-1)
            sp_k = jnp.take_along_axis(gp, order, axis=-1)[:, :KG]
            idx_k = order[:, :KG]
            act = jnp.cumsum(sp_k, axis=-1) <= GTP
            act = act.at[:, 0].set(True)
            mp = sp_k * act
            rn = mp / (jnp.sum(mp, axis=-1, keepdims=True) + 1e-09)
            w_group = jnp.zeros((N, G), xf.dtype).at[jnp.arange(N)[:, None], idx_k].set(rn)
            ep = jax.nn.softmax(jnp.einsum('nd,gde->nge', xf, Wgate) + bgate, axis=-1)
            eorder = jnp.argsort(-ep, axis=-1)
            esp = jnp.take_along_axis(ep, eorder, axis=-1)[:, :, :K]
            eidx = eorder[:, :, :K]
            eact = jnp.cumsum(esp, axis=-1) <= TP
            eact = eact.at[:, :, 0].set(True)
            emp = esp * eact
            ern = emp / (jnp.sum(emp, axis=-1, keepdims=True) + 1e-09)
            w_exp = jnp.zeros((N, G, EPG), xf.dtype).at[jnp.arange(N)[:, None, None], jnp.arange(G)[None, :, None], eidx].set(ern)
            return (w_group[:, :, None] * w_exp * SCALE).reshape(N, E)
        B, T, D = x.shape
        xf = x.reshape(-1, D)
        tw = _routing_weights(xf, Wr, br, Wgate, bgate)
        out = jnp.zeros_like(xf)
        for e in range(E):
            h = jax.nn.silu(xf @ W1[e]) * (xf @ W3[e])
            out = out + tw[:, e:e + 1] * (h @ W2[e])
        return out.reshape(B, T, D)

    def _L1_attn_ref(x, Wx, bx, Wfx, bfx, Wslice, bslice, Wq, Wk, Wv, Wout, bout, temperature):
        import jax, jax.numpy as jnp
        import numpy as np
        H, DH, M, DIN = (8, 64, 32, 128)
        INNER = H * DH
        B, N, D = x.shape
        scale = DH ** (-0.5)
        x_mid = (x @ Wx.T + bx).reshape(B, N, H, DH).transpose(0, 2, 1, 3)
        fx_mid = (x @ Wfx.T + bfx).reshape(B, N, H, DH).transpose(0, 2, 1, 3)
        slice_logits = (x_mid @ Wslice.T + bslice) / temperature
        slice_weights = jax.nn.softmax(slice_logits, axis=-1)
        slice_norm = slice_weights.sum(axis=2)
        slice_token = jnp.einsum('bhnd,bhnm->bhmd', fx_mid, slice_weights)
        slice_token = slice_token / (slice_norm[:, :, :, None] + 1e-05)
        q = slice_token @ Wq.T
        k = slice_token @ Wk.T
        v = slice_token @ Wv.T
        attn = jax.nn.softmax(jnp.einsum('bhmd,bhkd->bhmk', q, k) * scale, axis=-1)
        out_slice = jnp.einsum('bhmk,bhkd->bhmd', attn, v)
        out_x = jnp.einsum('bhmd,bhnm->bhnd', out_slice, slice_weights)
        out_x = out_x.transpose(0, 2, 1, 3).reshape(B, N, INNER)
        return out_x @ Wout.T + bout

    def _L1_ffn_ref(x, gate_weight, experts):
        import jax, jax.numpy as jnp
        import numpy as np
        EPS = 1e-06
        SINKHORN_ITERS = 8
        TEMPERATURE = 1.0
        B, N, D = (4, 2048, 128)
        E, OUT = (8, 128)
        H = 1

        def _sinkhorn(logits):
            t = jnp.log(jnp.clip(logits, EPS)) / TEMPERATURE
            for _ in range(SINKHORN_ITERS):
                t = t - jax.nn.logsumexp(t, axis=-2, keepdims=True)
                t = t - jax.nn.logsumexp(t, axis=-1, keepdims=True)
            return jnp.exp(t)
        b, n, d = x.shape
        e = experts.shape[0]
        m = n // e
        xh = x[:, None, :, :]
        gate_logits = jnp.einsum('bhnd,hde->bhne', xh, gate_weight)
        gates = _sinkhorn(gate_logits)
        g_t = jnp.swapaxes(gates, -1, -2)
        vals, idx = jax.lax.top_k(g_t, m)
        gate_values = jnp.transpose(vals, (2, 0, 1, 3))[..., None]
        routed = jnp.take_along_axis(xh[:, :, None, :, :], idx[..., None], axis=3)
        routed = jnp.transpose(routed, (2, 0, 1, 3, 4))
        expert_w = experts[:, None, :, :]
        outputs = jnp.einsum('ebhmi,ehio->ebhmo', routed, expert_w)
        outputs = outputs * gate_values
        bh_idx = idx.reshape(b, 1, e * m)
        bh_vals = jnp.transpose(outputs, (1, 2, 0, 3, 4)).reshape(b, 1, e * m, outputs.shape[-1])

        def scat(i1, v1):
            return jnp.zeros((n, v1.shape[-1]), dtype=v1.dtype).at[i1].set(v1)
        routed_back = jax.vmap(jax.vmap(scat))(bh_idx, bh_vals)
        return routed_back[:, 0]
    h = _L0_tok_ref(x, L0_tok_emb_weight, L0_tok_conv_weight)
    h = h + _L0_attn_ref(_layernorm(h, axis=-1), L0_attn_Wqkv, L0_attn_bqkv, L0_attn_Wout, L0_attn_bout, L0_attn_ln_gamma, L0_attn_ln_beta, L0_attn_decay_logits)
    h = h + _L0_ffn_ref(_layernorm(h, axis=-1), L0_ffn_Wr, L0_ffn_br, L0_ffn_Wgate, L0_ffn_bgate, L0_ffn_W1, L0_ffn_W3, L0_ffn_W2)
    h = h + _L1_attn_ref(_layernorm(h, axis=-1), L1_attn_Wx, L1_attn_bx, L1_attn_Wfx, L1_attn_bfx, L1_attn_Wslice, L1_attn_bslice, L1_attn_Wq, L1_attn_Wk, L1_attn_Wv, L1_attn_Wout, L1_attn_bout, L1_attn_temperature)
    h = h + _L1_ffn_ref(_layernorm(h, axis=-1), L1_ffn_gate_weight, L1_ffn_experts)
    return h

_drawn_inputs = setup_inputs


def setup_inputs(seed=0):
    import zlib

    import numpy as np

    out = dict(_drawn_inputs(seed))
    spreads = {'L0_attn_bqkv': (0.0, 0.1),
     'L0_attn_bout': (0.0, 0.1),
     'L0_attn_ln_gamma': (1.0, 0.2),
     'L0_attn_ln_beta': (0.0, 0.1),
     'L0_attn_decay_logits': (5.0, 0.2),
     'L0_ffn_br': (0.0, 0.8),
     'L0_ffn_bgate': (0.0, 0.8),
     'L1_attn_bx': (0.0, 0.8),
     'L1_attn_bfx': (0.0, 0.8),
     'L1_attn_bslice': (0.0, 2.0),
     'L1_attn_bout': (0.0, 0.269),
     'L1_attn_temperature': (0.5, 0.6)}
    factors = {'L0_ffn_Wr': 8.0,
     'L0_ffn_Wgate': 8.0,
     'L0_ffn_W1': 8.0,
     'L0_ffn_W3': 8.0,
     'L0_ffn_W2': 8.0,
     'L1_attn_Wx': 8.0,
     'L1_attn_Wfx': 4.472,
     'L1_attn_Wslice': 8.0,
     'L1_attn_Wq': 8.0,
     'L1_attn_Wk': 8.0,
     'L1_attn_Wv': 4.001,
     'L1_attn_Wout': 4.29}
    for name, (base, spread) in spreads.items():
        noise = np.random.default_rng([zlib.crc32(name.encode()), seed]).standard_normal(out[name].shape)
        drawn = base * np.exp(spread * noise) if base else spread * noise
        out[name] = jnp.asarray(drawn.astype(out[name].dtype))
    for name, factor in factors.items():
        out[name] = (out[name] * factor).astype(out[name].dtype)
    return out
```

```python
from contextlib import ExitStack

import concourse.bass as bass
from concourse import mybir

ALU = mybir.AluOpType
ACT = mybir.ActivationFunctionType
AX = mybir.AxisListType
F32 = mybir.dt.float32
I32 = mybir.dt.int32
RMAX = bass.bass_isa.ReduceOp.max



P = 128
D = 128
BATCH, SEQ = 32, 256
VOCAB = 125
TILES = BATCH * SEQ // P
TPG = 4
GROUPS = TILES // TPG
GT = TPG * P
HEADS0, E0 = 8, 16
ROUND = 12582912.0
LN_EPS = 1e-5
GRP, EXPERTS, HID = 4, 16, 512
TOP_P = 0.9
HEADS1, DH1, SLICES = 8, 64, 32
GATES, SINKHORN, GATE_EPS = 8, 8, 1e-6


def dyn(i, n):
    return bass.ds(i, n)


def layer_stats(nc, ctx, stats, mean, rstd, eps_t, tag):
    tmp = ctx.enter_context(nc.sbuf_tensor(f"ln_tmp_{tag}", [P, 3, TILES], F32))
    s_v = ctx.enter_context(nc.semaphore(f"s_ln_vec_{tag}"))
    s_sq = ctx.enter_context(nc.semaphore(f"s_ln_sqrt_{tag}"))

    with nc.Block() as block:
        @block.vector
        def _(dve):
            m_even, m_odd = stats[:, :, 1], stats[:, :, 4]
            nc.vector.tensor_tensor(tmp[:, 0, :], m_even, m_odd, ALU.subtract).then_inc(s_v, 1)
            nc.vector.tensor_tensor(tmp[:, 1, :], m_even, m_odd, ALU.add).then_inc(s_v, 1)
            nc.vector.tensor_tensor(tmp[:, 2, :], stats[:, :, 2], stats[:, :, 5], ALU.add).then_inc(s_v, 1)
            dve.wait_ge(s_v, 3)
            nc.vector.tensor_scalar(mean[:, :], tmp[:, 1, :], 0.5, None, ALU.mult).then_inc(s_v, 1)
            nc.vector.scalar_tensor_tensor(tmp[:, 0, :], tmp[:, 0, :], 0.25, tmp[:, 0, :],
                                           ALU.mult, ALU.mult).then_inc(s_v, 1)
            dve.wait_ge(s_v, 5)
            nc.vector.scalar_tensor_tensor(tmp[:, 2, :], tmp[:, 2, :], 1.0 / D, tmp[:, 0, :],
                                           ALU.mult, ALU.add).then_inc(s_v, 1)
            dve.wait_ge(s_sq, 1)
            nc.vector.reciprocal(rstd[:, :], tmp[:, 1, :]).then_inc(s_v, 1)

        @block.scalar
        def _(act):
            act.wait_ge(s_v, 6)
            nc.scalar.activation(tmp[:, 1, :], tmp[:, 2, :], ACT.Sqrt, bias=eps_t[:, 0:1]).then_inc(s_sq, 1)


def tower(nc, t, out):
    ctx = ExitStack()
    with ctx:
        def sbp(c, name, shape, dt=F32):
            return c.enter_context(nc.sbuf_tensor(name, shape, dt))

        def sem(c, name):
            return c.enter_context(nc.semaphore(name))

        h = sbp(ctx, "h", [P, TILES, D])
        stats = sbp(ctx, "stats", [P, TILES, 6])
        mean = sbp(ctx, "mean", [P, TILES])
        rstd = sbp(ctx, "rstd", [P, TILES])
        ident = sbp(ctx, "ident", [P, P])
        causal = sbp(ctx, "causal", [P, P])
        iota_p = sbp(ctx, "iota_p", [P, 1])
        eps_t = sbp(ctx, "eps_t", [P, 1])
        bank = [ctx.enter_context(nc.psum_tensor(f"bank{i}", [P, 512], F32)) for i in range(8)]

        s_setup = sem(ctx, "s_setup")
        with nc.Block() as block:
            @block.gpsimd
            def _(pool):
                nc.gpsimd.memset(ident[:, :], 0.0).then_inc(s_setup, 1)
                nc.gpsimd.memset(causal[:, :], 1.0).then_inc(s_setup, 1)
                pool.wait_ge(s_setup, 2)
                nc.gpsimd.affine_select(out=ident[:, :], in_=ident[:, :], compare_op=ALU.not_equal, fill=1.0,
                                        base=0, pattern=[[-1, P]], channel_multiplier=1).then_inc(s_setup, 1)
                nc.gpsimd.affine_select(out=causal[:, :], in_=causal[:, :], compare_op=ALU.is_ge, fill=0.0,
                                        base=0, pattern=[[1, P]], channel_multiplier=-1).then_inc(s_setup, 1)
                nc.gpsimd.iota(iota_p[:, :], pattern=[[0, 1]], base=0, channel_multiplier=1,
                               allow_small_or_imprecise_dtypes=True).then_inc(s_setup, 1)
                nc.gpsimd.memset(eps_t[:, :], LN_EPS).then_inc(s_setup, 1)

        cw = ExitStack()
        if True:
            w1 = sbp(cw, "w1", [P, EXPERTS, HID])
            w3 = sbp(cw, "w3", [P, EXPERTS, HID])
            s_wts = [sem(cw, f"s_wts{k}") for k in range(4)]
            with nc.Block() as block:
                @block.sync
                def _(sp):
                    for k in range(4):
                        e = slice(4 * k, 4 * k + 4)
                        sp.dma_start(w1[:, e, :], t["w1"][e].rearrange("e d f -> d e f")).then_inc(s_wts[k], 16)
                        sp.dma_start(w3[:, e, :], t["w3"][e].rearrange("e d f -> d e f")).then_inc(s_wts[k], 16)
        with ExitStack() as c:
            embed_phase(nc, c, t, h, stats, bank, iota_p)
        if True:
            with ExitStack() as c:
                layer_stats(nc, c, stats, mean, rstd, eps_t, "a0")
                attention_phase(nc, c, t, h, stats, mean, rstd, bank, ident, causal, eps_t)

        if True:
            with ExitStack() as c:
                layer_stats(nc, c, stats, mean, rstd, eps_t, "b0")
                xt_all = sbp(c, "xt_all", [P, TILES * P])
                tw = sbp(c, "tw", [P, TILES, EXPERTS])
                w2 = sbp(c, "w2", [P, EXPERTS, HID // P, D])
                with nc.Block() as block:
                    @block.sync
                    def _(sp):
                        for k in range(4):
                            e = slice(4 * k, 4 * k + 4)
                            sp.dma_start(w2[:, e, :, :], t["w2"][e].rearrange("e (c p) d -> p e c d", p=P))\
                                .then_inc(s_wts[k], 16)

                with ExitStack() as c2:
                    routing_phase(nc, c2, t, h, mean, rstd, bank, ident, xt_all, tw)
                with ExitStack() as c2:
                    ffn_phase(nc, c2, h, bank, w1, w3, w2, s_wts, xt_all, tw, stats)
        cw.close()
        if True:
            with ExitStack() as c:
                layer_stats(nc, c, stats, mean, rstd, eps_t, "c0")
                slice_attention_phase(nc, c, t, h, stats, mean, rstd, bank, ident)
        if True:
            with ExitStack() as c:
                layer_stats(nc, c, stats, mean, rstd, eps_t, "d0")
                expert_choice_phase(nc, c, t, h, mean, rstd, bank, ident)

        s_out = sem(ctx, "s_out")
        with nc.Block() as block:
            @block.sync
            def _(sp):
                ov = out.rearrange("(t p) d -> p t d", p=P)
                for q in range(4):
                    n = TILES // 4
                    sp.dma_start(ov[:, q * n:(q + 1) * n, :], h[:, q * n:(q + 1) * n, :]).then_inc(s_out, 16)
                sp.wait_ge(s_out, 64)


def embed_phase(nc, c, t, h, stats, bank, iota_p):
    def sb(name, shape, dt=F32):
        return c.enter_context(nc.sbuf_tensor(name, shape, dt))

    def sem(name):
        return c.enter_context(nc.semaphore(name))

    TAPS = 2
    ids = sb("ids", [P, BATCH, SEQ], I32)
    emb = sb("emb", [P, D])
    taps = sb("taps", [P, TAPS, D])
    work = sb("q_work", [P, 3, TAPS, D])
    amax = sb("amax", [P, 8])
    table = sb("table", [P, TAPS, D])
    onehot = sb("onehot", [P, 2, 2, SEQ + 1])

    s_in = sem("s_emb_in")
    s_ids = [sem(f"s_ids{q}") for q in range(4)]
    s_zero = sem("s_emb_zero")
    s_q = sem("s_quant")
    s_amax = sem("s_amax")
    s_oh = sem("s_onehot")
    s_rows = sem("s_emb_rows")
    s_h = sem("s_emb_h")
    s_st = sem("s_emb_stats")

    with nc.Block() as block:
        @block.sync
        def _(sp):
            sp.wait_ge(s_zero, 1)
            sp.dma_start(emb[0:VOCAB, :], t["emb"]).then_inc(s_in, 16)
            sp.dma_start(taps[:, :, :], t["conv"].partition_broadcast(P)).then_inc(s_in, 16)
            for q in range(4):
                n = BATCH // 4
                sp.dma_start(ids[:, q * n:(q + 1) * n, :],
                             t["x"][q * n:(q + 1) * n, :].partition_broadcast(P)).then_inc(s_ids[q], 16)

        @block.gpsimd
        def _(pool):
            nc.gpsimd.memset(emb[:, :], 0.0).then_inc(s_zero, 1)
            nc.gpsimd.memset(onehot[:, :, :, :], 0.0).then_inc(s_zero, 1)
            for k in range(2):
                pool.wait_ge(s_q, 2 * k + 2)
                nc.gpsimd.partition_all_reduce(amax[:, 2 + k:3 + k], amax[:, k:k + 1], P, RMAX).then_inc(s_amax, 1)

        @block.vector
        def _(dve):
            count = [0]

            def step(ins):
                count[0] += 1
                ins.then_inc(s_q, 1)
                dve.wait_ge(s_q, count[0])

            dve.wait_ge(s_in, 32)
            mats = [(emb[:, :], work[:, 0, 0, :], work[:, 1, 0, :]),
                    (taps[:, :, :], work[:, 0, :, :], work[:, 1, :, :])]
            for k, (w, a, _) in enumerate(mats):
                step(nc.vector.scalar_tensor_tensor(a, w, -1.0, w, ALU.mult, ALU.max))
                step(nc.vector.tensor_reduce(amax[:, k:k + 1], a, AX.X if k == 0 else AX.XY, ALU.max))
            for k, (w, a, b) in enumerate(mats):
                dve.wait_ge(s_amax, k + 1)
                scale, inv = amax[:, 4 + k:5 + k], amax[:, 6 + k:7 + k]
                step(nc.vector.tensor_scalar(scale, amax[:, 2 + k:3 + k], 1.0 / 127.0, None, ALU.mult))
                step(nc.vector.reciprocal(inv, scale))
                step(nc.vector.tensor_scalar(a, w, inv, ROUND, ALU.mult, ALU.add))
                step(nc.vector.tensor_scalar(a, a, ROUND, scale, ALU.subtract, ALU.mult))
                step(nc.vector.tensor_tensor(b, a, w, ALU.subtract))
                step(nc.vector.tensor_tensor(w, w, b, ALU.add))
            for k in range(TAPS):
                step(nc.vector.tensor_tensor(table[:, k, :], emb[:, :], taps[:, k, :], ALU.mult))

            dve.wait_ge(s_zero, 2)
            for q in range(4):
                dve.wait_ge(s_ids[q], 16)
            with dve.Fori(0, GROUPS // 2) as i:
                for u in range(2):
                    g = 2 * i + u
                    dve.wait_ge(s_rows, TPG * g + TPG)
                    nc.vector.tensor_scalar(onehot[:, u, :, 1:SEQ + 1], ids[:, dyn(2 * g, 2), :], float(VOCAB - 1),
                                            iota_p[:, 0:1], ALU.min, ALU.is_equal).then_inc(s_oh, 1)
                for u in range(2):
                    for j in range(TPG):
                        tile = (2 * i + u) * TPG + j
                        dve.wait_ge(s_h, tile + 1 + 2 * TPG)
                        nc.vector.bn_stats(stats[:, dyn(tile, 1), :], h[:, dyn(tile, 1), :]).then_inc(s_st, 1)

        @block.tensor
        def _(pe):
            pe.sem_inc(s_rows, 2 * TPG)
            pe.wait_ge(s_q, 18)
            with pe.Fori(0, GROUPS // 2) as i:
                for u in range(2):
                    g = 2 * i + u
                    pe.wait_ge(s_oh, g + 1)
                    for j in range(TPG):
                        b, at = j // 2, (j % 2) * P
                        pe.wait_ge(s_h, g * TPG + j + 1)
                        for k in range(TAPS):
                            mm = nc.tensor.matmul(bank[u * TPG + j][:, 0:D], onehot[:, u, b, at + k:at + k + P],
                                                  table[:, k, :], start=(k == 0), stop=(k == TAPS - 1))
                        mm.then_inc(s_rows, 1)

        @block.scalar
        def _(act):
            act.sem_inc(s_h, 2 * TPG)
            with act.Fori(0, GROUPS // 2) as i:
                for u in range(2):
                    g = 2 * i + u
                    for j in range(TPG):
                        act.wait_ge(s_rows, g * TPG + j + 1 + 2 * TPG)
                        nc.scalar.activation(h[:, dyn(g * TPG + j, 1), :], bank[u * TPG + j][:, 0:D],
                                             ACT.Relu).then_inc(s_h, 1)


def attention_phase(nc, c, t, h, stats, mean, rstd, bank, ident, causal, eps_t):
    def sb(name, shape, dt=F32):
        return c.enter_context(nc.sbuf_tensor(name, shape, dt))

    def sem(name):
        return c.enter_context(nc.semaphore(name))

    H, E, R, V = HEADS0, E0, 4, E0 + 1
    NQK = 4
    wqk = sb("wqk", [P, NQK, P])
    bqk = sb("bqk", [P, 2, NQK])
    wv = sb("wv", [P, D])
    wo = sb("wo", [P, D])
    rows = sb("rows0", [P, 4, D])
    lam = sb("lam", [P, 2])
    valid = sb("valid", [P, 2])
    powr = sb("powr", [P, 9, 2])
    decay = sb("decay", [P, 4, SEQ])
    bdiag = sb("bdiag", [P, 2, R, V])

    o_all = sb("o_all", [P, TILES, D])
    xn = sb("xn", [P, 2, TPG, D])
    xt = sb("xt", [P, 2, GT])
    ebuf = sb("ebuf", [P, 2, GT])
    xbuf = sb("xbuf", [P, 2, GT])
    qk = sb("qk", [P, 2, NQK, GT])
    v1 = sb("v1", [P, 2, TPG, H, V])
    ktok = sb("ktok", [P, 2 * P])
    state = sb("state", [P, 2, R * V])
    prob = sb("prob", [P, R, 4, P])
    den = sb("den", [P, 2, H])
    on = sb("on", [P, 2, D])
    ot = sb("ot", [P, 2 * P])
    off = sb("off", [P, 2, D])

    s_w = sem("s_a_weights")
    s_c = sem("s_a_consts")
    s_pool = sem("s_a_pool")
    names = ("xn", "xt_p", "xt", "qk_p", "qk_e", "qk", "v_p", "v", "kt_p", "kt", "st_p", "st", "sc_p", "sc",
             "pv_p", "den", "on", "ot_p", "ot", "o_p", "o", "stat")
    S = {n: sem("s_a_" + n) for n in names}

    with nc.Block() as block:
        @block.sync
        def _(sp):
            sp.dma_start(wqk[:, :, :], t["wqk"]).then_inc(s_w, 16)
            sp.dma_start(bqk[:, 0, :], t["bqk"]).then_inc(s_w, 16)
            sp.dma_start(wv[:, :], t["wv"]).then_inc(s_w, 16)
            sp.dma_start(wo[:, :], t["wo"]).then_inc(s_w, 16)
            sp.dma_start(rows[:, :, :], t["rows0"].partition_broadcast(P)).then_inc(s_w, 16)
            sp.dma_start(lam[:, :], t["lam"]).then_inc(s_w, 16)

        @block.gpsimd
        def _(pool):
            nc.gpsimd.memset(valid[:, 0:1], 0.0).then_inc(s_pool, 1)
            nc.gpsimd.memset(valid[:, 1:2], 1.0).then_inc(s_pool, 1)
            nc.gpsimd.memset(bdiag[:, :, :, :], 0.0).then_inc(s_pool, 1)
            nc.gpsimd.memset(v1[:, :, :, :, :], 1.0).then_inc(s_pool, 1)
            pool.wait_ge(s_pool, 4)
            for r in range(R):
                nc.gpsimd.memset(valid[32 * r:32 * r + E, 0:1], 1.0).then_inc(s_pool, 1)
                nc.gpsimd.memset(valid[32 * r:32 * r + E, 1:2], 0.0).then_inc(s_pool, 1)
                nc.gpsimd.memset(bdiag[32 * r:32 * r + 32, :, r, :], 1.0).then_inc(s_pool, 1)

        @block.scalar
        def _(act):
            act.wait_ge(s_w, 96)
            nc.scalar.activation(powr[:, 8, :], lam[:, :], ACT.Exp, scale=-1.0).then_inc(s_c, 1)

        @block.vector
        def _(dve):
            count = [1]

            def step(ins):
                count[0] += 1
                ins.then_inc(s_c, 1)
                dve.wait_ge(s_c, count[0])

            dve.wait_ge(s_pool, 4 + 3 * R)
            dve.wait_ge(s_c, 1)
            step(nc.vector.tensor_scalar(powr[:, 8, :], powr[:, 8, :], 1.0, None, ALU.add))
            step(nc.vector.reciprocal(lam[:, :], powr[:, 8, :]))
            step(nc.vector.tensor_scalar(powr[:, 0, :], lam[:, :], valid[:, 0:1], valid[:, 1:2], ALU.mult, ALU.add))
            step(nc.vector.memset(decay[:, :, 0:1], 1.0))
            for k in range(8):
                n = 1 << k
                for i in range(2):
                    step(nc.vector.tensor_scalar(decay[:, i, n:2 * n], decay[:, i, 0:n], powr[:, k, i:i + 1],
                                                 None, ALU.mult))
                step(nc.vector.tensor_tensor(powr[:, k + 1, :], powr[:, k, :], powr[:, k, :], ALU.mult))
            step(nc.vector.reciprocal(decay[:, 2:4, :], decay[:, 0:2, :]))
            step(nc.vector.tensor_scalar(decay[:, 0:2, :], decay[:, 0:2, :], E ** -0.5, valid[:, 0:1],
                                         ALU.mult, ALU.mult))
            step(nc.vector.tensor_scalar(decay[:, 2:4, :], decay[:, 2:4, :], valid[:, 0:1], None, ALU.mult))
            step(nc.vector.tensor_scalar(bqk[:, 1, :], bqk[:, 0, :], 1.0, None, ALU.add))

    with nc.Block() as block:
        @block.vector
        def _(dve):
            dve.sem_inc(S["qk"], 2)
            dve.sem_inc(S["v"], 1)
            dve.sem_inc(S["o"], 1)
            with dve.Fori(0, GROUPS // 2) as i:
                for u in range(2):
                    g = 2 * i + u
                    dve.wait_ge(S["xt_p"], g + 1)
                    for j in range(TPG):
                        ins = nc.vector.tensor_scalar(xn[:, u, j, :], h[:, dyn(g * TPG + j, 1), :],
                                                      mean[:, dyn(g * TPG + j, 1)], rstd[:, dyn(g * TPG + j, 1)],
                                                      ALU.subtract, ALU.mult)
                    ins.then_inc(S["xn"], 1)
                    for j in range(NQK):
                        dve.wait_ge(S["qk_e"], NQK * g + j + 1 + 2)
                        nc.vector.scalar_tensor_tensor(ebuf[:, j % 2, :], ebuf[:, j % 2, :], 1.0, xbuf[:, j % 2, :],
                                                       ALU.min, ALU.max).then_inc(S["den"], 1)
                        dve.wait_ge(S["den"], g * (NQK + 4) + j + 1)
                        if j == 0:
                            dve.wait_ge(S["pv_p"], 2 * g + 1)
                        nc.vector.tensor_tensor(
                            qk[:, u, j, :].rearrange("p (b t) -> p b t", b=2),
                            ebuf[:, j % 2, :].rearrange("p (b t) -> p b t", b=2),
                            decay[:, j:j + 1, :].broadcast_to([P, 2, SEQ]), ALU.mult).then_inc(S["qk"], 1)
                    dve.wait_ge(S["v_p"], g + 1)
                    nc.vector.tensor_tensor(v1[:, u, :, :, 0:E],
                                            bank[3][:, :].rearrange("p (t h e) -> p t h e", t=TPG, h=H),
                                            rows[:, 0:1, :].rearrange("p o (h e) -> p o h e", h=H)
                                            .broadcast_to([P, TPG, H, E]), ALU.add).then_inc(S["v"], 1)
                    for b in range(2):
                        n = 2 * g + b
                        dve.wait_ge(S["st_p"], n + 1)
                        nc.vector.tensor_tensor(state[:, :, :], bank[2][:, 0:2 * R * V].rearrange("p (i c) -> p i c", i=2),
                                                bdiag[:, :, :, :].rearrange("p i r v -> p i (r v)"),
                                                ALU.mult).then_inc(S["st"], 1)
                        for r in range(R):
                            dve.wait_ge(S["sc_p"], n + 1)
                            nc.vector.tensor_tensor(prob[:, r, :, :],
                                                    bank[4 + r][:, :].rearrange("p (x q) -> p x q", x=4),
                                                    causal[:, :].rearrange("p (o q) -> p o q", o=1)
                                                    .broadcast_to([P, 4, P]), ALU.mult).then_inc(S["sc"], 1)
                        dve.wait_ge(S["pv_p"], n + 1 + 4)
                        pv = bank[3][:, 0:2 * H * V].rearrange("p (t h v) -> p t h v", t=2, h=H)
                        base = g * (NQK + 4) + NQK + 2 * b
                        nc.vector.tensor_scalar(den[:, :, :], pv[:, :, :, E], LN_EPS, None, ALU.add).then_inc(S["den"], 1)
                        dve.wait_ge(S["den"], base + 1)
                        nc.vector.reciprocal(den[:, :, :], den[:, :, :]).then_inc(S["den"], 1)
                        dve.wait_ge(S["den"], base + 2)
                        nc.vector.tensor_tensor(on[:, :, :].rearrange("p t (h e) -> p t h e", h=H), pv[:, :, :, 0:E],
                                                den[:, :, :].rearrange("p t (h o) -> p t h o", o=1)
                                                .broadcast_to([P, 2, H, E]), ALU.mult).then_inc(S["on"], 1)
                        dve.wait_ge(S["o_p"], n + 1)
                        o = o_all[:, dyn(g * TPG + 2 * b, 2), :]
                        nc.vector.tensor_tensor(o, bank[2][:, 0:2 * D].rearrange("p (t d) -> p t d", t=2),
                                                rows[:, 1:2, :].broadcast_to([P, 2, D]), ALU.add).then_inc(S["o"], 1)
                        dve.wait_ge(S["o"], n + 1 + 1)
                        for j in range(2):
                            tile = g * TPG + 2 * b + j
                            nc.vector.bn_stats(stats[:, dyn(tile, 1), :], o_all[:, dyn(tile, 1), :]).then_inc(S["stat"], 1)

        @block.tensor
        def _(pe):
            pe.sem_inc(S["xt_p"], 2)
            pe.sem_inc(S["pv_p"], 4)
            with pe.Fori(0, GROUPS // 2) as i:
                for u in range(2):
                    g = 2 * i + u
                    pe.wait_ge(S["xn"], g + 1)
                    pe.wait_ge(S["ot"], 2 * g + 1)
                    for j in range(TPG):
                        mm = nc.tensor.transpose(bank[0][:, j * P:(j + 1) * P], xn[:, u, j, :], ident[:, :])
                    mm.then_inc(S["xt_p"], 1)
                    pe.wait_ge(S["xt"], g + 1 + 2)
                    for j in range(NQK):
                        pe.wait_ge(S["qk_e"], NQK * g + j + 1)
                        if j == 0:
                            pe.wait_ge(S["kt"], 2 * g + 1)
                        if j == 1:
                            pe.wait_ge(S["o"], 2 * g + 1)
                        nc.tensor.matmul(bank[1 + j % 2][:, :], wqk[:, j, :], xt[:, u, :], start=True,
                                         stop=True).then_inc(S["qk_p"], 1)
                    pe.wait_ge(S["on"], 2 * g + 1)
                    for j in range(TPG):
                        mm = nc.tensor.matmul(bank[3][:, j * D:(j + 1) * D], xt[:, u, j * P:(j + 1) * P], wv[:, :],
                                              start=(j == 0), stop=True, skip_group_check=True)
                    mm.then_inc(S["v_p"], 1)
                    for b in range(2):
                        n = 2 * g + b
                        first, second = 2 * b, 2 * b + 1
                        pe.wait_ge(S["qk"], NQK * g + NQK + 2)
                        pe.wait_ge(S["qk_e"], NQK * g + NQK + 2)
                        pe.wait_ge(S["kt"], n + 1)
                        for hf in range(2):
                            mm = nc.tensor.transpose(bank[1][:, hf * P:(hf + 1) * P],
                                                     qk[:, u, 2 + hf, first * P:(first + 1) * P], ident[:, :])
                        mm.then_inc(S["kt_p"], 1)
                        pe.wait_ge(S["sc"], 4 * n + 4)
                        for j, tl in enumerate((first, second)):
                            for hf in range(2):
                                for r in range(R):
                                    at = (2 * j + hf) * P
                                    mm = nc.tensor.matmul(
                                        bank[4 + r][:, at:at + P],
                                        qk[32 * r:32 * r + 32, u, 2 + hf, tl * P:(tl + 1) * P],
                                        qk[32 * r:32 * r + 32, u, hf, tl * P:(tl + 1) * P],
                                        start=(j == 0 and hf == 0), stop=True, skip_group_check=True)
                        mm.then_inc(S["sc_p"], 1)
                        pe.wait_ge(S["kt"], n + 2)
                        pe.wait_ge(S["v"], g + 2)
                        pe.wait_ge(S["o"], n + 1)
                        for hf in range(2):
                            mm = nc.tensor.matmul(bank[2][:, hf * R * V:(hf + 1) * R * V], ktok[:, hf * P:(hf + 1) * P],
                                                  v1[:, u, first, R * hf:R * hf + R, :].rearrange("p h v -> p (h v)"),
                                                  start=(hf == 0), stop=True, skip_group_check=True)
                        mm.then_inc(S["st_p"], 1)
                        pe.wait_ge(S["on"], n + 1)
                        pe.wait_ge(S["st"], n + 1)
                        for hf in range(2):
                            at = H * V + hf * R * V
                            nc.tensor.matmul(bank[3][:, at:at + R * V], qk[:, u, hf, second * P:(second + 1) * P],
                                             state[:, hf, :], start=(hf == 0), stop=False, skip_group_check=True)
                        for r in range(R):
                            pe.wait_ge(S["sc"], 4 * n + r + 1 + 4)
                            for j, tl in enumerate((first, second)):
                                for hf in range(2):
                                    hd = R * hf + r
                                    at = j * H * V + hd * V
                                    mm = nc.tensor.matmul(bank[3][:, at:at + V], prob[:, r, 2 * j + hf, :],
                                                          v1[:, u, tl, hd, :], start=False, stop=True,
                                                          skip_group_check=True)
                        mm.then_inc(S["pv_p"], 1)
                        pe.wait_ge(S["on"], n + 2)
                        pe.wait_ge(S["ot"], n + 1)
                        pe.wait_ge(S["xt"], g + 1 + 2)
                        for j in range(2):
                            mm = nc.tensor.transpose(bank[0][:, j * P:(j + 1) * P], on[:, j, :], ident[:, :])
                        mm.then_inc(S["ot_p"], 1)
                        pe.wait_ge(S["ot"], n + 2)
                        pe.wait_ge(S["st"], n + 1)
                        for j in range(2):
                            mm = nc.tensor.matmul(bank[2][:, j * D:(j + 1) * D], ot[:, j * P:(j + 1) * P], wo[:, :],
                                                  start=(j == 0), stop=True, skip_group_check=True)
                        mm.then_inc(S["o_p"], 1)

        @block.scalar
        def _(act):
            act.sem_inc(S["ot"], 1)
            act.sem_inc(S["xt"], 2)
            act.sem_inc(S["qk_e"], 2)
            act.sem_inc(S["kt"], 1)
            with act.Fori(0, GROUPS // 2) as i:
                for u in range(2):
                    g = 2 * i + u
                    act.wait_ge(S["xt_p"], g + 1 + 2)
                    nc.scalar.copy(xt[:, u, :], bank[0][:, :]).then_inc(S["xt"], 1)
                    for j in range(NQK):
                        act.wait_ge(S["qk_p"], NQK * g + j + 1)
                        act.wait_ge(S["qk"], NQK * g + j + 1)
                        nc.scalar.activation(ebuf[:, j % 2, :], bank[1 + j % 2][:, :], ACT.Exp, bias=bqk[:, 0, j:j + 1])
                        nc.scalar.activation(xbuf[:, j % 2, :], bank[1 + j % 2][:, :], ACT.Identity,
                                             bias=bqk[:, 1, j:j + 1]).then_inc(S["qk_e"], 1)
                    for b in range(2):
                        n = 2 * g + b
                        act.wait_ge(S["kt_p"], n + 1)
                        nc.scalar.copy(ktok[:, :], bank[1][:, 0:2 * P]).then_inc(S["kt"], 1)
                        act.wait_ge(S["ot_p"], n + 1)
                        nc.scalar.copy(ot[:, :], bank[0][:, 0:2 * P]).then_inc(S["ot"], 1)

        @block.gpsimd
        def _(pool):
            pool.sem_inc(S["sc"], 4)
            pool.sem_inc(S["on"], 1)

    layer_stats(nc, c, stats, mean, rstd, eps_t, "a1")
    s_ln = sem("s_a_ln")
    s_add = sem("s_a_add")
    s_nst = sem("s_a_newstats")
    with nc.Block() as block:
        @block.vector
        def _(dve):
            with dve.Fori(0, TILES // 2) as i:
                for u in range(2):
                    tl = 2 * i + u
                    nc.vector.scalar_tensor_tensor(off[:, u, :], o_all[:, dyn(tl, 1), :], mean[:, dyn(tl, 1)],
                                                   rows[:, 2, :], ALU.subtract, ALU.mult).then_inc(s_ln, 1)
                for u in range(2):
                    tl = 2 * i + u
                    dve.wait_ge(s_ln, 2 * i + 2)
                    dve.wait_ge(s_add, tl + 1)
                    nc.vector.scalar_tensor_tensor(h[:, dyn(tl, 1), :], off[:, u, :], rstd[:, dyn(tl, 1)],
                                                   h[:, dyn(tl, 1), :], ALU.mult, ALU.add).then_inc(s_nst, 1)
                for u in range(2):
                    tl = 2 * i + u
                    dve.wait_ge(s_nst, tl + 1)
                    nc.vector.bn_stats(stats[:, dyn(tl, 1), :], h[:, dyn(tl, 1), :])

        @block.gpsimd
        def _(pool):
            with pool.Fori(0, TILES) as tl:
                nc.gpsimd.tensor_tensor(h[:, dyn(tl, 1), :], h[:, dyn(tl, 1), :], rows[:, 3:4, :],
                                        ALU.add).then_inc(s_add, 1)


def routing_phase(nc, c, t, h, mean, rstd, bank, ident, xt_all, tw):
    def sb(name, shape, dt=F32):
        return c.enter_context(nc.sbuf_tensor(name, shape, dt))

    def sem(name):
        return c.enter_context(nc.semaphore(name))

    NL = GRP + EXPERTS
    SETS = 1 + GRP
    wr = sb("wr", [P, NL])
    br = sb("br", [P, NL])
    xn = sb("r_xn", [P, 2, TPG, D])
    xt = sb("r_xt", [P, 2, GT])
    pr = sb("r_prob", [P, TILES, SETS, 4])
    rank = sb("r_rank", [P, TILES, SETS, 4])
    sel = sb("r_sel", [P, TILES, SETS, 4])
    one = sb("r_one", [P, TILES, SETS])
    top = sb("r_top", [P, 3, TILES, SETS])
    s_w = sem("s_r_w")
    s_xn, s_xtp, s_xt, s_lp, s_l = (sem("s_r_" + n) for n in ("xn", "xt_p", "xt", "logit_p", "logit"))
    s_all = sem("s_r_all")

    with nc.Block() as block:
        @block.sync
        def _(sp):
            sp.dma_start(wr[:, :], t["wr"]).then_inc(s_w, 16)
            sp.dma_start(br[:, :], t["br"].partition_broadcast(P)).then_inc(s_w, 16)

        @block.vector
        def _(dve):
            dve.sem_inc(s_l, 2)
            dve.wait_ge(s_w, 32)
            with dve.Fori(0, GROUPS // 2) as i:
                for u in range(2):
                    g = 2 * i + u
                    dve.wait_ge(s_xtp, g + 1)
                    for j in range(TPG):
                        ins = nc.vector.tensor_scalar(xn[:, u, j, :], h[:, dyn(g * TPG + j, 1), :],
                                                      mean[:, dyn(g * TPG + j, 1)], rstd[:, dyn(g * TPG + j, 1)],
                                                      ALU.subtract, ALU.mult)
                    ins.then_inc(s_xn, 1)
                for u in range(2):
                    g = 2 * i + u
                    dve.wait_ge(s_lp, g + 1)
                    nc.vector.tensor_tensor(pr[:, dyn(g * TPG, TPG), :, :],
                                            bank[2 + u][:, 0:TPG * NL].rearrange("p (t s k) -> p t s k", t=TPG, k=4),
                                            br[:, :].rearrange("p (o s k) -> p o s k", o=1, k=4)
                                            .broadcast_to([P, TPG, SETS, 4]), ALU.add).then_inc(s_l, 1)

        @block.tensor
        def _(pe):
            pe.sem_inc(s_xtp, 2)
            pe.wait_ge(s_w, 32)
            with pe.Fori(0, GROUPS // 2) as i:
                for u in range(2):
                    g = 2 * i + u
                    pe.wait_ge(s_xn, g + 1)
                    pe.wait_ge(s_xt, g + 1)
                    for j in range(TPG):
                        mm = nc.tensor.transpose(bank[u][:, j * P:(j + 1) * P], xn[:, u, j, :], ident[:, :])
                    mm.then_inc(s_xtp, 1)
                for u in range(2):
                    g = 2 * i + u
                    pe.wait_ge(s_xt, g + 1 + 2)
                    pe.wait_ge(s_l, g + 1)
                    for j in range(TPG):
                        mm = nc.tensor.matmul(bank[2 + u][:, j * NL:(j + 1) * NL], xt[:, u, j * P:(j + 1) * P],
                                              wr[:, :], start=(j == 0), stop=True, skip_group_check=True)
                    mm.then_inc(s_lp, 1)

        @block.scalar
        def _(act):
            act.sem_inc(s_xt, 2)
            act.sem_inc(s_all, 2)
            with act.Fori(0, GROUPS // 2) as i:
                for u in range(2):
                    g = 2 * i + u
                    act.wait_ge(s_xtp, g + 1 + 2)
                    act.wait_ge(s_all, g + 1)
                    nc.scalar.copy(xt[:, u, :], bank[u][:, :]).then_inc(s_xt, 1)

        @block.gpsimd
        def _(pool):
            with pool.Fori(0, GROUPS // 2) as i:
                for u in range(2):
                    g = 2 * i + u
                    pool.wait_ge(s_xt, g + 1 + 2)
                    pool.wait_ge(s_lp, g + 1)
                    nc.gpsimd.tensor_copy(xt_all[:, dyn(g * GT, GT)], xt[:, u, :]).then_inc(s_all, 1)

    s_v = sem("s_r_chain")
    s_e = sem("s_r_exp")
    with nc.Block() as block:
        @block.scalar
        def _(act):
            act.wait_ge(s_v, 2)
            nc.scalar.activation(pr[:, :, :, :], pr[:, :, :, :], ACT.Exp).then_inc(s_e, 1)

        @block.vector
        def _(dve):
            count = [0]

            def step(ins):
                count[0] += 1
                ins.then_inc(s_v, 1)
                dve.wait_ge(s_v, count[0])

            def over4(a):
                return a.rearrange("p t (s o) -> p t s o", o=1).broadcast_to([P, TILES, SETS, 4])

            p4, r4, s4 = pr[:, :, :, :], rank[:, :, :, :], sel[:, :, :, :]
            m1, m2, keep = (top[:, k, :, :] for k in range(3))
            step(nc.vector.tensor_reduce(m1, p4, AX.X, ALU.max))
            step(nc.vector.tensor_tensor(p4, p4, over4(m1), ALU.subtract))
            dve.wait_ge(s_e, 1)
            step(nc.vector.tensor_reduce(m1, p4, AX.X, ALU.add))
            step(nc.vector.reciprocal(m1, m1))
            step(nc.vector.tensor_tensor(p4, p4, over4(m1), ALU.mult))
            for k in range(4):
                step(nc.vector.memset(rank[:, :, :, k], float(3 - k)))
            for a in range(4):
                for b in range(a + 1, 4):
                    step(nc.vector.tensor_tensor(one[:, :, :], pr[:, :, :, a], pr[:, :, :, b], ALU.is_ge))
                    step(nc.vector.tensor_tensor(rank[:, :, :, b], rank[:, :, :, b], one[:, :, :], ALU.add))
                    step(nc.vector.tensor_tensor(rank[:, :, :, a], rank[:, :, :, a], one[:, :, :], ALU.subtract))
            step(nc.vector.scalar_tensor_tensor(s4.rearrange("p t s k -> p (t s k)"), r4.rearrange("p t s k -> p (t s k)"),
                                                0.0, p4.rearrange("p t s k -> p (t s k)"), ALU.is_equal, ALU.mult))
            step(nc.vector.tensor_reduce(m1, s4, AX.X, ALU.add))
            step(nc.vector.scalar_tensor_tensor(r4.rearrange("p t s k -> p (t s k)"), r4.rearrange("p t s k -> p (t s k)"),
                                                1.0, p4.rearrange("p t s k -> p (t s k)"), ALU.is_equal, ALU.mult))
            step(nc.vector.tensor_reduce(m2, r4, AX.X, ALU.add))
            step(nc.vector.tensor_tensor(keep, m1, m2, ALU.add))
            step(nc.vector.tensor_scalar(keep, keep, TOP_P, None, ALU.is_le))
            step(nc.vector.tensor_tensor(m2, m2, keep, ALU.mult))
            step(nc.vector.tensor_tensor(r4, r4, over4(keep), ALU.mult))
            step(nc.vector.tensor_tensor(r4, r4, s4, ALU.add))
            step(nc.vector.tensor_tensor(m1, m1, m2, ALU.add))
            step(nc.vector.tensor_scalar(m1, m1, 1e-9, None, ALU.add))
            step(nc.vector.reciprocal(m1, m1))
            step(nc.vector.tensor_tensor(r4, r4, over4(m1), ALU.mult))
            step(nc.vector.tensor_tensor(tw[:, :, :].rearrange("p t (g k) -> p t g k", k=4), rank[:, :, 1:SETS, :],
                                         rank[:, :, 0, :].rearrange("p t (g o) -> p t g o", o=1)
                                         .broadcast_to([P, TILES, GRP, 4]), ALU.mult))
            step(nc.vector.tensor_scalar(tw[:, :, :], tw[:, :, :], GRP ** -0.5, None, ALU.mult))


def ffn_phase(nc, c, h, bank, w1, w3, w2, s_wts, xt_all, tw, stats):
    def sb(name, shape, dt=F32):
        return c.enter_context(nc.sbuf_tensor(name, shape, dt))

    def sem(name):
        return c.enter_context(nc.semaphore(name))

    CH = HID // P
    U = EXPERTS * CH
    RING = 4
    gate = sb("f_gate", [P, 2, GT])
    hid = sb("f_hid", [P, RING, GT])
    s_up, s_gate, s_hid, s_down, s_acc = (sem("s_f_" + n) for n in ("up", "gate", "hid", "down", "acc"))
    s_st = sem("s_f_stats")

    with nc.Block() as block:
        @block.tensor
        def _(pe):
            pe.sem_inc(s_down, RING)
            for k in range(4):
                pe.wait_ge(s_wts[k], 16 * 3)
            with pe.Fori(0, GROUPS) as g:
                def up(m):
                    e, ch = m // CH, m % CH
                    pe.wait_ge(s_hid, g * U + m + 1)
                    nc.tensor.matmul(bank[m % 2][:, :], w1[:, e, ch * P:(ch + 1) * P], xt_all[:, dyn(g * GT, GT)],
                                     start=True, stop=True)
                    nc.tensor.matmul(bank[2 + m % 2][:, :], w3[:, e, ch * P:(ch + 1) * P], xt_all[:, dyn(g * GT, GT)],
                                     start=True, stop=True).then_inc(s_up, 1)

                def down(m):
                    e, ch = m // CH, m % CH
                    pe.wait_ge(s_hid, g * U + m + 1 + 2)
                    if ch == 0:
                        pe.wait_ge(s_acc, g * EXPERTS + e + 1)
                    for j in range(TPG):
                        mm = nc.tensor.matmul(bank[4 + e % 2][:, j * D:(j + 1) * D], hid[:, m % RING, j * P:(j + 1) * P],
                                              w2[:, e, ch, :], start=(ch == 0 and j == 0), stop=(ch == CH - 1),
                                              skip_group_check=True)
                    mm.then_inc(s_down, 1)

                for m in range(U + 2):
                    if m < U:
                        up(m)
                    if m >= 2:
                        down(m - 2)

        @block.scalar
        def _(act):
            with act.Fori(0, GROUPS) as g:
                for m in range(U):
                    act.wait_ge(s_up, g * U + m + 1)
                    act.wait_ge(s_hid, g * U + m + 1)
                    nc.scalar.activation(gate[:, m % 2, :], bank[m % 2][:, :], ACT.Silu).then_inc(s_gate, 1)

        @block.vector
        def _(dve):
            dve.sem_inc(s_hid, 2)
            dve.sem_inc(s_acc, 2)
            with dve.Fori(0, GROUPS) as g:
                def add(e):
                    dve.wait_ge(s_down, g * U + (e + 1) * CH + RING)
                    for j in range(TPG):
                        tile = g * TPG + j
                        ins = nc.vector.scalar_tensor_tensor(h[:, dyn(tile, 1), :], bank[4 + e % 2][:, j * D:(j + 1) * D],
                                                             tw[:, dyn(tile, 1), e], h[:, dyn(tile, 1), :],
                                                             ALU.mult, ALU.add)
                    ins.then_inc(s_acc, 1)

                for m in range(U):
                    dve.wait_ge(s_gate, g * U + m + 1)
                    dve.wait_ge(s_down, g * U + m + 1)
                    nc.vector.tensor_tensor(hid[:, m % RING, :], bank[2 + m % 2][:, :], gate[:, m % 2, :],
                                            ALU.mult).then_inc(s_hid, 1)
                    if m % CH == CH - 1 and m >= 2 * CH - 1:
                        dve.wait_ge(s_acc, g * EXPERTS + m // CH - 1 + 2)
                        add(m // CH - 1)
                dve.wait_ge(s_acc, g * EXPERTS + EXPERTS - 1 + 2)
                add(EXPERTS - 1)
                dve.wait_ge(s_acc, g * EXPERTS + EXPERTS + 2)
                for j in range(TPG):
                    tile = g * TPG + j
                    nc.vector.bn_stats(stats[:, dyn(tile, 1), :], h[:, dyn(tile, 1), :])


def slice_attention_phase(nc, c, t, h, stats, mean, rstd, bank, ident):
    def sb(name, shape, dt=F32):
        return c.enter_context(nc.sbuf_tensor(name, shape, dt))

    def sem(name):
        return c.enter_context(nc.semaphore(name))

    H, DH, M = HEADS1, DH1, SLICES
    HM = H * M
    NB = 8
    OCT = BATCH // NB
    wx = sb("c_wx", [DH, H, D])
    wsl = sb("c_wsl", [DH, M])
    bx = sb("c_bx", [DH, H])
    bxr = sb("c_bxr", [DH, H, P])
    bsl = sb("c_bsl", [P, M])
    temp = sb("c_temp", [P, 2, H])
    wqkv = sb("c_wqkv", [DH, 3, DH])
    wot = sb("c_wot", [DH, H, D])
    wfx = sb("c_wfx", [P, H, DH])
    bfx = sb("c_bfx", [1, H, DH])
    bo = sb("c_bo", [P, 1, D])
    wl = sb("c_wl", [P, HM])
    bl = sb("c_bl", [P, 1, HM])
    gqk = sb("c_gqk", [DH, 2 * DH])
    wvo = sb("c_wvo", [DH, H, D])
    off_block = sb("c_off", [P, P])

    xn1 = sb("c_xn1", [P, 2, 2, D + 1])
    xt = sb("c_xt", [P, 2, SEQ])
    lg = sb("c_lg", [P, 2, 2 * H, M])
    mx = sb("c_mx", [P, 2 * H])
    sm = sb("c_sm", [P, 2 * H])
    w = sb("c_w", [P, 2, 2, HM])
    dn = sb("c_dn", [P, 2])
    xs = sb("c_xs", [P, 2, 2, D + 1])
    wt = sb("c_wt", [P, NB, 2, SEQ])
    xst = sb("c_xst", [P, NB, H, M])
    rt = sb("c_rt", [1, NB, H, M])
    tt = sb("c_tt", [DH, NB, H, M])
    ut = sb("c_ut", [DH, NB, H, M])
    at = sb("c_at", [P, 2, 4, P])
    amx = sb("c_amx", [P, 4])
    asm = sb("c_asm", [P, 4])
    att = sb("c_att", [P, 2, 4, P])
    vo = sb("c_vo", [P, 2, 4, P])
    os_ = sb("c_os", [P, 2, 4, D])

    s_w, s_m, s_k, s_f = (sem("s_c_" + n) for n in ("weights", "mask", "setup", "fold"))
    with nc.Block() as block:
        @block.sync
        def _(sp):
            for dst, name in ((wx[:, :, :], "wx"), (wsl[:, :], "wsl"), (bx[:, :], "bx"), (wqkv[:, :, :], "wqkv1"),
                              (wot[:, :, :], "wot"), (wfx[:, :, :], "wfx"), (bfx[:, :, :], "bfx")):
                sp.dma_start(dst, t[name]).then_inc(s_w, 16)
            sp.dma_start(bsl[:, :], t["bsl"].partition_broadcast(P)).then_inc(s_w, 16)
            sp.dma_start(temp[:, 0, :], t["temp"].partition_broadcast(P)).then_inc(s_w, 16)
            sp.dma_start(bo[:, 0, :], t["bo1"].partition_broadcast(P)).then_inc(s_w, 16)

        @block.gpsimd
        def _(pool):
            nc.gpsimd.memset(off_block[:, :], -1e30).then_inc(s_m, 1)
            nc.gpsimd.memset(xn1[:, :, :, :], 1.0).then_inc(s_m, 1)
            nc.gpsimd.memset(gqk[:, DH:2 * DH], 0.0).then_inc(s_m, 1)
            pool.wait_ge(s_m, 3)
            for r in range(4):
                nc.gpsimd.memset(off_block[32 * r:32 * r + 32, 32 * r:32 * r + 32], 0.0).then_inc(s_m, 1)

        @block.vector
        def _(dve):
            dve.wait_ge(s_w, 160)
            nc.vector.tensor_copy(bxr[:, :, :], bx[:, :].rearrange("p (h o) -> p h o", o=1)
                                  .broadcast_to([DH, H, P])).then_inc(s_k, 1)
            nc.vector.reciprocal(temp[:, 1, :], temp[:, 0, :]).then_inc(s_k, 1)
            dve.wait_ge(s_k, 2)
            inv = temp[:, 1, :].rearrange("p (h o) -> p h o", o=1).broadcast_to([P, H, M])
            dve.wait_ge(s_f, 1)
            nc.vector.tensor_tensor(wl[:, :].rearrange("p (h m) -> p h m", h=H),
                                    bank[0][:, 0:HM].rearrange("p (h m) -> p h m", h=H), inv, ALU.mult).then_inc(s_k, 1)
            nc.vector.tensor_tensor(bl[:, 0, :].rearrange("p (h m) -> p h m", h=H),
                                    bank[1][:, 0:HM].rearrange("p (h m) -> p h m", h=H),
                                    bsl[:, :].rearrange("p (o m) -> p o m", o=1).broadcast_to([P, H, M]),
                                    ALU.add).then_inc(s_k, 1)
            dve.wait_ge(s_k, 4)
            nc.vector.tensor_tensor(bl[:, 0, :].rearrange("p (h m) -> p h m", h=H),
                                    bl[:, 0, :].rearrange("p (h m) -> p h m", h=H), inv, ALU.mult).then_inc(s_k, 1)
            nc.vector.tensor_copy(gqk[:, 0:DH], bank[2][0:DH, 0:DH]).then_inc(s_k, 1)
            for k in range(2):
                nc.vector.tensor_copy(wvo[:, 4 * k:4 * k + 4, :],
                                      bank[3 + k][0:DH, :].rearrange("p (h d) -> p h d", h=4)).then_inc(s_k, 1)

        @block.tensor
        def _(pe):
            pe.wait_ge(s_w, 160)
            pe.wait_ge(s_k, 1)
            for hd in range(H):
                nc.tensor.matmul(bank[0][:, hd * M:(hd + 1) * M], wx[:, hd, :], wsl[:, :], start=True, stop=True)
                nc.tensor.matmul(bank[1][:, hd * M:(hd + 1) * M], bxr[:, hd, :], wsl[:, :], start=True, stop=True)
            nc.tensor.matmul(bank[2][0:DH, 0:DH], wqkv[:, 0, :], wqkv[:, 1, :], start=True, stop=True)
            for k in range(2):
                mm = nc.tensor.matmul(bank[3 + k][0:DH, :], wqkv[:, 2, :],
                                      wot[:, 4 * k:4 * k + 4, :].rearrange("p h d -> p (h d)"), start=True, stop=True)
            mm.then_inc(s_f, 1)

    names = ("xn", "xt_p", "xt", "lg_p", "sm1", "chain", "exp", "w", "wt_p", "wt", "xs_p", "xs", "xst_p", "xst",
             "tt_p", "tt", "ut_p", "ut", "al_p", "a1", "aexp", "a", "att_p", "att", "vo_p", "vo", "o_p", "o",
             "y_p", "y", "hb", "st", "hadd")
    S = {n: sem("s_c_" + n) for n in names}
    CH_SM, CH_A = 3, 3

    with nc.Block() as block:
        @block.vector
        def _(dve):
            dve.sem_inc(S["sm1"], 2)
            dve.sem_inc(S["xs"], 1)
            dve.sem_inc(S["ut"], 2)
            dve.sem_inc(S["a1"], 2)
            dve.sem_inc(S["o"], 1)
            dve.sem_inc(S["y"], 1)
            dve.sem_inc(S["a"], 2)
            PER = NB * 5 + (NB // 2) * 4
            with dve.Fori(0, OCT) as q:
                link = [0]

                def chained(ins):
                    link[0] += 1
                    ins.then_inc(S["chain"], 1)
                    dve.wait_ge(S["chain"], q * PER + link[0])

                def norm(k):
                    n = q * NB + k
                    dve.wait_ge(S["xs_p"], n + 1)
                    for j in range(2):
                        tl = n * 2 + j
                        ins = nc.vector.tensor_scalar(xn1[:, k % 2, j, 0:D], h[:, dyn(tl, 1), :], mean[:, dyn(tl, 1)],
                                                      rstd[:, dyn(tl, 1)], ALU.subtract, ALU.mult)
                    ins.then_inc(S["xn"], 1)

                def softmax_max(k):
                    n = q * NB + k
                    l4 = lg[:, k % 2, :, :]
                    dve.wait_ge(S["lg_p"], n + 1)
                    chained(nc.vector.tensor_tensor(l4.rearrange("p (t h) m -> p t (h m)", t=2),
                                                    bank[2 + k % 2][:, :].rearrange("p (t c) -> p t c", t=2),
                                                    bl[:, :, :].broadcast_to([P, 2, HM]), ALU.add))
                    chained(nc.vector.tensor_reduce(mx[:, :], l4, AX.X, ALU.max))
                    nc.vector.tensor_tensor(l4, l4, mx[:, :].rearrange("p (g o) -> p g o", o=1)
                                            .broadcast_to([P, 2 * H, M]), ALU.subtract).then_inc(S["sm1"], 1)

                def softmax_sum(k):
                    n = q * NB + k
                    l4 = lg[:, k % 2, :, :]
                    dve.wait_ge(S["exp"], n + 1)
                    chained(nc.vector.tensor_reduce(sm[:, :], l4, AX.X, ALU.add))
                    chained(nc.vector.reciprocal(sm[:, :], sm[:, :]))
                    nc.vector.tensor_tensor(w[:, k % 2, :, :].rearrange("p t (h m) -> p (t h) m", h=H), l4,
                                            sm[:, :].rearrange("p (g o) -> p g o", o=1)
                                            .broadcast_to([P, 2 * H, M]), ALU.mult).then_inc(S["w"], 1)

                def scale_slices(k):
                    n = q * NB + k
                    dve.wait_ge(S["xs_p"], n + 1 + 2)
                    xp = bank[6][:, 0:2 * (D + 1)].rearrange("p (i d) -> p i d", i=2)
                    link[0] += 1
                    nc.vector.tensor_scalar(dn[:, :], xp[:, :, D], LN_EPS, None, ALU.add).then_inc(S["chain"], 1)
                    dve.wait_ge(S["chain"], q * PER + link[0])
                    nc.vector.reciprocal(dn[:, :], dn[:, :]).then_inc(S["st"], 1)
                    dve.wait_ge(S["st"], n + 1)
                    nc.vector.tensor_tensor(xs[:, k % 2, :, :], xp, dn[:, :].rearrange("p (i o) -> p i o", o=1)
                                            .broadcast_to([P, 2, D + 1]), ALU.mult).then_inc(S["xs"], 1)

                for k in range(NB + 1):
                    if k < NB:
                        norm(k)
                    if k >= 1:
                        softmax_sum(k - 1)
                    if k < NB:
                        softmax_max(k)
                    if k >= 1:
                        scale_slices(k - 1)
                for k in range(NB // 2):
                    dve.wait_ge(S["ut_p"], q * (NB // 2) + k + 1)
                    nc.vector.tensor_copy(ut[:, 2 * k:2 * k + 2, :, :].rearrange("p b h m -> p (b h m)"),
                                          bank[4 + k % 2][0:DH, :]).then_inc(S["ut"], 1)
                for k in range(NB // 2):
                    n = q * (NB // 2) + k
                    a4 = at[:, k % 2, :, :]
                    dve.wait_ge(S["al_p"], n + 1)
                    dve.wait_ge(S["att_p"], n + 1)
                    chained(nc.vector.tensor_scalar(a4, bank[k % 2][:, :].rearrange("p (u c) -> p u c", u=4),
                                                    DH ** -0.5, None, ALU.mult))
                    chained(nc.vector.tensor_tensor(a4, a4, off_block[:, :].rearrange("p (o c) -> p o c", o=1)
                                                    .broadcast_to([P, 4, P]), ALU.add))
                    chained(nc.vector.tensor_reduce(amx[:, :], a4, AX.X, ALU.max))
                    nc.vector.tensor_tensor(a4, a4, amx[:, :].rearrange("p (u o) -> p u o", o=1)
                                            .broadcast_to([P, 4, P]), ALU.subtract).then_inc(S["a1"], 1)
                    dve.wait_ge(S["aexp"], n + 1)
                    chained(nc.vector.tensor_reduce(asm[:, :], a4, AX.X, ALU.add))
                    nc.vector.reciprocal(asm[:, :], asm[:, :]).then_inc(S["hb"], 1)
                    dve.wait_ge(S["hb"], n + 1)
                    nc.vector.tensor_tensor(a4, a4, asm[:, :].rearrange("p (u o) -> p u o", o=1)
                                            .broadcast_to([P, 4, P]), ALU.mult).then_inc(S["a"], 1)
                    dve.wait_ge(S["o_p"], n + 1)
                    nc.vector.tensor_copy(os_[:, k % 2, :, :], bank[6][:, :].rearrange("p (u c) -> p u c", u=4))\
                        .then_inc(S["o"], 1)
                    dve.wait_ge(S["y_p"], n + 1 + 1)
                    tl = (q * NB + 2 * k) * 2
                    h4 = h[:, dyn(tl, 4), :]
                    nc.vector.tensor_tensor(h4, bank[7][:, :].rearrange("p (u d) -> p u d", u=4), h4,
                                            ALU.add).then_inc(S["y"], 1)
                    dve.wait_ge(S["y"], n + 1 + 1)
                    nc.vector.tensor_tensor(h4, h4, bo[:, :, :].broadcast_to([P, 4, D]), ALU.add).then_inc(S["hadd"], 1)
                    dve.wait_ge(S["hadd"], n + 1)
                    for j in range(4):
                        nc.vector.bn_stats(stats[:, dyn(tl + j, 1), :], h[:, dyn(tl + j, 1), :])

        @block.tensor
        def _(pe):
            pe.sem_inc(S["xs_p"], 2)
            pe.sem_inc(S["att_p"], 2)
            pe.sem_inc(S["y_p"], 1)
            with pe.Fori(0, OCT) as q:
                for k in range(NB + 1):
                    n = q * NB + k
                    if k < NB:
                        pe.wait_ge(S["xn"], n + 1)
                        pe.wait_ge(S["xt"], n + 1)
                        if k < 2:
                            pe.wait_ge(S["a1"], q * (NB // 2) + 2)
                        for j in range(2):
                            mm = nc.tensor.transpose(bank[k % 2][:, j * P:(j + 1) * P], xn1[:, k % 2, j, 0:D], ident[:, :])
                        mm.then_inc(S["xt_p"], 1)
                    if k >= 1:
                        kk, n1 = (k - 1) % 2, q * NB + k - 1
                        pe.wait_ge(S["w"], n1 + 1)
                        pe.wait_ge(S["wt"], n1 + 1)
                        if k <= 2:
                            pe.wait_ge(S["vo"], q * (NB // 2) + 2)
                            pe.wait_ge(S["o"], q * (NB // 2) + 1)
                        for i in range(2):
                            for j in range(2):
                                mm = nc.tensor.transpose(bank[4 + kk][:, i * SEQ + j * P:i * SEQ + (j + 1) * P],
                                                         w[:, kk, j, i * P:(i + 1) * P], ident[:, :])
                        mm.then_inc(S["wt_p"], 1)
                        pe.wait_ge(S["xs"], n1 + 1)
                        for i in range(2):
                            for j in range(2):
                                mm = nc.tensor.matmul(bank[6][:, i * (D + 1):(i + 1) * (D + 1)],
                                                      w[:, kk, j, i * P:(i + 1) * P], xn1[:, kk, j, :],
                                                      start=(i == 0 and j == 0), stop=(j == 1), skip_group_check=True)
                        mm.then_inc(S["xs_p"], 1)
                    if k < NB:
                        pe.wait_ge(S["xt"], n + 1 + 2)
                        pe.wait_ge(S["sm1"], n + 1)
                        if k < 2:
                            pe.wait_ge(S["att"], q * (NB // 2) + 2)
                        for j in range(2):
                            mm = nc.tensor.matmul(bank[2 + k % 2][:, j * HM:(j + 1) * HM], xt[:, k % 2, j * P:(j + 1) * P],
                                                  wl[:, :], start=True, stop=True)
                        mm.then_inc(S["lg_p"], 1)
                    if k >= 1:
                        pe.wait_ge(S["xs"], n1 + 2)
                        pe.wait_ge(S["xst"], n1 + 1)
                        if k == 1:
                            pe.wait_ge(S["y"], q * (NB // 2) + 1)
                        for i in range(2):
                            nc.tensor.transpose(bank[7][:, i * P:(i + 1) * P], xs[:, kk, i, 0:D], ident[:, :])
                            mm = nc.tensor.transpose(bank[7][0:1, 2 * P + i * P:2 * P + (i + 1) * P], xs[:, kk, i, D:D + 1],
                                                     ident[:, :])
                        mm.then_inc(S["xst_p"], 1)
                pe.wait_ge(S["xst"], q * NB + NB + 1)
                for hd in range(H):
                    pe.wait_ge(S["tt"], q * H + hd + 1)
                    if hd in (2, 3):
                        pe.wait_ge(S["sm1"], q * NB + NB + 2)
                    nc.tensor.matmul(bank[hd % 4][0:DH, 0:NB * M], wfx[:, hd, :], xst[:, :, hd, :], start=True, stop=False)
                    nc.tensor.matmul(bank[hd % 4][0:DH, 0:NB * M], bfx[0:1, hd, :], rt[0:1, :, hd, :], start=False,
                                     stop=True).then_inc(S["tt_p"], 1)
                pe.wait_ge(S["tt"], q * H + H + 4)
                pe.wait_ge(S["wt"], q * NB + NB + 2)
                for k in range(NB // 2):
                    pe.wait_ge(S["ut"], q * (NB // 2) + k + 1)
                    nc.tensor.matmul(bank[4 + k % 2][:, :], gqk[:, :],
                                     tt[:, 2 * k:2 * k + 2, :, :].rearrange("p b h m -> p (b h m)"), start=True,
                                     stop=True).then_inc(S["ut_p"], 1)
                pe.wait_ge(S["ut"], q * (NB // 2) + NB // 2 + 2)
                for k in range(NB // 2):
                    n = q * (NB // 2) + k
                    pe.wait_ge(S["vo"], n + 1)
                    pe.wait_ge(S["a1"], n + 1)
                    for u in range(4):
                        b, i = 2 * k + u // 2, u % 2
                        hs = slice(4 * i, 4 * i + 4)
                        mm = nc.tensor.matmul(bank[k % 2][:, u * P:(u + 1) * P],
                                              ut[:, b, hs, :].rearrange("p h m -> p (h m)"),
                                              tt[:, b, hs, :].rearrange("p h m -> p (h m)"), start=True, stop=True)
                    mm.then_inc(S["al_p"], 1)
                    for u in range(4):
                        b, i = 2 * k + u // 2, u % 2
                        for r in range(4):
                            mm = nc.tensor.matmul(bank[4 + k % 2][32 * r:32 * r + 32, u * P:(u + 1) * P],
                                                  tt[:, b, 4 * i + r, :], wvo[:, 4 * i + r, :], start=True, stop=True)
                    mm.then_inc(S["vo_p"], 1)
                    pe.wait_ge(S["a"], n + 1 + 2)
                    pe.wait_ge(S["att"], n + 1)
                    for u in range(4):
                        mm = nc.tensor.transpose(bank[2 + k % 2][:, u * P:(u + 1) * P], at[:, k % 2, u, :], ident[:, :])
                    mm.then_inc(S["att_p"], 1)
                    pe.wait_ge(S["att"], n + 1 + 2)
                    pe.wait_ge(S["vo"], n + 1 + 2)
                    pe.wait_ge(S["o"], n + 1)
                    for u in range(4):
                        mm = nc.tensor.matmul(bank[6][:, u * D:(u + 1) * D], att[:, k % 2, u, :], vo[:, k % 2, u, :],
                                              start=True, stop=True)
                    mm.then_inc(S["o_p"], 1)
                    pe.wait_ge(S["o"], n + 2)
                    pe.wait_ge(S["y"], n + 1)
                    for u in range(4):
                        b, j = u // 2, u % 2
                        for i in range(2):
                            mm = nc.tensor.matmul(bank[7][:, u * D:(u + 1) * D],
                                                  wt[:, 2 * k + b, i, j * P:(j + 1) * P], os_[:, k % 2, 2 * b + i, :],
                                                  start=(u == 0 and i == 0), stop=(i == 1), skip_group_check=True)
                    mm.then_inc(S["y_p"], 1)

        @block.scalar
        def _(act):
            act.sem_inc(S["xt"], 2)
            act.sem_inc(S["wt"], 2)
            act.sem_inc(S["xst"], 1)
            act.sem_inc(S["tt"], 4)
            act.sem_inc(S["att"], 2)
            act.sem_inc(S["vo"], 2)
            with act.Fori(0, OCT) as q:
                for k in range(NB + 1):
                    n = q * NB + k
                    if k < NB:
                        act.wait_ge(S["xt_p"], n + 1)
                        act.wait_ge(S["sm1"], n + 1)
                        nc.scalar.copy(xt[:, k % 2, :], bank[k % 2][:, 0:SEQ]).then_inc(S["xt"], 1)
                    if k >= 1:
                        act.wait_ge(S["wt_p"], n)
                        if k == 1:
                            act.wait_ge(S["y_p"], q * (NB // 2) + 1)
                        nc.scalar.copy(wt[:, k - 1, :, :].rearrange("p i s -> p (i s)"),
                                       bank[4 + (k - 1) % 2][:, :]).then_inc(S["wt"], 1)
                    if k < NB:
                        act.wait_ge(S["sm1"], n + 1 + 2)
                        nc.scalar.activation(lg[:, k % 2, :, :], lg[:, k % 2, :, :], ACT.Exp).then_inc(S["exp"], 1)
                    if k >= 1:
                        act.wait_ge(S["xst_p"], n)
                        nc.scalar.copy(xst[:, k - 1, :, :].rearrange("p h m -> p (h m)"), bank[7][:, 0:HM])
                        nc.scalar.copy(rt[0:1, k - 1, :, :].rearrange("p h m -> p (h m)"), bank[7][0:1, HM:2 * HM])\
                            .then_inc(S["xst"], 1)
                for hd in range(H):
                    act.wait_ge(S["tt_p"], q * H + hd + 1)
                    nc.scalar.copy(tt[:, :, hd, :], bank[hd % 4][0:DH, 0:NB * M].rearrange("p (b m) -> p b m", b=NB))\
                        .then_inc(S["tt"], 1)
                for k in range(NB // 2):
                    n = q * (NB // 2) + k
                    act.wait_ge(S["vo_p"], n + 1)
                    nc.scalar.copy(vo[:, k % 2, :, :].rearrange("p u c -> p (u c)"), bank[4 + k % 2][:, :])\
                        .then_inc(S["vo"], 1)
                    act.wait_ge(S["a1"], n + 1 + 2)
                    nc.scalar.activation(at[:, k % 2, :, :], at[:, k % 2, :, :], ACT.Exp).then_inc(S["aexp"], 1)
                    act.wait_ge(S["att_p"], n + 1 + 2)
                    nc.scalar.copy(att[:, k % 2, :, :].rearrange("p u c -> p (u c)"), bank[2 + k % 2][:, :])\
                        .then_inc(S["att"], 1)


def expert_choice_phase(nc, c, t, h, mean, rstd, bank, ident):
    def sb(name, shape, dt=F32):
        return c.enter_context(nc.sbuf_tensor(name, shape, dt))

    def sem(name):
        return c.enter_context(nc.semaphore(name))

    E = GATES
    CAP = SEQ // E
    HB = P // E
    wg = sb("d_wg", [P, E])
    we = sb("d_we", [P, E, D])
    ones = sb("d_ones", [P, P])
    xn = sb("d_xn", [P, 2, TPG, D])
    xt = sb("d_xt", [P, 2, GT])
    gate_h = sb("d_gate", [P, 2, BATCH, E])
    gate = gate_h[:, :, :, :].rearrange("p n b e -> p (n b) e")
    rsum = sb("d_rsum", [P, TILES])
    csum = sb("d_csum", [P, BATCH, E])
    gt = sb("d_gt", [P, 2, SEQ])
    wk = sb("d_wk", [P, 2, 2, SEQ])
    top8 = sb("d_top8", [P, 2, 8])
    alive = sb("d_alive", [P, 2, TILES])
    s_w, s_one = sem("s_d_w"), sem("s_d_one")
    s_xn, s_xtp, s_xt, s_lp, s_l = (sem("s_d_" + n) for n in ("xn", "xt_p", "xt", "logit_p", "logit"))

    def normalise(dve, g, u):
        for j in range(TPG):
            ins = nc.vector.tensor_scalar(xn[:, u, j, :], h[:, dyn(g * TPG + j, 1), :], mean[:, dyn(g * TPG + j, 1)],
                                          rstd[:, dyn(g * TPG + j, 1)], ALU.subtract, ALU.mult)
        return ins

    with nc.Block() as block:
        @block.sync
        def _(sp):
            sp.dma_start(wg[:, :], t["wg"]).then_inc(s_w, 16)
            sp.dma_start(we[:, :, :], t["we"]).then_inc(s_w, 16)

        @block.gpsimd
        def _(pool):
            nc.gpsimd.memset(ones[:, :], 1.0).then_inc(s_one, 1)

        @block.vector
        def _(dve):
            dve.sem_inc(s_l, 2)
            with dve.Fori(0, GROUPS // 2) as i:
                for u in range(2):
                    g = 2 * i + u
                    dve.wait_ge(s_xtp, g + 1)
                    normalise(dve, g, u).then_inc(s_xn, 1)
                for u in range(2):
                    g = 2 * i + u
                    dve.wait_ge(s_lp, g + 1 + 2)
                    nc.vector.tensor_scalar(gate_h[:, :, dyn(2 * g, 2), :],
                                            bank[2 + u][:, 0:TPG * E].rearrange("p (b n e) -> p n b e", b=2, n=2),
                                            GATE_EPS, None, ALU.max).then_inc(s_l, 1)

        @block.tensor
        def _(pe):
            pe.sem_inc(s_xtp, 2)
            pe.sem_inc(s_lp, 2)
            pe.wait_ge(s_w, 32)
            with pe.Fori(0, GROUPS // 2) as i:
                for u in range(2):
                    g = 2 * i + u
                    pe.wait_ge(s_xn, g + 1)
                    pe.wait_ge(s_xt, g + 1)
                    for j in range(TPG):
                        mm = nc.tensor.transpose(bank[u][:, j * P:(j + 1) * P], xn[:, u, j, :], ident[:, :])
                    mm.then_inc(s_xtp, 1)
                for u in range(2):
                    g = 2 * i + u
                    pe.wait_ge(s_xt, g + 1 + 2)
                    pe.wait_ge(s_l, g + 1)
                    for j in range(TPG):
                        mm = nc.tensor.matmul(bank[2 + u][:, j * E:(j + 1) * E], xt[:, u, j * P:(j + 1) * P],
                                              wg[:, :], start=True, stop=True)
                    mm.then_inc(s_lp, 1)

        @block.scalar
        def _(act):
            act.sem_inc(s_xt, 2)
            with act.Fori(0, GROUPS // 2) as i:
                for u in range(2):
                    g = 2 * i + u
                    act.wait_ge(s_xtp, g + 1 + 2)
                    act.wait_ge(s_lp, g + 1)
                    nc.scalar.copy(xt[:, u, :], bank[u][:, :]).then_inc(s_xt, 1)

    s_v, s_cp, s_gp, s_bp = sem("s_d_chain"), sem("s_d_col_p"), sem("s_d_gt_p"), sem("s_d_back_p")
    with nc.Block() as block:
        @block.vector
        def _(dve):
            count = [0]

            def step(ins):
                count[0] += 1
                ins.then_inc(s_v, 1)
                dve.wait_ge(s_v, count[0])

            for it in range(SINKHORN):
                dve.wait_ge(s_cp, it + 1)
                step(nc.vector.reciprocal(csum[:, :, :], bank[0][:, 0:BATCH * E].rearrange("p (b e) -> p b e", e=E)))
                step(nc.vector.tensor_tensor(gate_h[:, :, :, :].rearrange("p n b e -> p n (b e)"),
                                             gate_h[:, :, :, :].rearrange("p n b e -> p n (b e)"),
                                             csum[:, :, :].rearrange("p (o b) e -> p o (b e)", o=1)
                                             .broadcast_to([P, 2, BATCH * E]), ALU.mult))
                step(nc.vector.tensor_reduce(rsum[:, :], gate[:, :, :], AX.X, ALU.add))
                step(nc.vector.reciprocal(rsum[:, :], rsum[:, :]))
                step(nc.vector.tensor_tensor(gate[:, :, :], gate[:, :, :],
                                             rsum[:, :].rearrange("p (t o) -> p t o", o=1)
                                             .broadcast_to([P, TILES, E]), ALU.mult))
            dve.wait_ge(s_gp, 1)
            step(nc.vector.tensor_copy(gt[:, :, :].rearrange("p m n -> p (m n)"), bank[1][:, :]))
            for m in range(2):
                src = gt[:, m, :]
                for r in range(CAP // 8):
                    dst = wk[:, m, r % 2, :]
                    step(nc.vector.max(top8[:, m, :], src))
                    step(nc.vector.match_replace(dst, top8[:, m, :], src, -1.0))
                    src = dst
                step(nc.vector.scalar_tensor_tensor(gt[:, m, :], src, 0.0, gt[:, m, :], ALU.is_lt, ALU.mult))
            dve.wait_ge(s_bp, 1)
            for m in range(2):
                for n in range(2):
                    step(nc.vector.tensor_copy(
                        gate_h[:, n, HB * m:HB * (m + 1), :],
                        bank[2][:, (2 * m + n) * P:(2 * m + n + 1) * P].rearrange("p (b e) -> p b e", e=E)))
            step(nc.vector.memset(alive[:, 0, :], 1.0))
            for e in range(E - 1, -1, -1):
                a, b = (E - 1 - e) % 2, (E - e) % 2
                step(nc.vector.scalar_tensor_tensor(alive[:, b, :], gate[:, :, e], 0.0, alive[:, a, :],
                                                    ALU.is_equal, ALU.mult))
                step(nc.vector.tensor_tensor(gate[:, :, e], gate[:, :, e], alive[:, a, :], ALU.mult))

        @block.tensor
        def _(pe):
            pe.wait_ge(s_one, 1)
            for it in range(SINKHORN):
                if it:
                    pe.wait_ge(s_v, 5 * it)
                for n in range(2):
                    mm = nc.tensor.matmul(bank[0][:, 0:BATCH * E], ones[:, :], gate_h[:, n, :, :].rearrange("p b e -> p (b e)"), start=(n == 0),
                                          stop=(n == 1))
                mm.then_inc(s_cp, 1)
            pe.wait_ge(s_v, 5 * SINKHORN)
            for m in range(2):
                for n in range(2):
                    mm = nc.tensor.transpose(bank[1][:, (2 * m + n) * P:(2 * m + n + 1) * P],
                                             gate_h[:, n, HB * m:HB * (m + 1), :].rearrange("p b e -> p (b e)"), ident[:, :])
            mm.then_inc(s_gp, 1)
            pe.wait_ge(s_v, 5 * SINKHORN + 1 + 2 * (2 * (CAP // 8) + 1))
            for m in range(2):
                for n in range(2):
                    mm = nc.tensor.transpose(bank[2][:, (2 * m + n) * P:(2 * m + n + 1) * P],
                                             gt[:, m, n * P:(n + 1) * P], ident[:, :])
            mm.then_inc(s_bp, 1)

    s2_xn, s2_xtp, s2_xt, s2_yp, s2_y, s2_c = (sem("s_e_" + n) for n in ("xn", "xt_p", "xt", "y_p", "y", "chain"))
    with nc.Block() as block:
        @block.vector
        def _(dve):
            dve.sem_inc(s2_y, 2)
            dve.sem_inc(s2_c, 1)
            with dve.Fori(0, GROUPS // 2) as i:
                for u in range(2):
                    g = 2 * i + u
                    dve.wait_ge(s2_xtp, g + 1)
                    normalise(dve, g, u).then_inc(s2_xn, 1)
                for u in range(2):
                    g = 2 * i + u
                    for j in range(TPG):
                        tl = g * TPG + j
                        dve.wait_ge(s2_yp, tl + 1)
                        for e in range(E):
                            y = bank[2 + 2 * (j % 2) + e // 4][:, (e % 4) * D:(e % 4 + 1) * D]
                            dve.wait_ge(s2_c, tl * E + e + 1)
                            ins = nc.vector.scalar_tensor_tensor(h[:, dyn(tl, 1), :], y, gate_h[:, j % 2, dyn(2 * g + j // 2, 1), e],
                                                                 h[:, dyn(tl, 1), :], ALU.mult, ALU.add)
                            ins.then_inc(s2_c, 1)
                        dve.wait_ge(s2_c, tl * E + E + 1)
                        dve.sem_inc(s2_y, 1)

        @block.tensor
        def _(pe):
            pe.sem_inc(s2_xtp, 2)
            with pe.Fori(0, GROUPS // 2) as i:
                for u in range(2):
                    g = 2 * i + u
                    pe.wait_ge(s2_xn, g + 1)
                    pe.wait_ge(s2_xt, g + 1)
                    for j in range(TPG):
                        mm = nc.tensor.transpose(bank[u][:, j * P:(j + 1) * P], xn[:, u, j, :], ident[:, :])
                    mm.then_inc(s2_xtp, 1)
                for u in range(2):
                    g = 2 * i + u
                    pe.wait_ge(s2_xt, g + 1 + 2)
                    for j in range(TPG):
                        tl = g * TPG + j
                        pe.wait_ge(s2_y, tl + 1)
                        for k in range(2):
                            mm = nc.tensor.matmul(bank[2 + 2 * (j % 2) + k][:, :], xt[:, u, j * P:(j + 1) * P],
                                                  we[:, 4 * k:4 * k + 4, :].rearrange("p e d -> p (e d)"), start=True,
                                                  stop=True)
                        mm.then_inc(s2_yp, 1)

        @block.scalar
        def _(act):
            act.sem_inc(s2_xt, 2)
            with act.Fori(0, GROUPS // 2) as i:
                for u in range(2):
                    g = 2 * i + u
                    act.wait_ge(s2_xtp, g + 1 + 2)
                    nc.scalar.copy(xt[:, u, :], bank[u][:, :]).then_inc(s2_xt, 1)


def kernel(**inputs):
    import numpy as np
    import concourse.bacc as bacc
    from concourse.bass_utils import run_bass_kernel_spmd as run

    nc = bacc.Bacc("TRN2", target_bir_lowering=False, num_devices=1)
    arrays, t = {}, {}

    def give(name, a):
        a = np.ascontiguousarray(a)
        arrays[f"in_{name}"] = a
        t[name] = nc.dram_tensor(f"in_{name}", a.shape, mybir.dt.from_np(a.dtype), kind="ExternalInput").ap()

    x = {k: np.asarray(v) for k, v in inputs.items()}
    give("x", x["x"])
    give("emb", x["L0_tok_emb_weight"])
    give("conv", x["L0_tok_conv_weight"].reshape(D, 2).T)
    wqkv, bqkv = x["L0_attn_Wqkv"], x["L0_attn_bqkv"]
    wqk = np.zeros((D, 4, 4, 32), wqkv.dtype)
    bqk = np.zeros((4, 32, 4), bqkv.dtype)
    lam = np.zeros((4, 32, 2), bqkv.dtype)
    for j in range(4):
        for r in range(4):
            at = (j // 2) * D + (4 * (j % 2) + r) * E0
            wqk[:, j, r, :E0] = wqkv[:, at:at + E0]
            bqk[r, :E0, j] = bqkv[at:at + E0]
            if j < 2:
                lam[r, :E0, j] = x["L0_attn_decay_logits"][4 * j + r]
    give("wqk", wqk.reshape(D, 4, P))
    give("bqk", bqk.reshape(P, 4))
    give("lam", lam.reshape(P, 2))
    give("wv", wqkv[:, 2 * D:])
    give("wo", x["L0_attn_Wout"])
    give("rows0", np.stack([bqkv[2 * D:], x["L0_attn_bout"], x["L0_attn_ln_gamma"], x["L0_attn_ln_beta"]]))
    give("wr", np.concatenate([x["L0_ffn_Wr"], x["L0_ffn_Wgate"].transpose(1, 0, 2).reshape(D, EXPERTS)], axis=1))
    give("br", np.concatenate([x["L0_ffn_br"], x["L0_ffn_bgate"].reshape(-1)]))
    for k in ("w1", "w3", "w2"):
        give(k, x["L0_ffn_" + k.upper()])
    inner = HEADS1 * DH1
    give("wx", x["L1_attn_Wx"].reshape(HEADS1, DH1, D).transpose(1, 0, 2))
    give("bx", x["L1_attn_bx"].reshape(HEADS1, DH1).T)
    give("wsl", x["L1_attn_Wslice"].T)
    give("bsl", x["L1_attn_bslice"])
    give("temp", x["L1_attn_temperature"].reshape(HEADS1))
    give("wqkv1", np.stack([x["L1_attn_Wq"], x["L1_attn_Wk"], x["L1_attn_Wv"]], axis=1))
    give("wot", x["L1_attn_Wout"].T.reshape(HEADS1, DH1, D).transpose(1, 0, 2))
    give("wfx", x["L1_attn_Wfx"].T.reshape(D, HEADS1, DH1))
    give("bfx", x["L1_attn_bfx"].reshape(1, HEADS1, DH1))
    give("bo1", x["L1_attn_bout"])
    give("wg", x["L1_ffn_gate_weight"][0])
    give("we", x["L1_ffn_experts"].transpose(1, 0, 2))
    out = nc.dram_tensor("out_0_dram", (BATCH * SEQ, D), F32, kind="ExternalOutput").ap()
    tower(nc, t, out)
    r = run(nc, [arrays], core_ids=[0])
    return r.results[0]["out_0_dram"].reshape(BATCH, SEQ, D)
```

```python
from contextlib import ExitStack

import concourse.bass as bass
from concourse import mybir

ALU = mybir.AluOpType
ACT = mybir.ActivationFunctionType
AX = mybir.AxisListType
F32 = mybir.dt.float32
I32 = mybir.dt.int32
U32 = mybir.dt.uint32
F16 = mybir.dt.float16
RMAX = bass.bass_isa.ReduceOp.max


P = 128
D = 128
BATCH, SEQ = 32, 256
VOCAB = 125
TILES = BATCH * SEQ // P
TPG = 4
GROUPS = TILES // TPG
GT = TPG * P
HEADS0, E0 = 8, 16
ROUND = 12582912.0
LN_EPS = 1e-5
GRP, EXPERTS, HID = 4, 16, 512
TOP_P = 0.9
PAIRS = 6
BUCKETS = GRP * PAIRS
SLOTS = 2 * TILES + BUCKETS
ROW = D + 4
W_SCALE, W_HID = 64.0, 0.25
HEADS1, DH1, SLICES = 8, 64, 32
GATES, SINKHORN, GATE_EPS = 8, 8, 1e-6


def dyn(i, n):
    return bass.ds(i, n)


def layer_stats(nc, ctx, stats, mean, rstd, eps_t, s_ln, turn):
    tmp = ctx.enter_context(nc.sbuf_tensor(f"ln_tmp_{turn}", [P, 3, TILES], F32))
    (s_v, s_sq), n_v, n_sq = s_ln, 7 * turn, turn

    with nc.Block() as block:
        @block.vector
        def _(dve):
            m_even, m_odd = stats[:, :, 1], stats[:, :, 4]
            nc.vector.tensor_tensor(tmp[:, 0, :], m_even, m_odd, ALU.subtract).then_inc(s_v, 1)
            nc.vector.tensor_tensor(tmp[:, 1, :], m_even, m_odd, ALU.add).then_inc(s_v, 1)
            nc.vector.tensor_tensor(tmp[:, 2, :], stats[:, :, 2], stats[:, :, 5], ALU.add).then_inc(s_v, 1)
            dve.wait_ge(s_v, n_v + 3)
            nc.vector.tensor_scalar(mean[:, :], tmp[:, 1, :], 0.5, None, ALU.mult).then_inc(s_v, 1)
            nc.vector.scalar_tensor_tensor(tmp[:, 0, :], tmp[:, 0, :], 0.25, tmp[:, 0, :],
                                           ALU.mult, ALU.mult).then_inc(s_v, 1)
            dve.wait_ge(s_v, n_v + 5)
            nc.vector.scalar_tensor_tensor(tmp[:, 2, :], tmp[:, 2, :], 1.0 / D, tmp[:, 0, :],
                                           ALU.mult, ALU.add).then_inc(s_v, 1)
            dve.wait_ge(s_sq, n_sq + 1)
            nc.vector.reciprocal(rstd[:, :], tmp[:, 1, :]).then_inc(s_v, 1)

        @block.scalar
        def _(act):
            act.wait_ge(s_v, n_v + 6)
            nc.scalar.activation(tmp[:, 1, :], tmp[:, 2, :], ACT.Sqrt, bias=eps_t[:, 0:1]).then_inc(s_sq, 1)


def tower(nc, t, out):
    ctx = ExitStack()
    with ctx:
        def sbp(c, name, shape, dt=F32):
            return c.enter_context(nc.sbuf_tensor(name, shape, dt))

        def sem(c, name):
            return c.enter_context(nc.semaphore(name))

        h = sbp(ctx, "h", [P, TILES, D])
        stats = sbp(ctx, "stats", [P, TILES, 6])
        mean = sbp(ctx, "mean", [P, TILES])
        rstd = sbp(ctx, "rstd", [P, TILES])
        ident = sbp(ctx, "ident", [P, P])
        causal = sbp(ctx, "causal", [P, P])
        iota_p = sbp(ctx, "iota_p", [P, 1])
        eps_t = sbp(ctx, "eps_t", [P, 1])
        bank = [ctx.enter_context(nc.psum_tensor(f"bank{i}", [P, 512], F32)) for i in range(8)]

        s_setup = sem(ctx, "s_setup")
        s_ln = (sem(ctx, "s_ln_vec"), sem(ctx, "s_ln_sqrt"))
        with nc.Block() as block:
            @block.gpsimd
            def _(pool):
                nc.gpsimd.memset(ident[:, :], 0.0).then_inc(s_setup, 1)
                nc.gpsimd.memset(causal[:, :], 1.0).then_inc(s_setup, 1)
                pool.wait_ge(s_setup, 2)
                nc.gpsimd.affine_select(out=ident[:, :], in_=ident[:, :], compare_op=ALU.not_equal, fill=1.0,
                                        base=0, pattern=[[-1, P]], channel_multiplier=1).then_inc(s_setup, 1)
                nc.gpsimd.affine_select(out=causal[:, :], in_=causal[:, :], compare_op=ALU.is_ge, fill=0.0,
                                        base=0, pattern=[[1, P]], channel_multiplier=-1).then_inc(s_setup, 1)
                nc.gpsimd.iota(iota_p[:, :], pattern=[[0, 1]], base=0, channel_multiplier=1,
                               allow_small_or_imprecise_dtypes=True).then_inc(s_setup, 1)
                nc.gpsimd.memset(eps_t[:, :], LN_EPS).then_inc(s_setup, 1)

        x_sorted = nc.dram_tensor("x_sorted", (SLOTS * P, ROW), F32).ap()
        y_sorted = nc.dram_tensor("y_sorted", (SLOTS * P, D), F32).ap()
        with ExitStack() as c:
            embed_phase(nc, c, t, h, stats, bank, iota_p, x_sorted)
        with ExitStack() as c:
            layer_stats(nc, c, stats, mean, rstd, eps_t, s_ln, 0)
            attention_phase(nc, c, t, h, stats, mean, rstd, bank, ident, causal, eps_t, s_ln)

        with ExitStack() as c:
            layer_stats(nc, c, stats, mean, rstd, eps_t, s_ln, 2)
            pos = sbp(c, "pos", [P, TILES, 2], I32)
            wrow = sbp(c, "wrow", [P, TILES, 2, 2])
            experts = sbp(c, "experts", [1, SLOTS, 2], I32)
            with ExitStack() as c2:
                routing_phase(nc, c2, t, h, mean, rstd, bank, ident, causal, pos, wrow, experts)
            with ExitStack() as c2:
                sorted_ffn_phase(nc, c2, t, h, mean, rstd, bank, ident, pos, wrow, experts, x_sorted, y_sorted, stats)
        with ExitStack() as c:
            layer_stats(nc, c, stats, mean, rstd, eps_t, s_ln, 3)
            slice_attention_phase(nc, c, t, h, stats, mean, rstd, bank, ident)
        with ExitStack() as c:
            layer_stats(nc, c, stats, mean, rstd, eps_t, s_ln, 4)
            expert_choice_phase(nc, c, t, h, mean, rstd, bank, ident)

        s_out = sem(ctx, "s_out")
        with nc.Block() as block:
            @block.sync
            def _(sp):
                ov = out.rearrange("(t p) d -> p t d", p=P)
                for q in range(4):
                    n = TILES // 4
                    sp.dma_start(ov[:, q * n:(q + 1) * n, :], h[:, q * n:(q + 1) * n, :]).then_inc(s_out, 16)
                sp.wait_ge(s_out, 64)


def embed_phase(nc, c, t, h, stats, bank, iota_p, x_sorted):
    def sb(name, shape, dt=F32):
        return c.enter_context(nc.sbuf_tensor(name, shape, dt))

    def sem(name):
        return c.enter_context(nc.semaphore(name))

    TAPS = 2
    ids = sb("ids", [P, BATCH, SEQ], I32)
    emb = sb("emb", [P, D])
    taps = sb("taps", [P, TAPS, D])
    work = sb("q_work", [P, 3, TAPS, D])
    amax = sb("amax", [P, 8])
    FILLS = 8
    zero = sb("zero_rows", [P, SLOTS // FILLS, ROW])
    s_fill, s_zeros = sem("s_emb_fill"), sem("s_emb_zeros")
    table = sb("table", [P, TAPS, D])
    onehot = sb("onehot", [P, 2, 2, SEQ + 1])

    s_in = sem("s_emb_in")
    s_ids = [sem(f"s_ids{q}") for q in range(4)]
    s_zero = sem("s_emb_zero")
    s_q = sem("s_quant")
    s_amax = sem("s_amax")
    s_oh = sem("s_onehot")
    s_rows = sem("s_emb_rows")
    s_h = sem("s_emb_h")
    s_st = sem("s_emb_stats")

    with nc.Block() as block:
        @block.sync
        def _(sp):
            sp.wait_ge(s_zero, 1)
            sp.dma_start(emb[0:VOCAB, :], t["emb"]).then_inc(s_in, 16)
            sp.dma_start(taps[:, :, :], t["conv"].partition_broadcast(P)).then_inc(s_in, 16)
            for q in range(4):
                n = BATCH // 4
                sp.dma_start(ids[:, q * n:(q + 1) * n, :],
                             t["x"][q * n:(q + 1) * n, :].partition_broadcast(P)).then_inc(s_ids[q], 16)
            sp.wait_ge(s_fill, 1)
            n = SLOTS // FILLS
            for k in range(FILLS):
                sp.dma_start(x_sorted.rearrange("(s p) d -> p s d", p=P)[:, k * n:(k + 1) * n, :], zero[:, :, :])\
                    .then_inc(s_zeros, 16)
            sp.wait_ge(s_zeros, 16 * FILLS)

        @block.gpsimd
        def _(pool):
            nc.gpsimd.memset(emb[:, :], 0.0).then_inc(s_zero, 1)
            nc.gpsimd.memset(onehot[:, :, :, :], 0.0).then_inc(s_zero, 1)
            nc.gpsimd.memset(zero[:, :, :], 0.0).then_inc(s_fill, 1)
            for k in range(2):
                pool.wait_ge(s_q, 2 * k + 2)
                nc.gpsimd.partition_all_reduce(amax[:, 2 + k:3 + k], amax[:, k:k + 1], P, RMAX).then_inc(s_amax, 1)

        @block.vector
        def _(dve):
            count = [0]

            def step(ins):
                count[0] += 1
                ins.then_inc(s_q, 1)
                dve.wait_ge(s_q, count[0])

            dve.wait_ge(s_in, 32)
            mats = [(emb[:, :], work[:, 0, 0, :], work[:, 1, 0, :]),
                    (taps[:, :, :], work[:, 0, :, :], work[:, 1, :, :])]
            for k, (w, a, _) in enumerate(mats):
                step(nc.vector.scalar_tensor_tensor(a, w, -1.0, w, ALU.mult, ALU.max))
                step(nc.vector.tensor_reduce(amax[:, k:k + 1], a, AX.X if k == 0 else AX.XY, ALU.max))
            for k, (w, a, b) in enumerate(mats):
                dve.wait_ge(s_amax, k + 1)
                scale, inv = amax[:, 4 + k:5 + k], amax[:, 6 + k:7 + k]
                step(nc.vector.tensor_scalar(scale, amax[:, 2 + k:3 + k], 1.0 / 127.0, None, ALU.mult))
                step(nc.vector.reciprocal(inv, scale))
                step(nc.vector.tensor_scalar(a, w, inv, ROUND, ALU.mult, ALU.add))
                step(nc.vector.tensor_scalar(a, a, ROUND, scale, ALU.subtract, ALU.mult))
                step(nc.vector.tensor_tensor(b, a, w, ALU.subtract))
                step(nc.vector.tensor_tensor(w, w, b, ALU.add))
            for k in range(TAPS):
                step(nc.vector.tensor_tensor(table[:, k, :], emb[:, :], taps[:, k, :], ALU.mult))

            dve.wait_ge(s_zero, 2)
            for q in range(4):
                dve.wait_ge(s_ids[q], 16)
            with dve.Fori(0, GROUPS // 2) as i:
                for u in range(2):
                    g = 2 * i + u
                    dve.wait_ge(s_rows, TPG * g + TPG)
                    nc.vector.tensor_scalar(onehot[:, u, :, 1:SEQ + 1], ids[:, dyn(2 * g, 2), :], float(VOCAB - 1),
                                            iota_p[:, 0:1], ALU.min, ALU.is_equal).then_inc(s_oh, 1)
                for u in range(2):
                    for j in range(TPG):
                        tile = (2 * i + u) * TPG + j
                        dve.wait_ge(s_h, tile + 1 + 2 * TPG)
                        nc.vector.bn_stats(stats[:, dyn(tile, 1), :], h[:, dyn(tile, 1), :]).then_inc(s_st, 1)

        @block.tensor
        def _(pe):
            pe.sem_inc(s_rows, 2 * TPG)
            pe.wait_ge(s_q, 18)
            with pe.Fori(0, GROUPS // 2) as i:
                for u in range(2):
                    g = 2 * i + u
                    pe.wait_ge(s_oh, g + 1)
                    for j in range(TPG):
                        b, at = j // 2, (j % 2) * P
                        pe.wait_ge(s_h, g * TPG + j + 1)
                        for k in range(TAPS):
                            mm = nc.tensor.matmul(bank[u * TPG + j][:, 0:D], onehot[:, u, b, at + k:at + k + P],
                                                  table[:, k, :], start=(k == 0), stop=(k == TAPS - 1))
                        mm.then_inc(s_rows, 1)

        @block.scalar
        def _(act):
            act.sem_inc(s_h, 2 * TPG)
            with act.Fori(0, GROUPS // 2) as i:
                for u in range(2):
                    g = 2 * i + u
                    for j in range(TPG):
                        act.wait_ge(s_rows, g * TPG + j + 1 + 2 * TPG)
                        nc.scalar.activation(h[:, dyn(g * TPG + j, 1), :], bank[u * TPG + j][:, 0:D],
                                             ACT.Relu).then_inc(s_h, 1)


def attention_phase(nc, c, t, h, stats, mean, rstd, bank, ident, causal, eps_t, s_ln):
    def sb(name, shape, dt=F32):
        return c.enter_context(nc.sbuf_tensor(name, shape, dt))

    def sem(name):
        return c.enter_context(nc.semaphore(name))

    H, E, R, V = HEADS0, E0, 4, E0 + 1
    NQK = 4
    PHI, PROB = 32.0, 16.0
    wall = sb("wall", [P, (NQK + 1) * P])
    wh = sb("wh", [P, (NQK + 1) * P], F16)
    wl = sb("wlo", [P, (NQK + 1) * P], F16)
    bqk = sb("bqk", [P, 2, NQK])
    wo = sb("wo", [P, D])
    rows = sb("rows0", [P, 4, D])
    lam = sb("lam", [P, 2])
    valid = sb("valid", [P, 2])
    powr = sb("powr", [P, 8, 2])
    fade = sb("fade", [P, 2, 2 * P])
    logits = sb("logits", [P, H])
    powh = sb("powh", [P, 7, H])
    tri = sb("tri", [P, H, P])
    diag = sb("diag", [P, H, P])
    tri4 = sb("tri4", [P, R, 4, P])
    bv4 = sb("bv4", [P, GT])
    col = sb("col", [P, 3, H])
    bdiag = sb("bdiag", [P, 2, R, V])

    o_all = sb("o_all", [P, TILES, D])
    xn = sb("xn", [P, 2, TPG, D])
    xh = sb("xh", [P, 2, GT], F16)
    xl = sb("xl", [P, 2, GT], F16)
    ebuf = sb("ebuf", [P, 2, GT])
    xbuf = sb("xbuf", [P, 2, GT])
    phi = sb("phi", [P, 2, NQK, GT])
    ph = sb("ph", [P, 2, NQK, GT], F16)
    pl = sb("pl", [P, 2, NQK, GT], F16)
    qd = sb("qd", [P, 2, 2, 2, P])
    vh = sb("vh", [P, 2, TPG, H, V], F16)
    vl = sb("vl", [P, 2, TPG, H, V], F16)
    v1 = sb("v1", [P, 2, TPG, H, V])
    ktok = sb("ktok", [P, 2 * P])
    state = sb("state", [P, 2, R * V])
    prob = sb("prob", [P, R, 4, P])
    prh = sb("prh", [P, R, 4, P], F16)
    prl = sb("prl", [P, R, 4, P], F16)
    den = sb("den", [P, 2, H])
    on = sb("on", [P, 2, D])
    ot = sb("ot", [P, 2 * P])
    off = sb("off", [P, 2, D])

    s_w = sem("s_a_weights")
    s_c = sem("s_a_consts")
    s_e = sem("s_a_exp")
    s_pool = sem("s_a_pool")
    names = ("xn", "xt_p", "xh", "xl", "qk_p", "qk_e", "elu", "ph", "pl", "qd", "v_p", "v", "vh", "vl", "kt_p", "kt",
             "st_p", "st", "sc_p", "sc", "prh", "prl", "pv_p", "den", "on", "ot_p", "ot", "o_p", "o")
    S = {n: sem("s_a_" + n) for n in names}

    with nc.Block() as block:
        @block.sync
        def _(sp):
            sp.dma_start(wall[:, 0:NQK * P], t["wqk"].rearrange("p j d -> p (j d)")).then_inc(s_w, 16)
            sp.dma_start(wall[:, NQK * P:], t["wv"]).then_inc(s_w, 16)
            sp.dma_start(bqk[:, 0, :], t["bqk"]).then_inc(s_w, 16)
            sp.dma_start(wo[:, :], t["wo"]).then_inc(s_w, 16)
            sp.dma_start(rows[:, :, :], t["rows0"].partition_broadcast(P)).then_inc(s_w, 16)
            sp.dma_start(lam[:, :], t["lam"]).then_inc(s_w, 16)
            sp.dma_start(logits[:, :], t["logits"].partition_broadcast(P)).then_inc(s_w, 16)

        @block.gpsimd
        def _(pool):
            nc.gpsimd.memset(valid[:, 0:1], 0.0).then_inc(s_pool, 1)
            nc.gpsimd.memset(valid[:, 1:2], 1.0).then_inc(s_pool, 1)
            nc.gpsimd.memset(bdiag[:, :, :, :], 0.0).then_inc(s_pool, 1)
            nc.gpsimd.memset(v1[:, :, :, :, :], 1.0).then_inc(s_pool, 1)
            pool.wait_ge(s_pool, 4)
            for r in range(R):
                nc.gpsimd.memset(valid[32 * r:32 * r + E, 0:1], 1.0).then_inc(s_pool, 1)
                nc.gpsimd.memset(valid[32 * r:32 * r + E, 1:2], 0.0).then_inc(s_pool, 1)
                nc.gpsimd.memset(bdiag[32 * r:32 * r + 32, :, r, :], 1.0).then_inc(s_pool, 1)

        @block.scalar
        def _(act):
            act.wait_ge(s_w, 112)
            nc.scalar.activation(lam[:, :], lam[:, :], ACT.Exp, scale=-1.0).then_inc(s_e, 1)
            nc.scalar.activation(logits[:, :], logits[:, :], ACT.Exp, scale=-1.0).then_inc(s_e, 1)
            nc.scalar.activation(wh[:, :], wall[:, :], ACT.Copy, scale=W_SCALE).then_inc(s_e, 1)

        @block.vector
        def _(dve):
            count = [0]

            def step(*links):
                for ins in links:
                    ins.then_inc(s_c, 1)
                count[0] += len(links)
                dve.wait_ge(s_c, count[0])

            def over_t(a):
                return a.rearrange("p (h o) -> p h o", o=1).broadcast_to([P, H, P])

            dve.wait_ge(s_pool, 4 + 3 * R)
            dve.wait_ge(s_e, 3)
            step(nc.vector.tensor_scalar(lam[:, :], lam[:, :], 1.0, None, ALU.add),
                 nc.vector.tensor_scalar(logits[:, :], logits[:, :], 1.0, None, ALU.add),
                 nc.vector.scalar_tensor_tensor(wl[:, :], wall[:, :], W_SCALE, wh[:, :], ALU.mult, ALU.subtract))
            step(nc.vector.reciprocal(lam[:, :], lam[:, :]),
                 nc.vector.reciprocal(powh[:, 0, :], logits[:, :]))
            step(nc.vector.tensor_scalar(powr[:, 0, :], lam[:, :], valid[:, 0:1], valid[:, 1:2], ALU.mult, ALU.add),
                 nc.vector.tensor_scalar(bqk[:, 1, :], bqk[:, 0, :], valid[:, 0:1], None, ALU.add),
                 nc.vector.tensor_scalar(col[:, 0, 0:1], valid[:, 1:2], -1e4, None, ALU.mult),
                 nc.vector.memset(fade[:, :, 0:1], 1.0),
                 nc.vector.memset(tri[:, :, 0:1], 1.0))
            step(nc.vector.tensor_scalar(bqk[:, 0, :], bqk[:, 0, :], col[:, 0, 0:1], None, ALU.add))
            for k in range(8):
                n = 1 << k
                links = [nc.vector.tensor_scalar(fade[:, i, n:2 * n], fade[:, i, 0:n], powr[:, k, i:i + 1],
                                                 None, ALU.mult) for i in range(2)]
                if k < 7:
                    links.append(nc.vector.tensor_tensor(tri[:, :, n:2 * n], tri[:, :, 0:n], powh[:, k, :]
                                                         .rearrange("p (h o) -> p h o", o=1).broadcast_to([P, H, n]),
                                                         ALU.mult))
                    links.append(nc.vector.tensor_tensor(powr[:, k + 1, :], powr[:, k, :], powr[:, k, :], ALU.mult))
                if k < 6:
                    links.append(nc.vector.tensor_tensor(powh[:, k + 1, :], powh[:, k, :], powh[:, k, :], ALU.mult))
                step(*links)
            step(nc.vector.reciprocal(col[:, 1, :], tri[:, :, P // 2]),
                 nc.vector.tensor_scalar(fade[:, :, 1:P + 1], fade[:, :, 1:P + 1], PROB * E ** -0.5, valid[:, 0:1],
                                         ALU.mult, ALU.mult))
            step(nc.vector.tensor_tensor(tri[:, :, :], tri[:, :, :], over_t(col[:, 1, :]), ALU.mult))
            step(nc.vector.tensor_tensor(diag[:, :, :], tri[:, :, :], ident[:, :].rearrange("p (o t) -> p o t", o=1)
                                         .broadcast_to([P, H, P]), ALU.mult))
            step(nc.vector.tensor_reduce(col[:, 0, :], diag[:, :, :], AX.X, ALU.add))
            step(nc.vector.reciprocal(col[:, 1, :], col[:, 0, :]))
            step(nc.vector.tensor_tensor(col[:, 2, :], col[:, 1, :], tri[:, :, P - 1], ALU.mult))
            step(nc.vector.tensor_tensor(tri[:, :, :], tri[:, :, :], over_t(col[:, 1, :]), ALU.mult))
            step(nc.vector.scalar_tensor_tensor(
                tri[:, :, :], tri[:, :, :], PROB * E ** -0.5 / (PHI * PHI),
                causal[:, :].rearrange("p (o t) -> p o t", o=1).broadcast_to([P, H, P]), ALU.mult, ALU.mult))
            for j in range(2):
                for r in range(R):
                    nc.vector.tensor_copy(tri4[:, r, 2 * j:2 * j + 2, :],
                                          tri[:, :, :].rearrange("p (f r) t -> p r f t", r=R)[:, r, :, :])
            for j in range(TPG):
                nc.vector.tensor_copy(bv4[:, j * D:(j + 1) * D], rows[:, 0, :])

    def after(eng, sem, count):
        if not isinstance(count, int) or count > 0:
            eng.wait_ge(sem, count)

    def steps(eng, prologue, batch, epilogue):
        prologue()
        for u in range(2):
            for b in range(2):
                batch(u, u, b, u == 0 and b == 0, True, True)
        with eng.Fori(1, GROUPS // 2 - 1) as i:
            for u in range(2):
                for b in range(2):
                    batch(2 * i + u, u, b, False, True, True)
        for u in range(2):
            for b in range(2):
                batch(GROUPS - 2 + u, u, b, False, u == 0, False)
        epilogue()

    with nc.Block() as block:
        @block.tensor
        def _(pe):
            def transpose_rows(g, u):
                pe.wait_ge(S["xn"], g + 1)
                for j in range(TPG):
                    mm = nc.tensor.transpose(bank[0][:, j * P:(j + 1) * P], xn[:, u, j, :], ident[:, :])
                mm.then_inc(S["xt_p"], 1)

            def project(g, u, j):
                pe.wait_ge(S["xl"], g + 1)
                after(pe, S["qk_e"], NQK * g + j)
                hi, lo = wh[:, j * P:(j + 1) * P], wl[:, j * P:(j + 1) * P]
                nc.tensor.matmul(bank[1][:, :], hi, xh[:, u, :], start=True, stop=False)
                nc.tensor.matmul(bank[1][:, :], hi, xl[:, u, :], start=False, stop=False)
                nc.tensor.matmul(bank[1][:, :], lo, xh[:, u, :], start=False, stop=True).then_inc(S["qk_p"], 1)

            def values(g, u):
                hi, lo = wh[:, NQK * P:], wl[:, NQK * P:]
                for j in range(TPG):
                    y, at = bank[0][:, j * D:(j + 1) * D], slice(j * P, (j + 1) * P)
                    nc.tensor.matmul(y, xh[:, u, at], hi, start=(j == 0), stop=False, skip_group_check=True)
                    nc.tensor.matmul(y, xh[:, u, at], lo, start=False, stop=False, skip_group_check=True)
                    mm = nc.tensor.matmul(y, xl[:, u, at], hi, start=False, stop=True, skip_group_check=True)
                mm.then_inc(S["v_p"], 1)

            def keys(g, u, b):
                pe.wait_ge(S["elu"], NQK * g + NQK)
                for hf in range(2):
                    mm = nc.tensor.transpose(bank[2][:, hf * P:(hf + 1) * P],
                                             phi[:, u, 2 + hf, 2 * b * P:(2 * b + 1) * P], ident[:, :])
                mm.then_inc(S["kt_p"], 1)

            def scores(g, u, b, r):
                pe.wait_ge(S["pl"], NQK * g + NQK)
                for j in range(2):
                    for hf in range(2):
                        to = bank[4 + r][:, (2 * j + hf) * P:(2 * j + hf + 1) * P]
                        at = slice((2 * b + j) * P, (2 * b + j + 1) * P)
                        rr = slice(32 * r, 32 * r + 32)
                        nc.tensor.matmul(to, ph[rr, u, 2 + hf, at], ph[rr, u, hf, at],
                                         start=(j == 0 and hf == 0), stop=False, skip_group_check=True)
                        nc.tensor.matmul(to, ph[rr, u, 2 + hf, at], pl[rr, u, hf, at],
                                         start=False, stop=False, skip_group_check=True)
                        mm = nc.tensor.matmul(to, pl[rr, u, 2 + hf, at], ph[rr, u, hf, at],
                                              start=False, stop=True, skip_group_check=True)
                mm.then_inc(S["sc_p"], 1)

            def make_state(n, u, b):
                pe.wait_ge(S["kt"], n + 1)
                for hf in range(2):
                    mm = nc.tensor.matmul(bank[2][:, hf * R * V:(hf + 1) * R * V], ktok[:, hf * P:(hf + 1) * P],
                                          v1[:, u, 2 * b, R * hf:R * hf + R, :].rearrange("p h v -> p (h v)"),
                                          start=(hf == 0), stop=True, skip_group_check=True)
                mm.then_inc(S["st_p"], 1)

            def use_state(g, n, u, b):
                pe.wait_ge(S["st"], n + 1)
                pe.wait_ge(S["qd"], 2 * g + 2)
                after(pe, S["o"], n)
                for hf in range(2):
                    at = H * V + hf * R * V
                    nc.tensor.matmul(bank[3][:, at:at + R * V], qd[:, u, hf, b, :],
                                     state[:, hf, :], start=(hf == 0), stop=False, skip_group_check=True)

            def weigh(n, u, b, r):
                pe.wait_ge(S["prl"], 4 * n + r + 1)
                for j in range(2):
                    for hf in range(2):
                        hd = R * hf + r
                        at = j * H * V + hd * V
                        to = bank[3][:, at:at + V]
                        hi, lo = vh[:, u, 2 * b + j, hd, :], vl[:, u, 2 * b + j, hd, :]
                        nc.tensor.matmul(to, prh[:, r, 2 * j + hf, :], hi, start=False, stop=False, skip_group_check=True)
                        nc.tensor.matmul(to, prh[:, r, 2 * j + hf, :], lo, start=False, stop=False, skip_group_check=True)
                        mm = nc.tensor.matmul(to, prl[:, r, 2 * j + hf, :], hi, start=False, stop=True,
                                              skip_group_check=True)
                if r == R - 1:
                    mm.then_inc(S["pv_p"], 1)

            def transpose_out(n):
                pe.wait_ge(S["on"], n + 1)
                for j in range(2):
                    mm = nc.tensor.transpose(bank[3][:, j * P:(j + 1) * P], on[:, j, :], ident[:, :])
                mm.then_inc(S["ot_p"], 1)

            def project_out(n):
                pe.wait_ge(S["ot"], n + 1)
                for j in range(2):
                    mm = nc.tensor.matmul(bank[3][:, j * D:(j + 1) * D], ot[:, j * P:(j + 1) * P], wo[:, :],
                                          start=(j == 0), stop=True, skip_group_check=True)
                mm.then_inc(S["o_p"], 1)

            def prologue():
                transpose_rows(0, 0)
                for j in range(NQK):
                    project(0, 0, j)
                values(0, 0)

            def batch(g, u, b, first, more, more2):
                n = 2 * g + b
                keys(g, u, b)
                if b == 0:
                    pe.wait_ge(S["vl"], g + 1)
                    if more:
                        transpose_rows(g + 1, 1 - u)
                scores(g, u, b, 0)
                if b == 1 and more:
                    project(g + 1, 1 - u, 3)
                scores(g, u, b, 1)
                if not first:
                    transpose_out(n - 1)
                make_state(n, u, b)
                if b == 0 and more:
                    project(g + 1, 1 - u, 0)
                scores(g, u, b, 2)
                if not first:
                    project_out(n - 1)
                if more:
                    if b == 0:
                        project(g + 1, 1 - u, 1)
                    else:
                        values(g + 1, 1 - u)
                scores(g, u, b, 3)
                use_state(g, n, u, b)
                for r in range(R):
                    weigh(n, u, b, r)
                if b == 0 and more:
                    project(g + 1, 1 - u, 2)

            def epilogue():
                transpose_out(BATCH - 1)
                project_out(BATCH - 1)

            steps(pe, prologue, batch, epilogue)

        @block.scalar
        def _(act):
            def rows_hi(g, u):
                act.wait_ge(S["xt_p"], g + 1)
                nc.scalar.copy(xh[:, u, :], bank[0][:, :]).then_inc(S["xh"], 1)

            def exponent(g, j):
                act.wait_ge(S["qk_p"], NQK * g + j + 1)
                after(act, S["elu"], NQK * g + j - 1)
                nc.scalar.activation(ebuf[:, j % 2, :], bank[1][:, :], ACT.Exp, scale=1.0 / W_SCALE,
                                     bias=bqk[:, 0, j:j + 1])
                nc.scalar.activation(xbuf[:, j % 2, :], bank[1][:, :], ACT.Identity, scale=1.0 / W_SCALE,
                                     bias=bqk[:, 1, j:j + 1]).then_inc(S["qk_e"], 1)

            def phi_hi(g, u, j):
                act.wait_ge(S["elu"], NQK * g + j + 1)
                nc.scalar.activation(ph[:, u, j, :], phi[:, u, j, :], ACT.Copy, scale=PHI).then_inc(S["ph"], 1)

            def prob_hi(n, r):
                act.wait_ge(S["sc"], 4 * n + r + 1)
                nc.scalar.copy(prh[:, r, :, :].rearrange("p x q -> p (x q)"),
                               prob[:, r, :, :].rearrange("p x q -> p (x q)")).then_inc(S["prh"], 1)

            def v_hi(g, u):
                act.wait_ge(S["v"], g + 1)
                nc.scalar.copy(vh[:, u, :, :, :].rearrange("p t h v -> p (t h v)"),
                               v1[:, u, :, :, :].rearrange("p t h v -> p (t h v)")).then_inc(S["vh"], 1)

            def out_copy(n):
                act.wait_ge(S["ot_p"], n + 1)
                nc.scalar.copy(ot[:, :], bank[3][:, 0:2 * P]).then_inc(S["ot"], 1)

            def prologue():
                rows_hi(0, 0)
                for j in range(NQK):
                    exponent(0, j)
                    phi_hi(0, 0, j)
                v_hi(0, 0)

            def batch(g, u, b, first, more, more2):
                n = 2 * g + b
                if b == 0 and more:
                    rows_hi(g + 1, 1 - u)
                prob_hi(n, 0)
                if b == 1 and more:
                    exponent(g + 1, 3)
                prob_hi(n, 1)
                if not first:
                    out_copy(n - 1)
                if more:
                    if b == 0:
                        exponent(g + 1, 0)
                    else:
                        phi_hi(g + 1, 1 - u, 3)
                prob_hi(n, 2)
                if more:
                    if b == 0:
                        phi_hi(g + 1, 1 - u, 0)
                        exponent(g + 1, 1)
                    else:
                        v_hi(g + 1, 1 - u)
                prob_hi(n, 3)
                if b == 0 and more:
                    phi_hi(g + 1, 1 - u, 1)
                    exponent(g + 1, 2)
                    phi_hi(g + 1, 1 - u, 2)

            steps(act, prologue, batch, lambda: out_copy(BATCH - 1))

        @block.vector
        def _(dve):
            def normalise(g, u):
                after(dve, S["xt_p"], g - 1)
                for j in range(TPG):
                    ins = nc.vector.tensor_scalar(xn[:, u, j, :], h[:, dyn(g * TPG + j, 1), :],
                                                  mean[:, dyn(g * TPG + j, 1)], rstd[:, dyn(g * TPG + j, 1)],
                                                  ALU.subtract, ALU.mult)
                ins.then_inc(S["xn"], 1)

            def rows_lo(g, u):
                dve.wait_ge(S["xh"], g + 1)
                nc.vector.tensor_tensor(xl[:, u, :], bank[0][:, :], xh[:, u, :], ALU.subtract).then_inc(S["xl"], 1)

            def elu(g, u, j):
                dve.wait_ge(S["qk_e"], NQK * g + j + 1)
                nc.vector.scalar_tensor_tensor(phi[:, u, j, :], ebuf[:, j % 2, :], 1.0, xbuf[:, j % 2, :],
                                               ALU.min, ALU.max).then_inc(S["elu"], 1)

            def phi_lo(g, u, j):
                dve.wait_ge(S["ph"], NQK * g + j + 1)
                nc.vector.scalar_tensor_tensor(pl[:, u, j, :], phi[:, u, j, :], PHI, ph[:, u, j, :],
                                               ALU.mult, ALU.subtract).then_inc(S["pl"], 1)

            def add_bias(g, u):
                dve.wait_ge(S["v_p"], g + 1)
                nc.vector.scalar_tensor_tensor(v1[:, u, :, :, 0:E].rearrange("p t h e -> p (t h) e"),
                                               bank[0][:, :].rearrange("p (x e) -> p x e", e=E), 1.0 / W_SCALE,
                                               bv4[:, :].rearrange("p (x e) -> p x e", e=E),
                                               ALU.mult, ALU.add).then_inc(S["v"], 1)

            def v_lo(g, u):
                dve.wait_ge(S["vh"], g + 1)
                nc.vector.tensor_tensor(vl[:, u, :, :, :].rearrange("p t h v -> p (t h v)"),
                                        v1[:, u, :, :, :].rearrange("p t h v -> p (t h v)"),
                                        vh[:, u, :, :, :].rearrange("p t h v -> p (t h v)"),
                                        ALU.subtract).then_inc(S["vl"], 1)

            def mask(n, r):
                dve.wait_ge(S["sc_p"], 4 * n + r + 1)
                nc.vector.tensor_tensor(prob[:, r, :, :], bank[4 + r][:, :].rearrange("p (x q) -> p x q", x=4),
                                        tri4[:, r, :, :], ALU.mult).then_inc(S["sc"], 1)

            def fade_keys(n):
                dve.wait_ge(S["kt_p"], n + 1)
                nc.vector.tensor_tensor(ktok[:, :].rearrange("p (h e) -> p h e", h=H),
                                        bank[2][:, 0:2 * P].rearrange("p (h e) -> p h e", h=H),
                                        col[:, 2, :].rearrange("p (h o) -> p h o", o=1).broadcast_to([P, H, 2 * E]),
                                        ALU.mult).then_inc(S["kt"], 1)

            def mask_state(n):
                dve.wait_ge(S["st_p"], n + 1)
                nc.vector.tensor_tensor(state[:, :, :], bank[2][:, 0:2 * R * V].rearrange("p (i c) -> p i c", i=2),
                                        bdiag[:, :, :, :].rearrange("p i r v -> p i (r v)"),
                                        ALU.mult).then_inc(S["st"], 1)

            def divide(n):
                dve.wait_ge(S["pv_p"], n + 1)
                pv = bank[3][:, 0:2 * H * V].rearrange("p (t h v) -> p t h v", t=2, h=H)
                nc.vector.tensor_scalar(den[:, :, :], pv[:, :, :, E], PROB * LN_EPS, None, ALU.add).then_inc(S["den"], 1)
                dve.wait_ge(S["den"], 2 * n + 1)
                nc.vector.reciprocal(den[:, :, :], den[:, :, :]).then_inc(S["den"], 1)
                dve.wait_ge(S["den"], 2 * n + 2)
                nc.vector.tensor_tensor(on[:, :, :].rearrange("p t (h e) -> p t h e", h=H), pv[:, :, :, 0:E],
                                        den[:, :, :].rearrange("p t (h o) -> p t h o", o=1)
                                        .broadcast_to([P, 2, H, E]), ALU.mult).then_inc(S["on"], 1)

            def out_rows(n):
                dve.wait_ge(S["o_p"], n + 1)
                nc.vector.tensor_tensor(o_all[:, dyn(2 * n, 2), :], bank[3][:, 0:2 * D].rearrange("p (t d) -> p t d", t=2),
                                        rows[:, 1:2, :].broadcast_to([P, 2, D]), ALU.add).then_inc(S["o"], 1)

            def out_stats(n):
                dve.wait_ge(S["o"], n + 1)
                for j in range(2):
                    nc.vector.bn_stats(stats[:, dyn(2 * n + j, 1), :], o_all[:, dyn(2 * n + j, 1), :])

            def prologue():
                for g in range(2):
                    normalise(g, g)
                rows_lo(0, 0)
                for j in range(NQK):
                    elu(0, 0, j)
                    phi_lo(0, 0, j)
                add_bias(0, 0)
                v_lo(0, 0)

            def batch(g, u, b, first, more, more2):
                n = 2 * g + b
                fade_keys(n)
                if b == 0 and more:
                    rows_lo(g + 1, 1 - u)
                mask(n, 0)
                if b == 1 and more:
                    elu(g + 1, 1 - u, 3)
                mask(n, 1)
                mask_state(n)
                if b == 0 and more:
                    elu(g + 1, 1 - u, 0)
                mask(n, 2)
                if b == 1 and more:
                    phi_lo(g + 1, 1 - u, 3)
                if not first:
                    out_rows(n - 1)
                if b == 1 and more:
                    add_bias(g + 1, 1 - u)
                mask(n, 3)
                if b == 0 and more:
                    elu(g + 1, 1 - u, 1)
                    phi_lo(g + 1, 1 - u, 0)
                    phi_lo(g + 1, 1 - u, 1)
                if not first:
                    out_stats(n - 1)
                if b == 1 and more:
                    v_lo(g + 1, 1 - u)
                if b == 1 and more2:
                    normalise(g + 2, u)
                divide(n)
                if b == 0 and more:
                    elu(g + 1, 1 - u, 2)
                    phi_lo(g + 1, 1 - u, 2)

            def epilogue():
                out_rows(BATCH - 1)
                out_stats(BATCH - 1)

            steps(dve, prologue, batch, epilogue)

        @block.gpsimd
        def _(pool):
            def fade_queries(g, u, j):
                pool.wait_ge(S["elu"], NQK * g + j + 1)
                nc.gpsimd.tensor_tensor(qd[:, u, j, :, :],
                                        phi[:, u, j, :].rearrange("p (b s t) -> p b s t", b=2, s=2)[:, :, 1, :],
                                        fade[:, j:j + 1, 1:P + 1].broadcast_to([P, 2, P]), ALU.mult).then_inc(S["qd"], 1)

            def prob_lo(n, r):
                pool.wait_ge(S["prh"], 4 * n + r + 1)
                nc.gpsimd.tensor_tensor(prl[:, r, :, :].rearrange("p x q -> p (x q)"),
                                        prob[:, r, :, :].rearrange("p x q -> p (x q)"),
                                        prh[:, r, :, :].rearrange("p x q -> p (x q)"),
                                        ALU.subtract).then_inc(S["prl"], 1)

            def prologue():
                for j in range(2):
                    fade_queries(0, 0, j)

            def batch(g, u, b, first, more, more2):
                for r in range(R):
                    prob_lo(2 * g + b, r)
                if b == 0 and more:
                    for j in range(2):
                        fade_queries(g + 1, 1 - u, j)

            steps(pool, prologue, batch, lambda: None)

    layer_stats(nc, c, stats, mean, rstd, eps_t, s_ln, 1)
    s_ln = sem("s_a_ln")
    s_add = sem("s_a_add")
    s_nst = sem("s_a_newstats")
    with nc.Block() as block:
        @block.vector
        def _(dve):
            with dve.Fori(0, TILES // 2) as i:
                for u in range(2):
                    tl = 2 * i + u
                    nc.vector.scalar_tensor_tensor(off[:, u, :], o_all[:, dyn(tl, 1), :], mean[:, dyn(tl, 1)],
                                                   rows[:, 2, :], ALU.subtract, ALU.mult).then_inc(s_ln, 1)
                for u in range(2):
                    tl = 2 * i + u
                    dve.wait_ge(s_ln, 2 * i + 2)
                    dve.wait_ge(s_add, tl + 1)
                    nc.vector.scalar_tensor_tensor(h[:, dyn(tl, 1), :], off[:, u, :], rstd[:, dyn(tl, 1)],
                                                   h[:, dyn(tl, 1), :], ALU.mult, ALU.add).then_inc(s_nst, 1)
                for u in range(2):
                    tl = 2 * i + u
                    dve.wait_ge(s_nst, tl + 1)
                    nc.vector.bn_stats(stats[:, dyn(tl, 1), :], h[:, dyn(tl, 1), :])

        @block.gpsimd
        def _(pool):
            with pool.Fori(0, TILES) as tl:
                nc.gpsimd.tensor_tensor(h[:, dyn(tl, 1), :], h[:, dyn(tl, 1), :], rows[:, 3:4, :],
                                        ALU.add).then_inc(s_add, 1)


def routing_phase(nc, c, t, h, mean, rstd, bank, ident, causal, pos, wrow, experts):
    def sb(name, shape, dt=F32):
        return c.enter_context(nc.sbuf_tensor(name, shape, dt))

    def sem(name):
        return c.enter_context(nc.semaphore(name))

    NL = GRP + EXPERTS
    SETS = 1 + GRP
    wr = sb("wr", [P, NL])
    br = sb("br", [P, NL])
    pr = sb("r_prob", [P, TILES, SETS, 4])
    rank = sb("r_rank", [P, TILES, SETS, 4])
    sel = sb("r_sel", [P, TILES, SETS, 4])
    one = sb("r_one", [P, TILES, SETS])
    top = sb("r_top", [P, 3, TILES, SETS])
    c_loop = ExitStack()
    xn = c_loop.enter_context(nc.sbuf_tensor("r_xn", [P, 2, TPG, D], F32))
    xt = c_loop.enter_context(nc.sbuf_tensor("r_xt", [P, 2, GT], F32))
    s_w = sem("s_r_w")
    s_xn, s_xtp, s_xt, s_lp, s_l = (sem("s_r_" + n) for n in ("xn", "xt_p", "xt", "logit_p", "logit"))

    with nc.Block() as block:
        @block.sync
        def _(sp):
            sp.dma_start(wr[:, :], t["wr"]).then_inc(s_w, 16)
            sp.dma_start(br[:, :], t["br"].partition_broadcast(P)).then_inc(s_w, 16)

        @block.vector
        def _(dve):
            dve.sem_inc(s_l, 2)
            dve.wait_ge(s_w, 32)
            with dve.Fori(0, GROUPS // 2) as i:
                for u in range(2):
                    g = 2 * i + u
                    dve.wait_ge(s_xtp, g + 1)
                    for j in range(TPG):
                        ins = nc.vector.tensor_scalar(xn[:, u, j, :], h[:, dyn(g * TPG + j, 1), :],
                                                      mean[:, dyn(g * TPG + j, 1)], rstd[:, dyn(g * TPG + j, 1)],
                                                      ALU.subtract, ALU.mult)
                    ins.then_inc(s_xn, 1)
                for u in range(2):
                    g = 2 * i + u
                    dve.wait_ge(s_lp, g + 1 + 2)
                    nc.vector.tensor_tensor(pr[:, dyn(g * TPG, TPG), :, :],
                                            bank[2 + u][:, 0:TPG * NL].rearrange("p (t s k) -> p t s k", t=TPG, k=4),
                                            br[:, :].rearrange("p (o s k) -> p o s k", o=1, k=4)
                                            .broadcast_to([P, TPG, SETS, 4]), ALU.add).then_inc(s_l, 1)

        @block.tensor
        def _(pe):
            pe.sem_inc(s_xtp, 2)
            pe.wait_ge(s_w, 32)
            with pe.Fori(0, GROUPS // 2) as i:
                for u in range(2):
                    g = 2 * i + u
                    pe.wait_ge(s_xn, g + 1)
                    pe.wait_ge(s_xt, g + 1)
                    for j in range(TPG):
                        mm = nc.tensor.transpose(bank[u][:, j * P:(j + 1) * P], xn[:, u, j, :], ident[:, :])
                    mm.then_inc(s_xtp, 1)
                for u in range(2):
                    g = 2 * i + u
                    pe.wait_ge(s_xt, g + 1 + 2)
                    pe.wait_ge(s_l, g + 1)
                    for j in range(TPG):
                        mm = nc.tensor.matmul(bank[2 + u][:, j * NL:(j + 1) * NL], xt[:, u, j * P:(j + 1) * P],
                                              wr[:, :], start=(j == 0), stop=True, skip_group_check=True)
                    mm.then_inc(s_lp, 1)

        @block.scalar
        def _(act):
            act.sem_inc(s_xt, 2)
            act.sem_inc(s_lp, 2)
            with act.Fori(0, GROUPS // 2) as i:
                for u in range(2):
                    g = 2 * i + u
                    act.wait_ge(s_xtp, g + 1 + 2)
                    act.wait_ge(s_lp, g + 1)
                    nc.scalar.copy(xt[:, u, :], bank[u][:, :]).then_inc(s_xt, 1)

    c_loop.close()
    tw = sb("r_tw", [P, TILES, EXPERTS])
    mem = sb("r_mem", [P, TILES, SETS, 4])
    gsel = sb("r_gsel", [P, 2, TILES, GRP])
    pair = sb("r_pair", [P, TILES, GRP, PAIRS])
    bk = sb("r_bk", [P, 3, TILES, BUCKETS])
    off = sb("r_off", [P, 2, TILES, BUCKETS])
    base = sb("r_base", [P, 4, BUCKETS])
    strict = sb("r_strict", [P, P])
    ones = sb("r_ones", [P, P])
    wab = sb("r_wab", [P, 3, TILES, GRP])
    posf = sb("r_posf", [P, 2, TILES])
    ends = sb("r_ends", [BUCKETS, 1])
    iota_s = sb("r_iota_s", [BUCKETS, SLOTS])
    delta = sb("r_delta", [BUCKETS, 2])
    s_cnt, s_io, s_te, s_tb, s_de = (sem("s_r_" + n) for n in ("count", "iota", "ends_p", "table_p", "delta"))
    s_v = sem("s_r_chain")
    s_e = sem("s_r_exp")
    with nc.Block() as block:
        @block.scalar
        def _(act):
            act.wait_ge(s_v, 2)
            nc.scalar.activation(pr[:, :, :, :], pr[:, :, :, :], ACT.Exp).then_inc(s_e, 1)

        @block.sync
        def _(sp):
            sp.dma_start(delta[:, :], t["delta"]).then_inc(s_de, 16)

        @block.gpsimd
        def _(pool):
            nc.gpsimd.iota(iota_s[:, :], pattern=[[1, SLOTS]], base=0, channel_multiplier=0,
                           allow_small_or_imprecise_dtypes=True).then_inc(s_io, 1)
            nc.gpsimd.memset(ones[:, :], 1.0).then_inc(s_io, 1)
            nc.gpsimd.tensor_tensor(strict[:, :], causal[:, :], ident[:, :], ALU.subtract).then_inc(s_io, 1)

        @block.tensor
        def _(pe):
            flat = bk[:, 2, :, :].rearrange("p t b -> p (t b)")
            pe.wait_ge(s_io, 3)
            pe.wait_ge(s_cnt, 1)
            for k in range(3):
                nc.tensor.matmul(bank[k][:, :], strict[:, :], flat[:, 512 * k:512 * k + 512], start=True, stop=True)
                mm = nc.tensor.matmul(bank[3 + k][:, :], ones[:, :], flat[:, 512 * k:512 * k + 512], start=True,
                                      stop=True)
            mm.then_inc(s_cnt, 1)
            pe.wait_ge(s_cnt, 3)
            nc.tensor.transpose(bank[6][0:BUCKETS, 0:P], base[:, 1, :], ident[:, :]).then_inc(s_te, 1)
            pe.wait_ge(s_cnt, 4)
            pe.wait_ge(s_de, 16)
            for k in range(2):
                mm = nc.tensor.matmul(bank[7][0:1, k * SLOTS:(k + 1) * SLOTS], delta[:, k:k + 1], iota_s[:, :],
                                      start=True, stop=True)
            mm.then_inc(s_tb, 1)

        @block.vector
        def _(dve):
            count = [0]

            def step(ins):
                count[0] += 1
                ins.then_inc(s_v, 1)
                dve.wait_ge(s_v, count[0])

            def over4(a):
                return a.rearrange("p t (s o) -> p t s o", o=1).broadcast_to([P, TILES, SETS, 4])

            p4, r4, s4 = pr[:, :, :, :], rank[:, :, :, :], sel[:, :, :, :]
            m1, m2, keep = (top[:, k, :, :] for k in range(3))
            step(nc.vector.tensor_reduce(m1, p4, AX.X, ALU.max))
            step(nc.vector.tensor_tensor(p4, p4, over4(m1), ALU.subtract))
            dve.wait_ge(s_e, 1)
            step(nc.vector.tensor_reduce(m1, p4, AX.X, ALU.add))
            step(nc.vector.reciprocal(m1, m1))
            step(nc.vector.tensor_tensor(p4, p4, over4(m1), ALU.mult))
            for k in range(4):
                step(nc.vector.memset(rank[:, :, :, k], float(3 - k)))
            for a in range(4):
                for b in range(a + 1, 4):
                    step(nc.vector.tensor_tensor(one[:, :, :], pr[:, :, :, a], pr[:, :, :, b], ALU.is_ge))
                    step(nc.vector.tensor_tensor(rank[:, :, :, b], rank[:, :, :, b], one[:, :, :], ALU.add))
                    step(nc.vector.tensor_tensor(rank[:, :, :, a], rank[:, :, :, a], one[:, :, :], ALU.subtract))
            step(nc.vector.tensor_scalar(mem[:, :, :, :], r4, 1.0, None, ALU.is_le))
            for k in range(2):
                step(nc.vector.tensor_scalar(gsel[:, k, :, :], rank[:, :, 0, :], float(k), None, ALU.is_equal))
            step(nc.vector.scalar_tensor_tensor(s4.rearrange("p t s k -> p (t s k)"), r4.rearrange("p t s k -> p (t s k)"),
                                                0.0, p4.rearrange("p t s k -> p (t s k)"), ALU.is_equal, ALU.mult))
            step(nc.vector.tensor_reduce(m1, s4, AX.X, ALU.add))
            step(nc.vector.scalar_tensor_tensor(r4.rearrange("p t s k -> p (t s k)"), r4.rearrange("p t s k -> p (t s k)"),
                                                1.0, p4.rearrange("p t s k -> p (t s k)"), ALU.is_equal, ALU.mult))
            step(nc.vector.tensor_reduce(m2, r4, AX.X, ALU.add))
            step(nc.vector.tensor_tensor(keep, m1, m2, ALU.add))
            step(nc.vector.tensor_scalar(keep, keep, TOP_P, None, ALU.is_le))
            step(nc.vector.tensor_tensor(m2, m2, keep, ALU.mult))
            step(nc.vector.tensor_tensor(r4, r4, over4(keep), ALU.mult))
            step(nc.vector.tensor_tensor(r4, r4, s4, ALU.add))
            step(nc.vector.tensor_tensor(m1, m1, m2, ALU.add))
            step(nc.vector.tensor_scalar(m1, m1, 1e-9, None, ALU.add))
            step(nc.vector.reciprocal(m1, m1))
            step(nc.vector.tensor_tensor(r4, r4, over4(m1), ALU.mult))
            step(nc.vector.tensor_tensor(tw[:, :, :].rearrange("p t (g k) -> p t g k", k=4), rank[:, :, 1:SETS, :],
                                         rank[:, :, 0, :].rearrange("p t (g o) -> p t g o", o=1)
                                         .broadcast_to([P, TILES, GRP, 4]), ALU.mult))
            step(nc.vector.tensor_scalar(tw[:, :, :], tw[:, :, :], GRP ** -0.5, None, ALU.mult))
            n = 0
            for a in range(4):
                for b in range(a + 1, 4):
                    step(nc.vector.tensor_tensor(pair[:, :, :, n], mem[:, :, 1:SETS, a], mem[:, :, 1:SETS, b], ALU.mult))
                    n += 1
            for k in range(2):
                step(nc.vector.tensor_tensor(bk[:, k, :, :].rearrange("p t (g m) -> p t g m", g=GRP), pair[:, :, :, :],
                                             gsel[:, k, :, :].rearrange("p t (g o) -> p t g o", o=1)
                                             .broadcast_to([P, TILES, GRP, PAIRS]), ALU.mult))
            step(nc.vector.tensor_tensor(bk[:, 2, :, :], bk[:, 0, :, :], bk[:, 1, :, :], ALU.add))
            dve.sem_inc(s_cnt, 1)
            w4 = tw[:, :, :].rearrange("p t (g k) -> p t g k", k=4)
            out4, wsum = mem, wab[:, 2, :, :]
            step(nc.vector.tensor_scalar(out4[:, :, :, :], mem[:, :, :, :], -1.0, 1.0, ALU.mult, ALU.add))
            for k, (x, y, z) in enumerate(((0, 1, 2), (3, 2, 1))):
                wk = wab[:, k, :, :]
                step(nc.vector.tensor_tensor(wsum, w4[:, :, :, z], out4[:, :, 1:SETS, y], ALU.mult))
                step(nc.vector.tensor_tensor(wsum, wsum, w4[:, :, :, y], ALU.add))
                step(nc.vector.tensor_tensor(wsum, wsum, out4[:, :, 1:SETS, x], ALU.mult))
                step(nc.vector.tensor_tensor(wk, wsum, w4[:, :, :, x], ALU.add))
            for ch in range(2):
                for k in range(2):
                    step(nc.vector.scalar_tensor_tensor(wsum.rearrange("p t g -> p (t g)"),
                                                        wab[:, k, :, :].rearrange("p t g -> p (t g)"), W_HID,
                                                        gsel[:, ch, :, :].rearrange("p t g -> p (t g)"),
                                                        ALU.mult, ALU.mult))
                    step(nc.vector.tensor_reduce(wrow[:, :, ch, k], wsum, AX.X, ALU.add))
            dve.wait_ge(s_cnt, 2)
            for k in range(3):
                step(nc.vector.tensor_copy(off[:, 0, :, :].rearrange("p t b -> p (t b)")[:, 512 * k:512 * k + 512],
                                           bank[3 + k][:, :]))
            a, b, n = 0, 1, 1
            while n < TILES:
                step(nc.vector.tensor_copy(off[:, b, 0:n, :], off[:, a, 0:n, :]))
                step(nc.vector.tensor_tensor(off[:, b, n:TILES, :], off[:, a, n:TILES, :], off[:, a, 0:TILES - n, :],
                                             ALU.add))
                a, b, n = b, a, 2 * n
            total = off[:, a, TILES - 1, :]
            step(nc.vector.tensor_scalar(base[:, 0, :], total, 1.0 / P, 0.5 - 0.5 / P, ALU.mult, ALU.add))
            step(nc.vector.tensor_scalar(base[:, 0, :], base[:, 0, :], ROUND, ROUND, ALU.add, ALU.subtract))
            step(nc.vector.tensor_copy(base[:, 1, :], base[:, 0, :]))
            for m in range(1, BUCKETS):
                step(nc.vector.tensor_tensor(base[:, 1, m:m + 1], base[:, 1, m - 1:m], base[:, 0, m:m + 1], ALU.add))
            dve.sem_inc(s_cnt, 1)
            step(nc.vector.tensor_tensor(base[:, 2, :], base[:, 1, :], base[:, 0, :], ALU.subtract))
            step(nc.vector.tensor_scalar(base[:, 2, :], base[:, 2, :], float(P), None, ALU.mult))
            step(nc.vector.memset(off[:, b, 0, :], 0.0))
            step(nc.vector.tensor_copy(off[:, b, 1:TILES, :], off[:, a, 0:TILES - 1, :]))
            fl = off[:, b, :, :].rearrange("p t b -> p (t b)")
            for k in range(3):
                step(nc.vector.tensor_tensor(fl[:, 512 * k:512 * k + 512], bank[k][:, :], fl[:, 512 * k:512 * k + 512],
                                             ALU.add))
            step(nc.vector.tensor_tensor(off[:, b, :, :], off[:, b, :, :],
                                         base[:, 2:3, :].broadcast_to([P, TILES, BUCKETS]), ALU.add))
            for ch in range(2):
                step(nc.vector.tensor_tensor(off[:, a, :, :], off[:, b, :, :], bk[:, ch, :, :], ALU.mult))
                step(nc.vector.tensor_reduce(posf[:, ch, :], off[:, a, :, :], AX.X, ALU.add))
                step(nc.vector.tensor_copy(pos[:, :, ch], posf[:, ch, :]))
            dve.wait_ge(s_te, 1)
            step(nc.vector.tensor_copy(ends[:, :], bank[6][0:BUCKETS, 0:1]))
            dve.wait_ge(s_io, 3)
            step(nc.vector.tensor_scalar(iota_s[:, :], iota_s[:, :], ends[:, 0:1], None, ALU.is_ge))
            dve.sem_inc(s_cnt, 1)
            dve.wait_ge(s_tb, 1)
            for k in range(2):
                step(nc.vector.tensor_scalar(experts[:, :, k], bank[7][0:1, k * SLOTS:(k + 1) * SLOTS], float(k), None,
                                             ALU.add))


def sorted_ffn_phase(nc, c, t, h, mean, rstd, bank, ident, pos, wrow, experts, x_sorted, y_sorted, stats):
    def sb(name, shape, dt=F32):
        return c.enter_context(nc.sbuf_tensor(name, shape, dt))

    def sem(name):
        return c.enter_context(nc.semaphore(name))

    CH = HID // P
    MATS = 3
    w1s, w3s = (sb(n, [P, EXPERTS, 2, HID], F16) for n in ("w1s", "w3s"))
    w2s = sb("w2s", [P, EXPERTS, CH, 2, D], F16)
    row = sb("g_row", [P, TPG, 2, ROW])
    idx = sb("g_idx", [P, TPG, 2], I32)
    c_load = ExitStack()
    stage = c_load.enter_context(nc.sbuf_tensor("w_stage", [P, 2, MATS, HID], F32))

    s_ld = [sem(f"s_g_wload{u}") for u in range(2)]
    s_whi, s_wlo = sem("s_g_w_hi"), sem("s_g_w_lo")
    s_row, s_copy, s_idx = sem("s_g_row"), sem("s_g_copy"), sem("s_g_idx")
    s_sc = [sem(f"s_g_rows{j}") for j in range(TPG)]
    s_pd, s_issue = sem("s_g_pad"), sem("s_g_issue")
    def hi_lo(e, u, k):
        m = stage[:, u, k, :]
        if k < 2:
            w = (w1s, w3s)[k]
            return w[:, dyn(e, 1), 0, :], w[:, dyn(e, 1), 1, :], m
        w = w2s[:, dyn(e, 1), :, :, :].rearrange("p e c t d -> p (e c) t d")
        return w[:, :, 0, :], w[:, :, 1, :], m.rearrange("p (c d) -> p c d", c=CH)

    with nc.Block() as block:
        @block.sync
        def _(sp):
            with sp.Fori(0, EXPERTS // 2) as i:
                for u in range(2):
                    e = 2 * i + u
                    sp.wait_ge(s_wlo, e + 1)
                    for k, n in enumerate(("w1", "w3", "w2")):
                        src = t[n][dyn(e, 1), :, :].rearrange("e (c p) d -> p (e c) d", p=P)
                        sp.dma_start(stage[:, u, k, :].rearrange("p (c d) -> p c d", c=src.shape[1]), src)\
                            .then_inc(s_ld[u], 16)

        @block.vector
        def _(dve):
            dve.sem_inc(s_wlo, 2)
            dve.wait_ge(s_pd, 1)

            def rows(g, first=False):
                for j in range(TPG):
                    tl = g * TPG + j
                    if not first:
                        dve.wait_ge(s_sc[j], 32 * g)
                    nc.vector.tensor_scalar(row[:, j, 0, 0:D], h[:, dyn(tl, 1), :], mean[:, dyn(tl, 1)],
                                            rstd[:, dyn(tl, 1)], ALU.subtract, ALU.mult).then_inc(s_row, 1)
                    nc.vector.tensor_copy(row[:, j, :, D:D + 2], wrow[:, dyn(tl, 1), :, :]
                                          .rearrange("p t a b -> p (t a) b")).then_inc(s_idx, 1)
                    nc.vector.tensor_copy(idx[:, j, :], pos[:, dyn(tl, 1), :]
                                          .rearrange("p t a -> p (t a)")).then_inc(s_idx, 1)

            def weights_lo(e, u):
                for k in range(MATS):
                    hi, lo, m = hi_lo(e, u, k)
                    dve.wait_ge(s_whi, MATS * e + k + 1)
                    ins = nc.vector.scalar_tensor_tensor(lo, m, W_SCALE, hi, ALU.mult, ALU.subtract)
                ins.then_inc(s_wlo, 1)

            for g in range(2):
                rows(g, first=g == 0)
                weights_lo(g, g)
            with dve.Fori(1, GROUPS // 2) as i:
                for u in range(2):
                    rows(2 * i + u)
                    weights_lo(2 * i + u, u)

        @block.scalar
        def _(act):
            with act.Fori(0, GROUPS // 2) as i:
                for u in range(2):
                    g = 2 * i + u
                    for j in range(TPG):
                        act.wait_ge(s_row, g * TPG + j + 1)
                        nc.scalar.copy(row[:, j, 1, 0:D], row[:, j, 0, 0:D]).then_inc(s_copy, 1)
                    act.wait_ge(s_ld[u], 16 * MATS * (i + 1))
                    for k in range(MATS):
                        hi, _, m = hi_lo(g, u, k)
                        nc.scalar.activation(hi, m, ACT.Copy, scale=W_SCALE).then_inc(s_whi, 1)

        @block.gpsimd
        def _(pool):
            nc.gpsimd.memset(row[:, :, :, D:ROW], 0.0).then_inc(s_pd, 1)
            with pool.Fori(0, GROUPS) as g:
                for j in range(TPG):
                    pool.wait_ge(s_copy, g * TPG + j + 1)
                    pool.wait_ge(s_idx, 2 * (g * TPG + j + 1))
                    pool.sem_inc(s_issue, 1)
                    for k in range(2):
                        nc.gpsimd.indirect_dma_start(
                            out=x_sorted, out_offset=bass.IndirectOffsetOnAxis(ap=idx[:, j, k:k + 1].bitcast(U32), axis=0),
                            in_=row[:, j, k, :], in_offset=None).then_inc(s_sc[j], 16)
            for j in range(TPG):
                pool.wait_ge(s_sc[j], 32 * GROUPS)

    c_load.close()
    SPT = 4
    NU = 2 * SPT
    TURNS = SLOTS // SPT
    xs = sb("g_xs", [P, SPT, ROW])
    xh = sb("g_xh", [P, 2, P], F16)
    xl = sb("g_xl", [P, 2, P], F16)
    gate = sb("g_gate", [P, 2, HID])
    hid = sb("g_hid", [P, 2, HID])
    hh = sb("g_hh", [P, 2, CH, P], F16)
    hl = sb("g_hl", [P, 2, CH, P], F16)
    yb = sb("g_yb", [P, 2, D])
    ys = sb("g_ys", [P, SPT, D])
    S = {n: sem("s_g_" + n) for n in ("xt_p", "xh", "xl", "up", "gate", "hid", "ht_p", "hh", "hl", "y_p", "yb", "ys")}
    s_xs = [sem(f"s_g_xs{u}") for u in range(SPT)]
    s_yo = [sem(f"s_g_yout{u}") for u in range(SPT)]
    x_t = x_sorted.rearrange("(s p) d -> s p d", p=P)
    y_t = y_sorted.rearrange("(s p) d -> s p d", p=P)

    with nc.Block() as block:
        @block.sync
        def _(sp):
            def load(i, u, first=False):
                if not first:
                    sp.wait_ge(S["hid"], NU * (i - 1) + 2 * u + 2)
                sp.dma_start(xs[:, u, :], x_t[dyn(SPT * i + u, 1), :, :].rearrange("s p d -> p (s d)"))\
                    .then_inc(s_xs[u], 16)

            def store(i, u):
                sp.wait_ge(S["ys"], SPT * i + u + 1)
                sp.dma_start(y_t[dyn(SPT * i + u, 1), :, :].rearrange("s p d -> p (s d)"), ys[:, u, :])\
                    .then_inc(s_yo[u], 16)

            for u in range(SPT):
                load(0, u, first=True)
            with sp.Fori(1, TURNS) as i:
                for u in range(SPT):
                    load(i, u)
                    store(i - 1, u)
            for u in range(SPT):
                store(TURNS - 1, u)
            for u in range(SPT):
                sp.wait_ge(s_yo[u], 16 * TURNS)

        @block.tensor
        def _(pe):
            def transpose_rows(i, u):
                pe.wait_ge(s_xs[u], 16 * i + 16)
                nc.tensor.transpose(bank[0][:, 0:P], xs[:, u, 0:D], ident[:, :]).then_inc(S["xt_p"], 1)

            def expert(i, u, k):
                return pe.value_load(experts[0:1, dyn(SPT * i + u, 1), k], min_val=0, max_val=EXPERTS - 1)

            def up(i, u, k, e):
                if k == 0:
                    pe.wait_ge(S["xl"], SPT * i + u + 1)
                for w, b in ((w1s, 1 + k), (w3s, 3 + k)):
                    hi, lo = w[:, dyn(e, 1), 0, :], w[:, dyn(e, 1), 1, :]
                    nc.tensor.matmul(bank[b][:, :], xh[:, u % 2, :], hi, start=True, stop=False)
                    nc.tensor.matmul(bank[b][:, :], xl[:, u % 2, :], hi, start=False, stop=False)
                    mm = nc.tensor.matmul(bank[b][:, :], xh[:, u % 2, :], lo, start=False, stop=True)
                mm.then_inc(S["up"], 1)

            def transpose_hidden(i, u, k):
                v = 2 * (SPT * i + u) + k
                pe.wait_ge(S["hid"], v + 1)
                for m in range(CH):
                    mm = nc.tensor.transpose(bank[5 + k][:, m * P:(m + 1) * P], hid[:, k, m * P:(m + 1) * P],
                                             ident[:, :])
                mm.then_inc(S["ht_p"], 1)

            def down(i, u, k, e, first=False):
                s = SPT * i + u
                pe.wait_ge(S["hl"], 2 * s + k + 1)
                if k == 0 and not (first and u == 0):
                    pe.wait_ge(S["ys"], s)
                y = bank[7][:, 0:2 * D]
                for m in range(CH):
                    both = w2s[:, dyn(e, 1), m, :, :].rearrange("p e t d -> p (e t d)")
                    hi = w2s[:, dyn(e, 1), m, 0, :]
                    start, stop = k == 0 and m == 0, k == 1 and m == CH - 1
                    nc.tensor.matmul(y, hh[:, k, m, :], both, start=start, stop=False)
                    mm = nc.tensor.matmul(y[:, 0:D], hl[:, k, m, :], hi, start=False, stop=stop)
                mm.then_inc(S["y_p"], 1)

            def turn(i, first=False, last=False):
                if first:
                    transpose_rows(0, 0)
                es = {}
                for v in range(NU):
                    es[v] = expert(i, v // 2, v % 2)
                    up(i, v // 2, v % 2, es[v])
                    if v % 2 == 0 and v + 2 < NU:
                        transpose_rows(i, v // 2 + 1)
                    if v + 2 == NU and not last:
                        transpose_rows(i + 1, 0)
                    if not (first and v == 0):
                        w = (v - 1) % NU
                        transpose_hidden(i if v >= 1 else i - 1, w // 2, w % 2)
                    if v >= 2:
                        down(i, v // 2 - 1, v % 2, es[v - 2], first)
                    elif not first:
                        down(i - 1, SPT - 1, v, expert(i - 1, SPT - 1, v))

            turn(0, first=True)
            with pe.Fori(1, TURNS - 1) as i:
                turn(i)
            turn(TURNS - 1, last=True)
            transpose_hidden(TURNS - 1, SPT - 1, 1)
            for k in range(2):
                down(TURNS - 1, SPT - 1, k, expert(TURNS - 1, SPT - 1, k))

        @block.scalar
        def _(act):
            def split_rows(s, u):
                act.wait_ge(S["xt_p"], s + 1)
                nc.scalar.copy(xh[:, u % 2, :], bank[0][:, 0:P]).then_inc(S["xh"], 1)

            def silu(s, k):
                act.wait_ge(S["up"], 2 * s + k + 1)
                nc.scalar.activation(gate[:, k, :], bank[1 + k][:, :], ACT.Silu, scale=1.0 / W_SCALE)\
                    .then_inc(S["gate"], 1)

            def split_hidden(s, k):
                act.wait_ge(S["ht_p"], 2 * s + k + 1)
                nc.scalar.copy(hh[:, k, :, :].rearrange("p c n -> p (c n)"), bank[5 + k][:, :]).then_inc(S["hh"], 1)

            def rows_lo(s, u):
                act.wait_ge(S["y_p"], 2 * s + 2)
                nc.scalar.activation(yb[:, u % 2, :], bank[7][:, D:2 * D], ACT.Copy,
                                     scale=1.0 / (W_SCALE * W_SCALE * W_HID)).then_inc(S["yb"], 1)

            def turn(i, first=False, last=False):
                if first:
                    split_rows(0, 0)
                for v in range(NU):
                    u, k = v // 2, v % 2
                    silu(SPT * i + u, k)
                    if v % 2 == 0 and not (last and v + 2 == NU):
                        split_rows(SPT * i + u + 1, u + 1)
                    if not (first and v == 0):
                        w = (v - 1) % NU
                        split_hidden(SPT * (i if v >= 1 else i - 1) + w // 2, w % 2)
                    if v % 2 == 1 and not (first and v == 1):
                        w = (v // 2 - 1) % SPT
                        rows_lo(SPT * (i if v > 1 else i - 1) + w, w)

            turn(0, first=True)
            with act.Fori(1, TURNS - 1) as i:
                turn(i)
            turn(TURNS - 1, last=True)
            split_hidden(SLOTS - 1, 1)
            rows_lo(SLOTS - 1, SPT - 1)

        @block.vector
        def _(dve):
            def rest_rows(s, u):
                dve.wait_ge(S["xh"], s + 1)
                nc.vector.tensor_tensor(xl[:, u % 2, :], bank[0][:, 0:P], xh[:, u % 2, :], ALU.subtract).then_inc(S["xl"], 1)

            def hidden(s, u, k):
                dve.wait_ge(S["gate"], 2 * s + k + 1)
                nc.vector.scalar_tensor_tensor(hid[:, k, :], bank[3 + k][:, :], xs[:, u, D + k:D + k + 1], gate[:, k, :],
                                               ALU.mult, ALU.mult).then_inc(S["hid"], 1)

            def rest_hidden(s, k):
                dve.wait_ge(S["hh"], 2 * s + k + 1)
                nc.vector.tensor_tensor(hl[:, k, :, :].rearrange("p c n -> p (c n)"), bank[5 + k][:, :],
                                        hh[:, k, :, :].rearrange("p c n -> p (c n)"), ALU.subtract).then_inc(S["hl"], 1)

            def rows_out(i, u, first=False):
                dve.wait_ge(S["yb"], SPT * i + u + 1)
                if not first:
                    dve.wait_ge(s_yo[u], 16 * i)
                nc.vector.scalar_tensor_tensor(ys[:, u, :], bank[7][:, 0:D],
                                               1.0 / (W_SCALE * W_SCALE * W_HID), yb[:, u % 2, :],
                                               ALU.mult, ALU.add).then_inc(S["ys"], 1)

            def turn(i, first=False, last=False, second=False):
                if first:
                    rest_rows(0, 0)
                for v in range(NU):
                    u, k = v // 2, v % 2
                    if v % 2 == 0 and v >= 4:
                        rows_out(i, v // 2 - 2, first)
                    elif v % 2 == 0 and not first:
                        rows_out(i - 1, v // 2 - 2 + SPT, second)
                    hidden(SPT * i + u, u, k)
                    if v % 2 == 0 and not (last and v + 2 == NU):
                        rest_rows(SPT * i + u + 1, u + 1)
                    if not (first and v == 0):
                        w = (v - 1) % NU
                        rest_hidden(SPT * (i if v >= 1 else i - 1) + w // 2, w % 2)

            turn(0, first=True)
            turn(1, second=True)
            with dve.Fori(2, TURNS - 1) as i:
                turn(i)
            turn(TURNS - 1, last=True)
            rows_out(TURNS - 1, SPT - 2)
            rest_hidden(SLOTS - 1, 1)
            rows_out(TURNS - 1, SPT - 1)

    yg = sb("g_yg", [P, TPG, 2, D])
    s_gi, s_ga, s_gb = sem("s_g_gidx"), sem("s_g_add0"), sem("s_g_add1")
    with nc.Block() as block:
        @block.gpsimd
        def _(pool):
            with pool.Fori(0, GROUPS) as g:
                for j in range(TPG):
                    pool.wait_ge(s_gi, g * TPG + j + 1)
                    pool.sem_inc(s_issue, 1)
                    for k in range(2):
                        nc.gpsimd.indirect_dma_start(
                            out=yg[:, j, k, :], out_offset=None, in_=y_sorted,
                            in_offset=bass.IndirectOffsetOnAxis(ap=idx[:, j, k:k + 1].bitcast(U32), axis=0))\
                            .then_inc(s_sc[j], 16)

        @block.vector
        def _(dve):
            for j in range(TPG):
                nc.vector.tensor_copy(idx[:, j, :], pos[:, j, :]).then_inc(s_gi, 1)

            def add(g, j, more):
                tl = g * TPG + j
                dve.wait_ge(s_sc[j], 32 * GROUPS + 32 * g + 32)
                nc.vector.tensor_tensor(yg[:, j, 0, :], yg[:, j, 0, :], yg[:, j, 1, :], ALU.add).then_inc(s_ga, 1)
                dve.wait_ge(s_ga, tl + 1)
                nc.vector.tensor_tensor(h[:, dyn(tl, 1), :], h[:, dyn(tl, 1), :],
                                        yg[:, j, 0:1, :], ALU.add).then_inc(s_gb, 1)
                dve.wait_ge(s_gb, tl + 1)
                nc.vector.bn_stats(stats[:, dyn(tl, 1), :], h[:, dyn(tl, 1), :])
                if more:
                    nc.vector.tensor_copy(idx[:, j, :], pos[:, dyn(tl + TPG, 1), :]
                                          .rearrange("p t a -> p (t a)")).then_inc(s_gi, 1)

            with dve.Fori(0, GROUPS - 1) as g:
                for j in range(TPG):
                    add(g, j, True)
            for j in range(TPG):
                add(GROUPS - 1, j, False)


def slice_attention_phase(nc, c, t, h, stats, mean, rstd, bank, ident):
    def sb(name, shape, dt=F32):
        return c.enter_context(nc.sbuf_tensor(name, shape, dt))

    def sem(name):
        return c.enter_context(nc.semaphore(name))

    H, DH, M = HEADS1, DH1, SLICES
    HM = H * M
    NB = 8
    OCT = BATCH // NB
    wx = sb("c_wx", [DH, H, D])
    wsl = sb("c_wsl", [DH, M])
    bx = sb("c_bx", [DH, H])
    bxr = sb("c_bxr", [DH, H, P])
    bsl = sb("c_bsl", [P, M])
    temp = sb("c_temp", [P, 2, H])
    wqkv = sb("c_wqkv", [DH, 3, DH])
    wot = sb("c_wot", [DH, H, D])
    wfx = sb("c_wfx", [P, H, DH])
    bfx = sb("c_bfx", [1, H, DH])
    bo = sb("c_bo", [P, 1, D])
    wl = sb("c_wl", [P, HM])
    bl = sb("c_bl", [P, 1, HM])
    gqk = sb("c_gqk", [DH, 2 * DH])
    wvo = sb("c_wvo", [DH, H, D])
    off_block = sb("c_off", [P, P])

    xn1 = sb("c_xn1", [P, 2, 2, D + 1])
    xt = sb("c_xt", [P, 2, SEQ])
    lg = sb("c_lg", [P, 2, 2 * H, M])
    mx = sb("c_mx", [P, 2 * H])
    sm = sb("c_sm", [P, 2 * H])
    w = sb("c_w", [P, 2, 2, HM])
    dn = sb("c_dn", [P, 2])
    xs = sb("c_xs", [P, 2, 2, D + 1])
    wt = sb("c_wt", [P, NB, 2, SEQ])
    xst = sb("c_xst", [P, NB, H, M])
    rt = sb("c_rt", [1, NB, H, M])
    tt = sb("c_tt", [DH, NB, H, M])
    ut = sb("c_ut", [DH, NB, H, M])
    at = sb("c_at", [P, 2, 4, P])
    amx = sb("c_amx", [P, 4])
    asm = sb("c_asm", [P, 4])
    att = sb("c_att", [P, 2, 4, P])
    vo = sb("c_vo", [P, 2, 4, P])
    os_ = sb("c_os", [P, 2, 4, D])

    s_w, s_m, s_k, s_f = (sem("s_c_" + n) for n in ("weights", "mask", "setup", "fold"))
    with nc.Block() as block:
        @block.sync
        def _(sp):
            for dst, name in ((wx[:, :, :], "wx"), (wsl[:, :], "wsl"), (bx[:, :], "bx"), (wqkv[:, :, :], "wqkv1"),
                              (wot[:, :, :], "wot"), (wfx[:, :, :], "wfx"), (bfx[:, :, :], "bfx")):
                sp.dma_start(dst, t[name]).then_inc(s_w, 16)
            sp.dma_start(bsl[:, :], t["bsl"].partition_broadcast(P)).then_inc(s_w, 16)
            sp.dma_start(temp[:, 0, :], t["temp"].partition_broadcast(P)).then_inc(s_w, 16)
            sp.dma_start(bo[:, 0, :], t["bo1"].partition_broadcast(P)).then_inc(s_w, 16)

        @block.gpsimd
        def _(pool):
            nc.gpsimd.memset(off_block[:, :], -1e30).then_inc(s_m, 1)
            nc.gpsimd.memset(xn1[:, :, :, :], 1.0).then_inc(s_m, 1)
            nc.gpsimd.memset(gqk[:, DH:2 * DH], 0.0).then_inc(s_m, 1)
            pool.wait_ge(s_m, 3)
            for r in range(4):
                nc.gpsimd.memset(off_block[32 * r:32 * r + 32, 32 * r:32 * r + 32], 0.0).then_inc(s_m, 1)

        @block.vector
        def _(dve):
            dve.wait_ge(s_w, 160)
            nc.vector.tensor_copy(bxr[:, :, :], bx[:, :].rearrange("p (h o) -> p h o", o=1)
                                  .broadcast_to([DH, H, P])).then_inc(s_k, 1)
            nc.vector.reciprocal(temp[:, 1, :], temp[:, 0, :]).then_inc(s_k, 1)
            dve.wait_ge(s_k, 2)
            inv = temp[:, 1, :].rearrange("p (h o) -> p h o", o=1).broadcast_to([P, H, M])
            dve.wait_ge(s_f, 1)
            nc.vector.tensor_tensor(wl[:, :].rearrange("p (h m) -> p h m", h=H),
                                    bank[0][:, 0:HM].rearrange("p (h m) -> p h m", h=H), inv, ALU.mult).then_inc(s_k, 1)
            nc.vector.tensor_tensor(bl[:, 0, :].rearrange("p (h m) -> p h m", h=H),
                                    bank[1][:, 0:HM].rearrange("p (h m) -> p h m", h=H),
                                    bsl[:, :].rearrange("p (o m) -> p o m", o=1).broadcast_to([P, H, M]),
                                    ALU.add).then_inc(s_k, 1)
            dve.wait_ge(s_k, 4)
            nc.vector.tensor_tensor(bl[:, 0, :].rearrange("p (h m) -> p h m", h=H),
                                    bl[:, 0, :].rearrange("p (h m) -> p h m", h=H), inv, ALU.mult).then_inc(s_k, 1)
            nc.vector.tensor_copy(gqk[:, 0:DH], bank[2][0:DH, 0:DH]).then_inc(s_k, 1)
            for k in range(2):
                nc.vector.tensor_copy(wvo[:, 4 * k:4 * k + 4, :],
                                      bank[3 + k][0:DH, :].rearrange("p (h d) -> p h d", h=4)).then_inc(s_k, 1)

        @block.tensor
        def _(pe):
            pe.wait_ge(s_w, 160)
            pe.wait_ge(s_k, 1)
            for hd in range(H):
                nc.tensor.matmul(bank[0][:, hd * M:(hd + 1) * M], wx[:, hd, :], wsl[:, :], start=True, stop=True)
                nc.tensor.matmul(bank[1][:, hd * M:(hd + 1) * M], bxr[:, hd, :], wsl[:, :], start=True, stop=True)
            nc.tensor.matmul(bank[2][0:DH, 0:DH], wqkv[:, 0, :], wqkv[:, 1, :], start=True, stop=True)
            for k in range(2):
                mm = nc.tensor.matmul(bank[3 + k][0:DH, :], wqkv[:, 2, :],
                                      wot[:, 4 * k:4 * k + 4, :].rearrange("p h d -> p (h d)"), start=True, stop=True)
            mm.then_inc(s_f, 1)

    names = ("xn", "xt_p", "xt", "lg_p", "sm1", "chain", "exp", "w", "wt_p", "wt", "xs_p", "xs", "xst_p", "xst",
             "tt_p", "tt", "ut_p", "ut", "al_p", "a1", "aexp", "a", "att_p", "att", "vo_p", "vo", "o_p", "o",
             "y_p", "y", "hb", "st", "hadd")
    S = {n: sem("s_c_" + n) for n in names}
    CH_SM, CH_A = 3, 3

    with nc.Block() as block:
        @block.vector
        def _(dve):
            dve.sem_inc(S["sm1"], 2)
            dve.sem_inc(S["xs"], 1)
            dve.sem_inc(S["ut"], 2)
            dve.sem_inc(S["a1"], 2)
            dve.sem_inc(S["o"], 1)
            dve.sem_inc(S["y"], 1)
            dve.sem_inc(S["a"], 2)
            PER = NB * 5 + (NB // 2) * 4
            with dve.Fori(0, OCT) as q:
                link = [0]

                def chained(ins):
                    link[0] += 1
                    ins.then_inc(S["chain"], 1)
                    dve.wait_ge(S["chain"], q * PER + link[0])

                def norm(k):
                    n = q * NB + k
                    dve.wait_ge(S["xs_p"], n + 1)
                    for j in range(2):
                        tl = n * 2 + j
                        ins = nc.vector.tensor_scalar(xn1[:, k % 2, j, 0:D], h[:, dyn(tl, 1), :], mean[:, dyn(tl, 1)],
                                                      rstd[:, dyn(tl, 1)], ALU.subtract, ALU.mult)
                    ins.then_inc(S["xn"], 1)

                def softmax_max(k):
                    n = q * NB + k
                    l4 = lg[:, k % 2, :, :]
                    dve.wait_ge(S["lg_p"], n + 1)
                    chained(nc.vector.tensor_tensor(l4.rearrange("p (t h) m -> p t (h m)", t=2),
                                                    bank[2 + k % 2][:, :].rearrange("p (t c) -> p t c", t=2),
                                                    bl[:, :, :].broadcast_to([P, 2, HM]), ALU.add))
                    chained(nc.vector.tensor_reduce(mx[:, :], l4, AX.X, ALU.max))
                    nc.vector.tensor_tensor(l4, l4, mx[:, :].rearrange("p (g o) -> p g o", o=1)
                                            .broadcast_to([P, 2 * H, M]), ALU.subtract).then_inc(S["sm1"], 1)

                def softmax_sum(k):
                    n = q * NB + k
                    l4 = lg[:, k % 2, :, :]
                    dve.wait_ge(S["exp"], n + 1)
                    chained(nc.vector.tensor_reduce(sm[:, :], l4, AX.X, ALU.add))
                    chained(nc.vector.reciprocal(sm[:, :], sm[:, :]))
                    nc.vector.tensor_tensor(w[:, k % 2, :, :].rearrange("p t (h m) -> p (t h) m", h=H), l4,
                                            sm[:, :].rearrange("p (g o) -> p g o", o=1)
                                            .broadcast_to([P, 2 * H, M]), ALU.mult).then_inc(S["w"], 1)

                def scale_slices(k):
                    n = q * NB + k
                    dve.wait_ge(S["xs_p"], n + 1 + 2)
                    xp = bank[6][:, 0:2 * (D + 1)].rearrange("p (i d) -> p i d", i=2)
                    link[0] += 1
                    nc.vector.tensor_scalar(dn[:, :], xp[:, :, D], LN_EPS, None, ALU.add).then_inc(S["chain"], 1)
                    dve.wait_ge(S["chain"], q * PER + link[0])
                    nc.vector.reciprocal(dn[:, :], dn[:, :]).then_inc(S["st"], 1)
                    dve.wait_ge(S["st"], n + 1)
                    nc.vector.tensor_tensor(xs[:, k % 2, :, :], xp, dn[:, :].rearrange("p (i o) -> p i o", o=1)
                                            .broadcast_to([P, 2, D + 1]), ALU.mult).then_inc(S["xs"], 1)

                for k in range(NB + 1):
                    if k < NB:
                        norm(k)
                    if k >= 1:
                        softmax_sum(k - 1)
                    if k < NB:
                        softmax_max(k)
                    if k >= 1:
                        scale_slices(k - 1)
                for k in range(NB // 2):
                    dve.wait_ge(S["ut_p"], q * (NB // 2) + k + 1)
                    nc.vector.tensor_copy(ut[:, 2 * k:2 * k + 2, :, :].rearrange("p b h m -> p (b h m)"),
                                          bank[4 + k % 2][0:DH, :]).then_inc(S["ut"], 1)
                for k in range(NB // 2):
                    n = q * (NB // 2) + k
                    a4 = at[:, k % 2, :, :]
                    dve.wait_ge(S["al_p"], n + 1)
                    dve.wait_ge(S["att_p"], n + 1)
                    chained(nc.vector.tensor_scalar(a4, bank[k % 2][:, :].rearrange("p (u c) -> p u c", u=4),
                                                    DH ** -0.5, None, ALU.mult))
                    chained(nc.vector.tensor_tensor(a4, a4, off_block[:, :].rearrange("p (o c) -> p o c", o=1)
                                                    .broadcast_to([P, 4, P]), ALU.add))
                    chained(nc.vector.tensor_reduce(amx[:, :], a4, AX.X, ALU.max))
                    nc.vector.tensor_tensor(a4, a4, amx[:, :].rearrange("p (u o) -> p u o", o=1)
                                            .broadcast_to([P, 4, P]), ALU.subtract).then_inc(S["a1"], 1)
                    dve.wait_ge(S["aexp"], n + 1)
                    chained(nc.vector.tensor_reduce(asm[:, :], a4, AX.X, ALU.add))
                    nc.vector.reciprocal(asm[:, :], asm[:, :]).then_inc(S["hb"], 1)
                    dve.wait_ge(S["hb"], n + 1)
                    nc.vector.tensor_tensor(a4, a4, asm[:, :].rearrange("p (u o) -> p u o", o=1)
                                            .broadcast_to([P, 4, P]), ALU.mult).then_inc(S["a"], 1)
                    dve.wait_ge(S["o_p"], n + 1)
                    nc.vector.tensor_copy(os_[:, k % 2, :, :], bank[6][:, :].rearrange("p (u c) -> p u c", u=4))\
                        .then_inc(S["o"], 1)
                    dve.wait_ge(S["y_p"], n + 1 + 1)
                    tl = (q * NB + 2 * k) * 2
                    h4 = h[:, dyn(tl, 4), :]
                    nc.vector.tensor_tensor(h4, bank[7][:, :].rearrange("p (u d) -> p u d", u=4), h4,
                                            ALU.add).then_inc(S["y"], 1)
                    dve.wait_ge(S["y"], n + 1 + 1)
                    nc.vector.tensor_tensor(h4, h4, bo[:, :, :].broadcast_to([P, 4, D]), ALU.add).then_inc(S["hadd"], 1)
                    dve.wait_ge(S["hadd"], n + 1)
                    for j in range(4):
                        nc.vector.bn_stats(stats[:, dyn(tl + j, 1), :], h[:, dyn(tl + j, 1), :])

        @block.tensor
        def _(pe):
            pe.sem_inc(S["xs_p"], 2)
            pe.sem_inc(S["att_p"], 2)
            pe.sem_inc(S["y_p"], 1)
            with pe.Fori(0, OCT) as q:
                for k in range(NB + 1):
                    n = q * NB + k
                    if k < NB:
                        pe.wait_ge(S["xn"], n + 1)
                        pe.wait_ge(S["xt"], n + 1)
                        if k < 2:
                            pe.wait_ge(S["a1"], q * (NB // 2) + 2)
                        for j in range(2):
                            mm = nc.tensor.transpose(bank[k % 2][:, j * P:(j + 1) * P], xn1[:, k % 2, j, 0:D], ident[:, :])
                        mm.then_inc(S["xt_p"], 1)
                    if k >= 1:
                        kk, n1 = (k - 1) % 2, q * NB + k - 1
                        pe.wait_ge(S["w"], n1 + 1)
                        pe.wait_ge(S["wt"], n1 + 1)
                        if k <= 2:
                            pe.wait_ge(S["vo"], q * (NB // 2) + 2)
                            pe.wait_ge(S["o"], q * (NB // 2) + 1)
                        for i in range(2):
                            for j in range(2):
                                mm = nc.tensor.transpose(bank[4 + kk][:, i * SEQ + j * P:i * SEQ + (j + 1) * P],
                                                         w[:, kk, j, i * P:(i + 1) * P], ident[:, :])
                        mm.then_inc(S["wt_p"], 1)
                        pe.wait_ge(S["xs"], n1 + 1)
                        for i in range(2):
                            for j in range(2):
                                mm = nc.tensor.matmul(bank[6][:, i * (D + 1):(i + 1) * (D + 1)],
                                                      w[:, kk, j, i * P:(i + 1) * P], xn1[:, kk, j, :],
                                                      start=(i == 0 and j == 0), stop=(j == 1), skip_group_check=True)
                        mm.then_inc(S["xs_p"], 1)
                    if k < NB:
                        pe.wait_ge(S["xt"], n + 1 + 2)
                        pe.wait_ge(S["sm1"], n + 1)
                        if k < 2:
                            pe.wait_ge(S["att"], q * (NB // 2) + 2)
                        for j in range(2):
                            mm = nc.tensor.matmul(bank[2 + k % 2][:, j * HM:(j + 1) * HM], xt[:, k % 2, j * P:(j + 1) * P],
                                                  wl[:, :], start=True, stop=True)
                        mm.then_inc(S["lg_p"], 1)
                    if k >= 1:
                        pe.wait_ge(S["xs"], n1 + 2)
                        pe.wait_ge(S["xst"], n1 + 1)
                        if k == 1:
                            pe.wait_ge(S["y"], q * (NB // 2) + 1)
                        for i in range(2):
                            nc.tensor.transpose(bank[7][:, i * P:(i + 1) * P], xs[:, kk, i, 0:D], ident[:, :])
                            mm = nc.tensor.transpose(bank[7][0:1, 2 * P + i * P:2 * P + (i + 1) * P], xs[:, kk, i, D:D + 1],
                                                     ident[:, :])
                        mm.then_inc(S["xst_p"], 1)
                pe.wait_ge(S["xst"], q * NB + NB + 1)
                for hd in range(H):
                    pe.wait_ge(S["tt"], q * H + hd + 1)
                    if hd in (2, 3):
                        pe.wait_ge(S["sm1"], q * NB + NB + 2)
                    nc.tensor.matmul(bank[hd % 4][0:DH, 0:NB * M], wfx[:, hd, :], xst[:, :, hd, :], start=True, stop=False)
                    nc.tensor.matmul(bank[hd % 4][0:DH, 0:NB * M], bfx[0:1, hd, :], rt[0:1, :, hd, :], start=False,
                                     stop=True).then_inc(S["tt_p"], 1)
                pe.wait_ge(S["tt"], q * H + H + 4)
                pe.wait_ge(S["wt"], q * NB + NB + 2)
                for k in range(NB // 2):
                    pe.wait_ge(S["ut"], q * (NB // 2) + k + 1)
                    nc.tensor.matmul(bank[4 + k % 2][:, :], gqk[:, :],
                                     tt[:, 2 * k:2 * k + 2, :, :].rearrange("p b h m -> p (b h m)"), start=True,
                                     stop=True).then_inc(S["ut_p"], 1)
                pe.wait_ge(S["ut"], q * (NB // 2) + NB // 2 + 2)
                for k in range(NB // 2):
                    n = q * (NB // 2) + k
                    pe.wait_ge(S["vo"], n + 1)
                    pe.wait_ge(S["a1"], n + 1)
                    for u in range(4):
                        b, i = 2 * k + u // 2, u % 2
                        hs = slice(4 * i, 4 * i + 4)
                        mm = nc.tensor.matmul(bank[k % 2][:, u * P:(u + 1) * P],
                                              ut[:, b, hs, :].rearrange("p h m -> p (h m)"),
                                              tt[:, b, hs, :].rearrange("p h m -> p (h m)"), start=True, stop=True)
                    mm.then_inc(S["al_p"], 1)
                    for u in range(4):
                        b, i = 2 * k + u // 2, u % 2
                        for r in range(4):
                            mm = nc.tensor.matmul(bank[4 + k % 2][32 * r:32 * r + 32, u * P:(u + 1) * P],
                                                  tt[:, b, 4 * i + r, :], wvo[:, 4 * i + r, :], start=True, stop=True)
                    mm.then_inc(S["vo_p"], 1)
                    pe.wait_ge(S["a"], n + 1 + 2)
                    pe.wait_ge(S["att"], n + 1)
                    for u in range(4):
                        mm = nc.tensor.transpose(bank[2 + k % 2][:, u * P:(u + 1) * P], at[:, k % 2, u, :], ident[:, :])
                    mm.then_inc(S["att_p"], 1)
                    pe.wait_ge(S["att"], n + 1 + 2)
                    pe.wait_ge(S["vo"], n + 1 + 2)
                    pe.wait_ge(S["o"], n + 1)
                    for u in range(4):
                        mm = nc.tensor.matmul(bank[6][:, u * D:(u + 1) * D], att[:, k % 2, u, :], vo[:, k % 2, u, :],
                                              start=True, stop=True)
                    mm.then_inc(S["o_p"], 1)
                    pe.wait_ge(S["o"], n + 2)
                    pe.wait_ge(S["y"], n + 1)
                    for u in range(4):
                        b, j = u // 2, u % 2
                        for i in range(2):
                            mm = nc.tensor.matmul(bank[7][:, u * D:(u + 1) * D],
                                                  wt[:, 2 * k + b, i, j * P:(j + 1) * P], os_[:, k % 2, 2 * b + i, :],
                                                  start=(u == 0 and i == 0), stop=(i == 1), skip_group_check=True)
                    mm.then_inc(S["y_p"], 1)

        @block.scalar
        def _(act):
            act.sem_inc(S["xt"], 2)
            act.sem_inc(S["wt"], 2)
            act.sem_inc(S["xst"], 1)
            act.sem_inc(S["tt"], 4)
            act.sem_inc(S["att"], 2)
            act.sem_inc(S["vo"], 2)
            with act.Fori(0, OCT) as q:
                for k in range(NB + 1):
                    n = q * NB + k
                    if k < NB:
                        act.wait_ge(S["xt_p"], n + 1)
                        act.wait_ge(S["sm1"], n + 1)
                        nc.scalar.copy(xt[:, k % 2, :], bank[k % 2][:, 0:SEQ]).then_inc(S["xt"], 1)
                    if k >= 1:
                        act.wait_ge(S["wt_p"], n)
                        if k == 1:
                            act.wait_ge(S["y_p"], q * (NB // 2) + 1)
                        nc.scalar.copy(wt[:, k - 1, :, :].rearrange("p i s -> p (i s)"),
                                       bank[4 + (k - 1) % 2][:, :]).then_inc(S["wt"], 1)
                    if k < NB:
                        act.wait_ge(S["sm1"], n + 1 + 2)
                        nc.scalar.activation(lg[:, k % 2, :, :], lg[:, k % 2, :, :], ACT.Exp).then_inc(S["exp"], 1)
                    if k >= 1:
                        act.wait_ge(S["xst_p"], n)
                        nc.scalar.copy(xst[:, k - 1, :, :].rearrange("p h m -> p (h m)"), bank[7][:, 0:HM])
                        nc.scalar.copy(rt[0:1, k - 1, :, :].rearrange("p h m -> p (h m)"), bank[7][0:1, HM:2 * HM])\
                            .then_inc(S["xst"], 1)
                for hd in range(H):
                    act.wait_ge(S["tt_p"], q * H + hd + 1)
                    nc.scalar.copy(tt[:, :, hd, :], bank[hd % 4][0:DH, 0:NB * M].rearrange("p (b m) -> p b m", b=NB))\
                        .then_inc(S["tt"], 1)
                for k in range(NB // 2):
                    n = q * (NB // 2) + k
                    act.wait_ge(S["vo_p"], n + 1)
                    nc.scalar.copy(vo[:, k % 2, :, :].rearrange("p u c -> p (u c)"), bank[4 + k % 2][:, :])\
                        .then_inc(S["vo"], 1)
                    act.wait_ge(S["a1"], n + 1 + 2)
                    nc.scalar.activation(at[:, k % 2, :, :], at[:, k % 2, :, :], ACT.Exp).then_inc(S["aexp"], 1)
                    act.wait_ge(S["att_p"], n + 1 + 2)
                    nc.scalar.copy(att[:, k % 2, :, :].rearrange("p u c -> p (u c)"), bank[2 + k % 2][:, :])\
                        .then_inc(S["att"], 1)


def expert_choice_phase(nc, c, t, h, mean, rstd, bank, ident):
    def sb(name, shape, dt=F32):
        return c.enter_context(nc.sbuf_tensor(name, shape, dt))

    def sem(name):
        return c.enter_context(nc.semaphore(name))

    E = GATES
    CAP = SEQ // E
    HB = P // E
    wg = sb("d_wg", [P, E])
    we = sb("d_we", [P, E, D])
    ones = sb("d_ones", [P, P])
    xn = sb("d_xn", [P, 2, TPG, D])
    xt = sb("d_xt", [P, 2, GT])
    gate_h = sb("d_gate", [P, 2, BATCH, E])
    gate = gate_h[:, :, :, :].rearrange("p n b e -> p (n b) e")
    rsum = sb("d_rsum", [P, TILES])
    csum = sb("d_csum", [P, BATCH, E])
    gt = sb("d_gt", [P, 2, SEQ])
    wk = sb("d_wk", [P, 2, 2, SEQ])
    top8 = sb("d_top8", [P, 2, 8])
    alive = sb("d_alive", [P, 2, TILES])
    s_w, s_one = sem("s_d_w"), sem("s_d_one")
    s_xn, s_xtp, s_xt, s_lp, s_l = (sem("s_d_" + n) for n in ("xn", "xt_p", "xt", "logit_p", "logit"))

    def normalise(dve, g, u):
        for j in range(TPG):
            ins = nc.vector.tensor_scalar(xn[:, u, j, :], h[:, dyn(g * TPG + j, 1), :], mean[:, dyn(g * TPG + j, 1)],
                                          rstd[:, dyn(g * TPG + j, 1)], ALU.subtract, ALU.mult)
        return ins

    with nc.Block() as block:
        @block.sync
        def _(sp):
            sp.dma_start(wg[:, :], t["wg"]).then_inc(s_w, 16)
            sp.dma_start(we[:, :, :], t["we"]).then_inc(s_w, 16)

        @block.gpsimd
        def _(pool):
            nc.gpsimd.memset(ones[:, :], 1.0).then_inc(s_one, 1)

        @block.vector
        def _(dve):
            dve.sem_inc(s_l, 2)
            with dve.Fori(0, GROUPS // 2) as i:
                for u in range(2):
                    g = 2 * i + u
                    dve.wait_ge(s_xtp, g + 1)
                    normalise(dve, g, u).then_inc(s_xn, 1)
                for u in range(2):
                    g = 2 * i + u
                    dve.wait_ge(s_lp, g + 1 + 2)
                    nc.vector.tensor_scalar(gate_h[:, :, dyn(2 * g, 2), :],
                                            bank[2 + u][:, 0:TPG * E].rearrange("p (b n e) -> p n b e", b=2, n=2),
                                            GATE_EPS, None, ALU.max).then_inc(s_l, 1)

        @block.tensor
        def _(pe):
            pe.sem_inc(s_xtp, 2)
            pe.sem_inc(s_lp, 2)
            pe.wait_ge(s_w, 32)
            with pe.Fori(0, GROUPS // 2) as i:
                for u in range(2):
                    g = 2 * i + u
                    pe.wait_ge(s_xn, g + 1)
                    pe.wait_ge(s_xt, g + 1)
                    for j in range(TPG):
                        mm = nc.tensor.transpose(bank[u][:, j * P:(j + 1) * P], xn[:, u, j, :], ident[:, :])
                    mm.then_inc(s_xtp, 1)
                for u in range(2):
                    g = 2 * i + u
                    pe.wait_ge(s_xt, g + 1 + 2)
                    pe.wait_ge(s_l, g + 1)
                    for j in range(TPG):
                        mm = nc.tensor.matmul(bank[2 + u][:, j * E:(j + 1) * E], xt[:, u, j * P:(j + 1) * P],
                                              wg[:, :], start=True, stop=True)
                    mm.then_inc(s_lp, 1)

        @block.scalar
        def _(act):
            act.sem_inc(s_xt, 2)
            with act.Fori(0, GROUPS // 2) as i:
                for u in range(2):
                    g = 2 * i + u
                    act.wait_ge(s_xtp, g + 1 + 2)
                    act.wait_ge(s_lp, g + 1)
                    nc.scalar.copy(xt[:, u, :], bank[u][:, :]).then_inc(s_xt, 1)

    s_v, s_cp, s_gp, s_bp = sem("s_d_chain"), sem("s_d_col_p"), sem("s_d_gt_p"), sem("s_d_back_p")
    with nc.Block() as block:
        @block.vector
        def _(dve):
            count = [0]

            def step(ins):
                count[0] += 1
                ins.then_inc(s_v, 1)
                dve.wait_ge(s_v, count[0])

            for it in range(SINKHORN):
                dve.wait_ge(s_cp, it + 1)
                step(nc.vector.reciprocal(csum[:, :, :], bank[0][:, 0:BATCH * E].rearrange("p (b e) -> p b e", e=E)))
                step(nc.vector.tensor_tensor(gate_h[:, :, :, :].rearrange("p n b e -> p n (b e)"),
                                             gate_h[:, :, :, :].rearrange("p n b e -> p n (b e)"),
                                             csum[:, :, :].rearrange("p (o b) e -> p o (b e)", o=1)
                                             .broadcast_to([P, 2, BATCH * E]), ALU.mult))
                step(nc.vector.tensor_reduce(rsum[:, :], gate[:, :, :], AX.X, ALU.add))
                step(nc.vector.reciprocal(rsum[:, :], rsum[:, :]))
                step(nc.vector.tensor_tensor(gate[:, :, :], gate[:, :, :],
                                             rsum[:, :].rearrange("p (t o) -> p t o", o=1)
                                             .broadcast_to([P, TILES, E]), ALU.mult))
            dve.wait_ge(s_gp, 1)
            step(nc.vector.tensor_copy(gt[:, :, :].rearrange("p m n -> p (m n)"), bank[1][:, :]))
            for m in range(2):
                src = gt[:, m, :]
                for r in range(CAP // 8):
                    dst = wk[:, m, r % 2, :]
                    step(nc.vector.max(top8[:, m, :], src))
                    step(nc.vector.match_replace(dst, top8[:, m, :], src, -1.0))
                    src = dst
                step(nc.vector.scalar_tensor_tensor(gt[:, m, :], src, 0.0, gt[:, m, :], ALU.is_lt, ALU.mult))
            dve.wait_ge(s_bp, 1)
            for m in range(2):
                for n in range(2):
                    step(nc.vector.tensor_copy(
                        gate_h[:, n, HB * m:HB * (m + 1), :],
                        bank[2][:, (2 * m + n) * P:(2 * m + n + 1) * P].rearrange("p (b e) -> p b e", e=E)))
            step(nc.vector.memset(alive[:, 0, :], 1.0))
            for e in range(E - 1, -1, -1):
                a, b = (E - 1 - e) % 2, (E - e) % 2
                step(nc.vector.scalar_tensor_tensor(alive[:, b, :], gate[:, :, e], 0.0, alive[:, a, :],
                                                    ALU.is_equal, ALU.mult))
                step(nc.vector.tensor_tensor(gate[:, :, e], gate[:, :, e], alive[:, a, :], ALU.mult))

        @block.tensor
        def _(pe):
            pe.wait_ge(s_one, 1)
            for it in range(SINKHORN):
                if it:
                    pe.wait_ge(s_v, 5 * it)
                for n in range(2):
                    mm = nc.tensor.matmul(bank[0][:, 0:BATCH * E], ones[:, :], gate_h[:, n, :, :].rearrange("p b e -> p (b e)"), start=(n == 0),
                                          stop=(n == 1))
                mm.then_inc(s_cp, 1)
            pe.wait_ge(s_v, 5 * SINKHORN)
            for m in range(2):
                for n in range(2):
                    mm = nc.tensor.transpose(bank[1][:, (2 * m + n) * P:(2 * m + n + 1) * P],
                                             gate_h[:, n, HB * m:HB * (m + 1), :].rearrange("p b e -> p (b e)"), ident[:, :])
            mm.then_inc(s_gp, 1)
            pe.wait_ge(s_v, 5 * SINKHORN + 1 + 2 * (2 * (CAP // 8) + 1))
            for m in range(2):
                for n in range(2):
                    mm = nc.tensor.transpose(bank[2][:, (2 * m + n) * P:(2 * m + n + 1) * P],
                                             gt[:, m, n * P:(n + 1) * P], ident[:, :])
            mm.then_inc(s_bp, 1)

    s2_xn, s2_xtp, s2_xt, s2_yp, s2_y, s2_c = (sem("s_e_" + n) for n in ("xn", "xt_p", "xt", "y_p", "y", "chain"))
    with nc.Block() as block:
        @block.vector
        def _(dve):
            dve.sem_inc(s2_y, 2)
            dve.sem_inc(s2_c, 1)
            with dve.Fori(0, GROUPS // 2) as i:
                for u in range(2):
                    g = 2 * i + u
                    dve.wait_ge(s2_xtp, g + 1)
                    normalise(dve, g, u).then_inc(s2_xn, 1)
                for u in range(2):
                    g = 2 * i + u
                    for j in range(TPG):
                        tl = g * TPG + j
                        dve.wait_ge(s2_yp, tl + 1)
                        for e in range(E):
                            y = bank[2 + 2 * (j % 2) + e // 4][:, (e % 4) * D:(e % 4 + 1) * D]
                            dve.wait_ge(s2_c, tl * E + e + 1)
                            ins = nc.vector.scalar_tensor_tensor(h[:, dyn(tl, 1), :], y, gate_h[:, j % 2, dyn(2 * g + j // 2, 1), e],
                                                                 h[:, dyn(tl, 1), :], ALU.mult, ALU.add)
                            ins.then_inc(s2_c, 1)
                        dve.wait_ge(s2_c, tl * E + E + 1)
                        dve.sem_inc(s2_y, 1)

        @block.tensor
        def _(pe):
            pe.sem_inc(s2_xtp, 2)
            with pe.Fori(0, GROUPS // 2) as i:
                for u in range(2):
                    g = 2 * i + u
                    pe.wait_ge(s2_xn, g + 1)
                    pe.wait_ge(s2_xt, g + 1)
                    for j in range(TPG):
                        mm = nc.tensor.transpose(bank[u][:, j * P:(j + 1) * P], xn[:, u, j, :], ident[:, :])
                    mm.then_inc(s2_xtp, 1)
                for u in range(2):
                    g = 2 * i + u
                    pe.wait_ge(s2_xt, g + 1 + 2)
                    for j in range(TPG):
                        tl = g * TPG + j
                        pe.wait_ge(s2_y, tl + 1)
                        for k in range(2):
                            mm = nc.tensor.matmul(bank[2 + 2 * (j % 2) + k][:, :], xt[:, u, j * P:(j + 1) * P],
                                                  we[:, 4 * k:4 * k + 4, :].rearrange("p e d -> p (e d)"), start=True,
                                                  stop=True)
                        mm.then_inc(s2_yp, 1)

        @block.scalar
        def _(act):
            act.sem_inc(s2_xt, 2)
            with act.Fori(0, GROUPS // 2) as i:
                for u in range(2):
                    g = 2 * i + u
                    act.wait_ge(s2_xtp, g + 1 + 2)
                    nc.scalar.copy(xt[:, u, :], bank[u][:, :]).then_inc(s2_xt, 1)


def kernel(**inputs):
    import numpy as np
    import concourse.bacc as bacc
    from concourse.bass_utils import run_bass_kernel_spmd as run

    nc = bacc.Bacc("TRN2", target_bir_lowering=False, num_devices=1)
    arrays, t = {}, {}

    def give(name, a):
        a = np.ascontiguousarray(a)
        arrays[f"in_{name}"] = a
        t[name] = nc.dram_tensor(f"in_{name}", a.shape, mybir.dt.from_np(a.dtype), kind="ExternalInput").ap()

    x = {k: np.asarray(v) for k, v in inputs.items()}
    give("x", x["x"])
    give("emb", x["L0_tok_emb_weight"])
    give("conv", x["L0_tok_conv_weight"].reshape(D, 2).T)
    wqkv, bqkv = x["L0_attn_Wqkv"], x["L0_attn_bqkv"]
    wqk = np.zeros((D, 4, 4, 32), wqkv.dtype)
    bqk = np.zeros((4, 32, 4), bqkv.dtype)
    lam = np.zeros((4, 32, 2), bqkv.dtype)
    for j in range(4):
        for r in range(4):
            at = (j // 2) * D + (4 * (j % 2) + r) * E0
            wqk[:, j, r, :E0] = wqkv[:, at:at + E0]
            bqk[r, :E0, j] = bqkv[at:at + E0]
            if j < 2:
                lam[r, :E0, j] = x["L0_attn_decay_logits"][4 * j + r]
    give("wqk", wqk.reshape(D, 4, P))
    give("bqk", bqk.reshape(P, 4))
    give("lam", lam.reshape(P, 2))
    give("wv", wqkv[:, 2 * D:])
    give("logits", x["L0_attn_decay_logits"])
    give("wo", x["L0_attn_Wout"])
    give("rows0", np.stack([bqkv[2 * D:], x["L0_attn_bout"], x["L0_attn_ln_gamma"], x["L0_attn_ln_beta"]]))
    give("wr", np.concatenate([x["L0_ffn_Wr"], x["L0_ffn_Wgate"].transpose(1, 0, 2).reshape(D, EXPERTS)], axis=1))
    give("br", np.concatenate([x["L0_ffn_br"], x["L0_ffn_bgate"].reshape(-1)]))
    of = np.array([(4 * g + a, 4 * g + b) for g in range(GRP) for a in range(4) for b in range(a + 1, 4)])
    give("delta", np.concatenate([np.diff(of, axis=0), [[0, 0]]]).astype(np.float32))
    for k in ("w1", "w3", "w2"):
        give(k, x["L0_ffn_" + k.upper()])
    inner = HEADS1 * DH1
    give("wx", x["L1_attn_Wx"].reshape(HEADS1, DH1, D).transpose(1, 0, 2))
    give("bx", x["L1_attn_bx"].reshape(HEADS1, DH1).T)
    give("wsl", x["L1_attn_Wslice"].T)
    give("bsl", x["L1_attn_bslice"])
    give("temp", x["L1_attn_temperature"].reshape(HEADS1))
    give("wqkv1", np.stack([x["L1_attn_Wq"], x["L1_attn_Wk"], x["L1_attn_Wv"]], axis=1))
    give("wot", x["L1_attn_Wout"].T.reshape(HEADS1, DH1, D).transpose(1, 0, 2))
    give("wfx", x["L1_attn_Wfx"].T.reshape(D, HEADS1, DH1))
    give("bfx", x["L1_attn_bfx"].reshape(1, HEADS1, DH1))
    give("bo1", x["L1_attn_bout"])
    give("wg", x["L1_ffn_gate_weight"][0])
    give("we", x["L1_ffn_experts"].transpose(1, 0, 2))
    out = nc.dram_tensor("out_0_dram", (BATCH * SEQ, D), F32, kind="ExternalOutput").ap()
    tower(nc, t, out)
    r = run(nc, [arrays], core_ids=[0])
    return r.results[0]["out_0_dram"].reshape(BATCH, SEQ, D)
```

```python
from contextlib import ExitStack

import concourse.bass as bass
from concourse import mybir

ALU = mybir.AluOpType
ACT = mybir.ActivationFunctionType
AX = mybir.AxisListType
F32 = mybir.dt.float32
I32 = mybir.dt.int32
U32 = mybir.dt.uint32
F16 = mybir.dt.float16
RMAX = bass.bass_isa.ReduceOp.max


P = 128
D = 128
BATCH, SEQ = 32, 256
VOCAB = 125
TILES = BATCH * SEQ // P
TPG = 4
GROUPS = TILES // TPG
GT = TPG * P
HEADS0, E0 = 8, 16
ROUND = 12582912.0
LN_EPS = 1e-5
GRP, EXPERTS, HID = 4, 16, 512
TOP_P = 0.9
PAIRS = 6
BUCKETS = GRP * PAIRS
SLOTS = 2 * TILES + BUCKETS
ROW = D + 4
W_SCALE, W_HID = 64.0, 0.25
HEADS1, DH1, SLICES = 8, 64, 32
OCTET = 8
GATES, SINKHORN, GATE_EPS = 8, 8, 1e-6


def dyn(i, n):
    return bass.ds(i, n)


def stats_vector(nc, dve, stats, mean, rstd, tmp, s_ln, turn, at):
    (s_v, s_sq), n_v = s_ln, 7 * turn
    st = stats[:, at, :]
    m_even, m_odd = st[:, :, 1], st[:, :, 4]
    nc.vector.tensor_tensor(tmp[:, 0, :], m_even, m_odd, ALU.subtract).then_inc(s_v, 1)
    nc.vector.tensor_tensor(tmp[:, 1, :], m_even, m_odd, ALU.add).then_inc(s_v, 1)
    nc.vector.tensor_tensor(tmp[:, 2, :], st[:, :, 2], st[:, :, 5], ALU.add).then_inc(s_v, 1)
    dve.wait_ge(s_v, n_v + 3)
    nc.vector.tensor_scalar(mean[:, at], tmp[:, 1, :], 0.5, None, ALU.mult).then_inc(s_v, 1)
    nc.vector.scalar_tensor_tensor(tmp[:, 0, :], tmp[:, 0, :], 0.25, tmp[:, 0, :],
                                   ALU.mult, ALU.mult).then_inc(s_v, 1)
    dve.wait_ge(s_v, n_v + 5)
    nc.vector.scalar_tensor_tensor(tmp[:, 2, :], tmp[:, 2, :], 1.0 / D, tmp[:, 0, :],
                                   ALU.mult, ALU.add).then_inc(s_v, 1)
    dve.wait_ge(s_sq, turn + 1)
    nc.vector.reciprocal(rstd[:, at], tmp[:, 1, :]).then_inc(s_v, 1)


def stats_scalar(nc, act, tmp, eps_t, s_ln, turn):
    (s_v, s_sq), n_v = s_ln, 7 * turn
    act.wait_ge(s_v, n_v + 6)
    nc.scalar.activation(tmp[:, 1, :], tmp[:, 2, :], ACT.Sqrt, bias=eps_t[:, 0:1]).then_inc(s_sq, 1)


def layer_stats(nc, ctx, stats, mean, rstd, eps_t, s_ln, turn, tiles=TILES):
    tmp = ctx.enter_context(nc.sbuf_tensor(f"ln_tmp_{turn}", [P, 3, tiles], F32))

    with nc.Block() as block:
        @block.vector
        def _(dve):
            stats_vector(nc, dve, stats, mean, rstd, tmp, s_ln, turn, slice(0, tiles))

        @block.scalar
        def _(act):
            stats_scalar(nc, act, tmp, eps_t, s_ln, turn)


def run_ahead(eng, ahead, behind, behind_first=False):
    def both(i):
        def lead():
            for u in range(2):
                ahead(2 * i + 2 + u, u)

        def follow():
            for u in range(2):
                behind(2 * i + u, u)

        for step in (follow, lead) if behind_first else (lead, follow):
            step()

    for u in range(2):
        ahead(u, u)
    with eng.Fori(0, GROUPS // 2 - 1) as i:
        both(i)
    for u in range(2):
        behind(GROUPS - 2 + u, u)


def tower(nc, t, out):
    ctx = ExitStack()
    with ctx:
        def sbp(c, name, shape, dt=F32):
            return c.enter_context(nc.sbuf_tensor(name, shape, dt))

        def sem(c, name):
            return c.enter_context(nc.semaphore(name))

        h = sbp(ctx, "h", [P, TILES, D])
        stats = sbp(ctx, "stats", [P, TILES, 6])
        mean = sbp(ctx, "mean", [P, TILES])
        rstd = sbp(ctx, "rstd", [P, TILES])
        ident = sbp(ctx, "ident", [P, P])
        causal = sbp(ctx, "causal", [P, P])
        iota_p = sbp(ctx, "iota_p", [P, 1])
        eps_t = sbp(ctx, "eps_t", [P, 1])
        bank = [ctx.enter_context(nc.psum_tensor(f"bank{i}", [P, 512], F32)) for i in range(8)]

        pos = sbp(ctx, "pos", [P, TILES, 2], I32)
        s_setup = sem(ctx, "s_setup")
        s_rows = [sem(ctx, f"s_rows{j}") for j in range(TPG)]
        s_issue = sem(ctx, "s_issue")
        s_io = [sem(ctx, f"s_io{u}") for u in range(4)]
        s_ln = (sem(ctx, "s_ln_vec"), sem(ctx, "s_ln_sqrt"))
        with nc.Block() as block:
            @block.gpsimd
            def _(pool):
                nc.gpsimd.memset(ident[:, :], 0.0).then_inc(s_setup, 1)
                nc.gpsimd.memset(causal[:, :], 1.0).then_inc(s_setup, 1)
                pool.wait_ge(s_setup, 2)
                nc.gpsimd.affine_select(out=ident[:, :], in_=ident[:, :], compare_op=ALU.not_equal, fill=1.0,
                                        base=0, pattern=[[-1, P]], channel_multiplier=1).then_inc(s_setup, 1)
                nc.gpsimd.affine_select(out=causal[:, :], in_=causal[:, :], compare_op=ALU.is_ge, fill=0.0,
                                        base=0, pattern=[[1, P]], channel_multiplier=-1).then_inc(s_setup, 1)
                nc.gpsimd.iota(iota_p[:, :], pattern=[[0, 1]], base=0, channel_multiplier=1,
                               allow_small_or_imprecise_dtypes=True).then_inc(s_setup, 1)
                nc.gpsimd.memset(eps_t[:, :], LN_EPS).then_inc(s_setup, 1)

        x_sorted = nc.dram_tensor("x_sorted", (SLOTS * P, ROW), F32).ap()
        y_sorted = nc.dram_tensor("y_sorted", (SLOTS * P, D), F32).ap()
        with ExitStack() as c:
            embed_phase(nc, c, t, h, stats, bank, iota_p, x_sorted, s_io)
        with ExitStack() as c:
            layer_stats(nc, c, stats, mean, rstd, eps_t, s_ln, 0)
            attention_phase(nc, c, t, h, stats, mean, rstd, bank, ident, causal, eps_t, s_ln)

        with ExitStack() as c:
            layer_stats(nc, c, stats, mean, rstd, eps_t, s_ln, 2)
            wrow = sbp(c, "wrow", [P, TILES, 2, 2])
            experts = sbp(c, "experts", [1, SLOTS, 2], I32)
            with ExitStack() as c2:
                routing_phase(nc, c2, t, h, mean, rstd, bank, ident, causal, pos, wrow, experts)
            with ExitStack() as c2:
                sorted_ffn_phase(nc, c2, t, h, mean, rstd, bank, ident, pos, wrow, experts, x_sorted, y_sorted,
                                 s_io, s_rows, s_issue)
        with ExitStack() as c:
            slice_attention_phase(nc, c, t, h, stats, mean, rstd, bank, ident, eps_t, s_ln, 3, pos, y_sorted,
                                  s_rows, s_issue)
        with ExitStack() as c:
            layer_stats(nc, c, stats, mean, rstd, eps_t, s_ln, 3 + BATCH // OCTET)
            expert_choice_phase(nc, c, t, h, mean, rstd, bank, ident, out)


def embed_phase(nc, c, t, h, stats, bank, iota_p, x_sorted, s_io):
    def sb(name, shape, dt=F32):
        return c.enter_context(nc.sbuf_tensor(name, shape, dt))

    def sem(name):
        return c.enter_context(nc.semaphore(name))

    TAPS = 2
    ids = sb("ids", [P, BATCH, SEQ], I32)
    emb = sb("emb", [P, D])
    taps = sb("taps", [P, TAPS, D])
    work = sb("q_work", [P, 3, TAPS, D])
    amax = sb("amax", [P, 8])
    FILLS = 8
    zero = sb("zero_rows", [P, SLOTS // FILLS, ROW])
    s_fill, s_zeros = sem("s_emb_fill"), sem("s_emb_zeros")
    table = sb("table", [P, TAPS, D])
    PARTS = 3
    parts = sb("table_parts", [P, TAPS, PARTS, D], F16)
    rest = sb("table_rest", [P, TAPS, D])
    onehot = sb("onehot", [P, 2, 2, SEQ + 1], F16)

    s_in = sem("s_emb_in")
    s_ids = s_io
    s_zero = sem("s_emb_zero")
    s_q = sem("s_quant")
    s_amax = sem("s_amax")
    s_oh = sem("s_onehot")
    s_rows = sem("s_emb_rows")
    s_h = sem("s_emb_h")
    s_st = sem("s_emb_stats")

    with nc.Block() as block:
        @block.sync
        def _(sp):
            sp.wait_ge(s_zero, 1)
            sp.dma_start(emb[0:VOCAB, :], t["emb"]).then_inc(s_in, 16)
            sp.dma_start(taps[:, :, :], t["conv"].partition_broadcast(P)).then_inc(s_in, 16)
            for q in range(4):
                n = BATCH // 4
                sp.dma_start(ids[:, q * n:(q + 1) * n, :],
                             t["x"][q * n:(q + 1) * n, :].partition_broadcast(P)).then_inc(s_ids[q], 16)
            sp.wait_ge(s_fill, 1)
            n = SLOTS // FILLS
            for k in range(FILLS):
                sp.dma_start(x_sorted.rearrange("(s p) d -> p s d", p=P)[:, k * n:(k + 1) * n, :], zero[:, :, :])\
                    .then_inc(s_zeros, 16)
            sp.wait_ge(s_zeros, 16 * FILLS)

        @block.gpsimd
        def _(pool):
            nc.gpsimd.memset(emb[:, :], 0.0).then_inc(s_zero, 1)
            nc.gpsimd.memset(onehot[:, :, :, :], 0.0).then_inc(s_zero, 1)
            nc.gpsimd.memset(zero[:, :, :], 0.0).then_inc(s_fill, 1)
            for k in range(2):
                pool.wait_ge(s_q, 2 * k + 2)
                nc.gpsimd.partition_all_reduce(amax[:, 2 + k:3 + k], amax[:, k:k + 1], P, RMAX).then_inc(s_amax, 1)

        @block.vector
        def _(dve):
            count = [0]

            def step(ins):
                count[0] += 1
                ins.then_inc(s_q, 1)
                dve.wait_ge(s_q, count[0])

            dve.wait_ge(s_in, 32)
            mats = [(emb[:, :], work[:, 0, 0, :], work[:, 1, 0, :]),
                    (taps[:, :, :], work[:, 0, :, :], work[:, 1, :, :])]
            for k, (w, a, _) in enumerate(mats):
                step(nc.vector.scalar_tensor_tensor(a, w, -1.0, w, ALU.mult, ALU.max))
                step(nc.vector.tensor_reduce(amax[:, k:k + 1], a, AX.X if k == 0 else AX.XY, ALU.max))
            for k, (w, a, b) in enumerate(mats):
                dve.wait_ge(s_amax, k + 1)
                scale, inv = amax[:, 4 + k:5 + k], amax[:, 6 + k:7 + k]
                step(nc.vector.tensor_scalar(scale, amax[:, 2 + k:3 + k], 1.0 / 127.0, None, ALU.mult))
                step(nc.vector.reciprocal(inv, scale))
                step(nc.vector.tensor_scalar(a, w, inv, ROUND, ALU.mult, ALU.add))
                step(nc.vector.tensor_scalar(a, a, ROUND, scale, ALU.subtract, ALU.mult))
                step(nc.vector.tensor_tensor(b, a, w, ALU.subtract))
                step(nc.vector.tensor_tensor(w, w, b, ALU.add))
            for k in range(TAPS):
                step(nc.vector.tensor_tensor(table[:, k, :], emb[:, :], taps[:, k, :], ALU.mult))
            step(nc.vector.tensor_scalar(rest[:, :, :], table[:, :, :], W_SCALE, None, ALU.mult))
            for m in range(PARTS):
                step(nc.vector.tensor_copy(parts[:, :, m, :], rest[:, :, :]))
                if m < PARTS - 1:
                    step(nc.vector.tensor_tensor(rest[:, :, :], rest[:, :, :], parts[:, :, m, :], ALU.subtract))

            dve.wait_ge(s_zero, 2)
            for q in range(4):
                dve.wait_ge(s_ids[q], 16)

            def encode(g, u):
                dve.wait_ge(s_rows, TPG * g + TPG)
                nc.vector.tensor_scalar(onehot[:, u, :, 1:SEQ + 1], ids[:, dyn(2 * g, 2), :], float(VOCAB - 1),
                                        iota_p[:, 0:1], ALU.min, ALU.is_equal).then_inc(s_oh, 1)

            def row_stats(g, u):
                for j in range(TPG):
                    tile = g * TPG + j
                    dve.wait_ge(s_h, tile + 1 + 2 * TPG)
                    nc.vector.bn_stats(stats[:, dyn(tile, 1), :], h[:, dyn(tile, 1), :]).then_inc(s_st, 1)

            run_ahead(dve, encode, row_stats)

        @block.tensor
        def _(pe):
            pe.sem_inc(s_rows, 2 * TPG)
            pe.wait_ge(s_q, 18 + 2 * PARTS)
            with pe.Fori(0, GROUPS // 2) as i:
                for u in range(2):
                    g = 2 * i + u
                    pe.wait_ge(s_oh, g + 1)
                    for j in range(TPG):
                        b, at = j // 2, (j % 2) * P
                        pe.wait_ge(s_h, g * TPG + j + 1)
                        for k in range(TAPS):
                            for m in range(PARTS):
                                mm = nc.tensor.matmul(bank[u * TPG + j][:, 0:D], onehot[:, u, b, at + k:at + k + P],
                                                      parts[:, k, m, :], start=(k == 0 and m == 0),
                                                      stop=(k == TAPS - 1 and m == PARTS - 1))
                        mm.then_inc(s_rows, 1)

        @block.scalar
        def _(act):
            act.sem_inc(s_h, 2 * TPG)

            def turn(i):
                for u in range(2):
                    g = 2 * i + u
                    for j in range(TPG):
                        act.wait_ge(s_rows, g * TPG + j + 1 + 2 * TPG)
                        nc.scalar.activation(h[:, dyn(g * TPG + j, 1), :], bank[u * TPG + j][:, 0:D],
                                             ACT.Relu, scale=1.0 / W_SCALE).then_inc(s_h, 1)

            turn(0)
            with act.Fori(1, GROUPS // 2) as i:
                turn(i)


def attention_phase(nc, c, t, h, stats, mean, rstd, bank, ident, causal, eps_t, s_ln):
    def sb(name, shape, dt=F32):
        return c.enter_context(nc.sbuf_tensor(name, shape, dt))

    def sem(name):
        return c.enter_context(nc.semaphore(name))

    H, E, R, V = HEADS0, E0, 4, E0 + 1
    NQK = 4
    PHI, PROB = 32.0, 16.0
    wall = sb("wall", [P, (NQK + 1) * P])
    wh = sb("wh", [P, (NQK + 1) * P], F16)
    wl = sb("wlo", [P, (NQK + 1) * P], F16)
    bqk = sb("bqk", [P, 2, NQK])
    wo = sb("wo", [P, D])
    rows = sb("rows0", [P, 4, D])
    lam = sb("lam", [P, 2])
    valid = sb("valid", [P, 2])
    powr = sb("powr", [P, 8, 2])
    fade = sb("fade", [P, 2, 2 * P])
    logits = sb("logits", [P, H])
    powh = sb("powh", [P, 7, H])
    tri = sb("tri", [P, H, P])
    diag = sb("diag", [P, H, P])
    tri4 = sb("tri4", [P, R, 4, P])
    bv4 = sb("bv4", [P, GT])
    col = sb("col", [P, 3, H])
    bdiag = sb("bdiag", [P, 2, R, V])

    o_all = sb("o_all", [P, TILES, D])
    xn = sb("xn", [P, 2, TPG, D])
    xh = sb("xh", [P, 2, GT], F16)
    xl = sb("xl", [P, 2, GT], F16)
    ebuf = sb("ebuf", [P, 2, GT])
    xbuf = sb("xbuf", [P, 2, GT])
    phi = sb("phi", [P, 2, NQK, GT])
    ph = sb("ph", [P, 2, NQK, GT], F16)
    pl = sb("pl", [P, 2, NQK, GT], F16)
    qd = sb("qd", [P, 2, 2, 2, P])
    vh = sb("vh", [P, 2, TPG, H, V], F16)
    vl = sb("vl", [P, 2, TPG, H, V], F16)
    v1 = sb("v1", [P, 2, TPG, H, V])
    ktok = sb("ktok", [P, 2 * P])
    state = sb("state", [P, 2, R * V])
    prob = sb("prob", [P, R, 4, P])
    prh = sb("prh", [P, R, 4, P], F16)
    prl = sb("prl", [P, R, 4, P], F16)
    den = sb("den", [P, 2, H])
    on = sb("on", [P, 2, D])
    ot = sb("ot", [P, 2 * P])
    off = sb("off", [P, 4, D])

    s_w = sem("s_a_weights")
    s_c = sem("s_a_consts")
    s_e = sem("s_a_exp")
    s_pool = sem("s_a_pool")
    names = ("xn", "xt_p", "xh", "xl", "qk_p", "qk_e", "elu", "ph", "pl", "qd", "v_p", "v", "vh", "vl", "kt_p", "kt",
             "st_p", "st", "sc_p", "sc", "prh", "prl", "pv_p", "den", "on", "ot_p", "ot", "o_p", "o")
    S = {n: sem("s_a_" + n) for n in names}

    with nc.Block() as block:
        @block.sync
        def _(sp):
            sp.dma_start(wall[:, 0:NQK * P], t["wqk"].rearrange("p j d -> p (j d)")).then_inc(s_w, 16)
            sp.dma_start(wall[:, NQK * P:], t["wv"]).then_inc(s_w, 16)
            sp.dma_start(bqk[:, 0, :], t["bqk"]).then_inc(s_w, 16)
            sp.dma_start(wo[:, :], t["wo"]).then_inc(s_w, 16)
            sp.dma_start(rows[:, :, :], t["rows0"].partition_broadcast(P)).then_inc(s_w, 16)
            sp.dma_start(lam[:, :], t["lam"]).then_inc(s_w, 16)
            sp.dma_start(logits[:, :], t["logits"].partition_broadcast(P)).then_inc(s_w, 16)

        @block.gpsimd
        def _(pool):
            nc.gpsimd.memset(valid[:, 0:1], 0.0).then_inc(s_pool, 1)
            nc.gpsimd.memset(valid[:, 1:2], 1.0).then_inc(s_pool, 1)
            nc.gpsimd.memset(bdiag[:, :, :, :], 0.0).then_inc(s_pool, 1)
            nc.gpsimd.memset(v1[:, :, :, :, :], 1.0).then_inc(s_pool, 1)
            pool.wait_ge(s_pool, 4)
            for r in range(R):
                nc.gpsimd.memset(valid[32 * r:32 * r + E, 0:1], 1.0).then_inc(s_pool, 1)
                nc.gpsimd.memset(valid[32 * r:32 * r + E, 1:2], 0.0).then_inc(s_pool, 1)
                nc.gpsimd.memset(bdiag[32 * r:32 * r + 32, :, r, :], 1.0).then_inc(s_pool, 1)

        @block.scalar
        def _(act):
            act.wait_ge(s_w, 112)
            nc.scalar.activation(lam[:, :], lam[:, :], ACT.Exp, scale=-1.0).then_inc(s_e, 1)
            nc.scalar.activation(logits[:, :], logits[:, :], ACT.Exp, scale=-1.0).then_inc(s_e, 1)
            nc.scalar.activation(wh[:, :], wall[:, :], ACT.Copy, scale=W_SCALE).then_inc(s_e, 1)

        @block.vector
        def _(dve):
            count = [0]

            def step(*links):
                for ins in links:
                    ins.then_inc(s_c, 1)
                count[0] += len(links)
                dve.wait_ge(s_c, count[0])

            def over_t(a):
                return a.rearrange("p (h o) -> p h o", o=1).broadcast_to([P, H, P])

            dve.wait_ge(s_pool, 4 + 3 * R)
            dve.wait_ge(s_e, 3)
            step(nc.vector.tensor_scalar(lam[:, :], lam[:, :], 1.0, None, ALU.add),
                 nc.vector.tensor_scalar(logits[:, :], logits[:, :], 1.0, None, ALU.add),
                 nc.vector.scalar_tensor_tensor(wl[:, :], wall[:, :], W_SCALE, wh[:, :], ALU.mult, ALU.subtract))
            step(nc.vector.reciprocal(lam[:, :], lam[:, :]),
                 nc.vector.reciprocal(powh[:, 0, :], logits[:, :]))
            step(nc.vector.tensor_scalar(powr[:, 0, :], lam[:, :], valid[:, 0:1], valid[:, 1:2], ALU.mult, ALU.add),
                 nc.vector.tensor_scalar(bqk[:, 1, :], bqk[:, 0, :], valid[:, 0:1], None, ALU.add),
                 nc.vector.tensor_scalar(col[:, 0, 0:1], valid[:, 1:2], -1e4, None, ALU.mult),
                 nc.vector.memset(fade[:, :, 0:1], 1.0),
                 nc.vector.memset(tri[:, :, 0:1], 1.0))
            step(nc.vector.tensor_scalar(bqk[:, 0, :], bqk[:, 0, :], col[:, 0, 0:1], None, ALU.add))
            for k in range(8):
                n = 1 << k
                links = [nc.vector.tensor_scalar(fade[:, i, n:2 * n], fade[:, i, 0:n], powr[:, k, i:i + 1],
                                                 None, ALU.mult) for i in range(2)]
                if k < 7:
                    links.append(nc.vector.tensor_tensor(tri[:, :, n:2 * n], tri[:, :, 0:n], powh[:, k, :]
                                                         .rearrange("p (h o) -> p h o", o=1).broadcast_to([P, H, n]),
                                                         ALU.mult))
                    links.append(nc.vector.tensor_tensor(powr[:, k + 1, :], powr[:, k, :], powr[:, k, :], ALU.mult))
                if k < 6:
                    links.append(nc.vector.tensor_tensor(powh[:, k + 1, :], powh[:, k, :], powh[:, k, :], ALU.mult))
                step(*links)
            step(nc.vector.reciprocal(col[:, 1, :], tri[:, :, P // 2]),
                 nc.vector.tensor_scalar(fade[:, :, 1:P + 1], fade[:, :, 1:P + 1], PROB * E ** -0.5, valid[:, 0:1],
                                         ALU.mult, ALU.mult))
            step(nc.vector.tensor_tensor(tri[:, :, :], tri[:, :, :], over_t(col[:, 1, :]), ALU.mult))
            step(nc.vector.tensor_tensor(diag[:, :, :], tri[:, :, :], ident[:, :].rearrange("p (o t) -> p o t", o=1)
                                         .broadcast_to([P, H, P]), ALU.mult))
            step(nc.vector.tensor_reduce(col[:, 0, :], diag[:, :, :], AX.X, ALU.add))
            step(nc.vector.reciprocal(col[:, 1, :], col[:, 0, :]))
            step(nc.vector.tensor_tensor(col[:, 2, :], col[:, 1, :], tri[:, :, P - 1], ALU.mult))
            step(nc.vector.tensor_tensor(tri[:, :, :], tri[:, :, :], over_t(col[:, 1, :]), ALU.mult))
            step(nc.vector.scalar_tensor_tensor(
                tri[:, :, :], tri[:, :, :], PROB * E ** -0.5 / (PHI * PHI),
                causal[:, :].rearrange("p (o t) -> p o t", o=1).broadcast_to([P, H, P]), ALU.mult, ALU.mult))
            for j in range(2):
                for r in range(R):
                    nc.vector.tensor_copy(tri4[:, r, 2 * j:2 * j + 2, :],
                                          tri[:, :, :].rearrange("p (f r) t -> p r f t", r=R)[:, r, :, :])
            for j in range(TPG):
                nc.vector.tensor_copy(bv4[:, j * D:(j + 1) * D], rows[:, 0, :])

    def after(eng, sem, count):
        if not isinstance(count, int) or count > 0:
            eng.wait_ge(sem, count)

    def steps(eng, prologue, batch, epilogue):
        prologue()
        for u in range(2):
            for b in range(2):
                batch(u, u, b, u == 0 and b == 0, True, True)
        with eng.Fori(1, GROUPS // 2 - 1) as i:
            for u in range(2):
                for b in range(2):
                    batch(2 * i + u, u, b, False, True, True)
        for u in range(2):
            for b in range(2):
                batch(GROUPS - 2 + u, u, b, False, u == 0, False)
        epilogue()

    with nc.Block() as block:
        @block.tensor
        def _(pe):
            def transpose_rows(g, u):
                pe.wait_ge(S["xn"], g + 1)
                for j in range(TPG):
                    mm = nc.tensor.transpose(bank[0][:, j * P:(j + 1) * P], xn[:, u, j, :], ident[:, :])
                mm.then_inc(S["xt_p"], 1)

            def project(g, u, j):
                pe.wait_ge(S["xl"], g + 1)
                after(pe, S["qk_e"], NQK * g + j)
                hi, lo = wh[:, j * P:(j + 1) * P], wl[:, j * P:(j + 1) * P]
                nc.tensor.matmul(bank[1][:, :], hi, xh[:, u, :], start=True, stop=False)
                nc.tensor.matmul(bank[1][:, :], hi, xl[:, u, :], start=False, stop=False)
                nc.tensor.matmul(bank[1][:, :], lo, xh[:, u, :], start=False, stop=True).then_inc(S["qk_p"], 1)

            def values(g, u):
                hi, lo = wh[:, NQK * P:], wl[:, NQK * P:]
                for j in range(TPG):
                    y, at = bank[0][:, j * D:(j + 1) * D], slice(j * P, (j + 1) * P)
                    nc.tensor.matmul(y, xh[:, u, at], hi, start=(j == 0), stop=False, skip_group_check=True)
                    nc.tensor.matmul(y, xh[:, u, at], lo, start=False, stop=False, skip_group_check=True)
                    mm = nc.tensor.matmul(y, xl[:, u, at], hi, start=False, stop=True, skip_group_check=True)
                mm.then_inc(S["v_p"], 1)

            def keys(g, u, b):
                pe.wait_ge(S["elu"], NQK * g + NQK)
                for hf in range(2):
                    mm = nc.tensor.transpose(bank[2][:, hf * P:(hf + 1) * P],
                                             phi[:, u, 2 + hf, 2 * b * P:(2 * b + 1) * P], ident[:, :])
                mm.then_inc(S["kt_p"], 1)

            def scores(g, u, b, r):
                pe.wait_ge(S["pl"], NQK * g + NQK)
                for j in range(2):
                    for hf in range(2):
                        to = bank[4 + r][:, (2 * j + hf) * P:(2 * j + hf + 1) * P]
                        at = slice((2 * b + j) * P, (2 * b + j + 1) * P)
                        rr = slice(32 * r, 32 * r + 32)
                        nc.tensor.matmul(to, ph[rr, u, 2 + hf, at], ph[rr, u, hf, at],
                                         start=(j == 0 and hf == 0), stop=False, skip_group_check=True)
                        nc.tensor.matmul(to, ph[rr, u, 2 + hf, at], pl[rr, u, hf, at],
                                         start=False, stop=False, skip_group_check=True)
                        mm = nc.tensor.matmul(to, pl[rr, u, 2 + hf, at], ph[rr, u, hf, at],
                                              start=False, stop=True, skip_group_check=True)
                mm.then_inc(S["sc_p"], 1)

            def make_state(n, u, b):
                pe.wait_ge(S["kt"], n + 1)
                for hf in range(2):
                    mm = nc.tensor.matmul(bank[2][:, hf * R * V:(hf + 1) * R * V], ktok[:, hf * P:(hf + 1) * P],
                                          v1[:, u, 2 * b, R * hf:R * hf + R, :].rearrange("p h v -> p (h v)"),
                                          start=(hf == 0), stop=True, skip_group_check=True)
                mm.then_inc(S["st_p"], 1)

            def use_state(g, n, u, b):
                pe.wait_ge(S["st"], n + 1)
                pe.wait_ge(S["qd"], 2 * g + 2)
                after(pe, S["o"], n)
                for hf in range(2):
                    at = H * V + hf * R * V
                    nc.tensor.matmul(bank[3][:, at:at + R * V], qd[:, u, hf, b, :],
                                     state[:, hf, :], start=(hf == 0), stop=False, skip_group_check=True)

            def weigh(n, u, b, r):
                pe.wait_ge(S["prl"], 4 * n + r + 1)
                for j in range(2):
                    for hf in range(2):
                        hd = R * hf + r
                        at = j * H * V + hd * V
                        to = bank[3][:, at:at + V]
                        hi, lo = vh[:, u, 2 * b + j, hd, :], vl[:, u, 2 * b + j, hd, :]
                        nc.tensor.matmul(to, prh[:, r, 2 * j + hf, :], hi, start=False, stop=False, skip_group_check=True)
                        nc.tensor.matmul(to, prh[:, r, 2 * j + hf, :], lo, start=False, stop=False, skip_group_check=True)
                        mm = nc.tensor.matmul(to, prl[:, r, 2 * j + hf, :], hi, start=False, stop=True,
                                              skip_group_check=True)
                if r == R - 1:
                    mm.then_inc(S["pv_p"], 1)

            def transpose_out(n):
                pe.wait_ge(S["on"], n + 1)
                for j in range(2):
                    mm = nc.tensor.transpose(bank[3][:, j * P:(j + 1) * P], on[:, j, :], ident[:, :])
                mm.then_inc(S["ot_p"], 1)

            def project_out(n):
                pe.wait_ge(S["ot"], n + 1)
                for j in range(2):
                    mm = nc.tensor.matmul(bank[3][:, j * D:(j + 1) * D], ot[:, j * P:(j + 1) * P], wo[:, :],
                                          start=(j == 0), stop=True, skip_group_check=True)
                mm.then_inc(S["o_p"], 1)

            def prologue():
                transpose_rows(0, 0)
                for j in range(NQK):
                    project(0, 0, j)
                values(0, 0)

            def batch(g, u, b, first, more, more2):
                n = 2 * g + b
                keys(g, u, b)
                if b == 0:
                    pe.wait_ge(S["vl"], g + 1)
                    if more:
                        transpose_rows(g + 1, 1 - u)
                scores(g, u, b, 0)
                if b == 1 and more:
                    project(g + 1, 1 - u, 3)
                scores(g, u, b, 1)
                if not first:
                    transpose_out(n - 1)
                make_state(n, u, b)
                if b == 0 and more:
                    project(g + 1, 1 - u, 0)
                scores(g, u, b, 2)
                scores(g, u, b, 3)
                if not first:
                    project_out(n - 1)
                if more:
                    if b == 0:
                        project(g + 1, 1 - u, 1)
                    else:
                        values(g + 1, 1 - u)
                use_state(g, n, u, b)
                for r in range(R):
                    weigh(n, u, b, r)
                if b == 0 and more:
                    project(g + 1, 1 - u, 2)

            def epilogue():
                transpose_out(BATCH - 1)
                project_out(BATCH - 1)

            steps(pe, prologue, batch, epilogue)

        @block.scalar
        def _(act):
            def rows_hi(g, u):
                act.wait_ge(S["xt_p"], g + 1)
                nc.scalar.copy(xh[:, u, :], bank[0][:, :]).then_inc(S["xh"], 1)

            def exponent(g, j):
                act.wait_ge(S["qk_p"], NQK * g + j + 1)
                after(act, S["elu"], NQK * g + j - 1)
                nc.scalar.activation(ebuf[:, j % 2, :], bank[1][:, :], ACT.Exp, scale=1.0 / W_SCALE,
                                     bias=bqk[:, 0, j:j + 1])
                nc.scalar.activation(xbuf[:, j % 2, :], bank[1][:, :], ACT.Identity, scale=1.0 / W_SCALE,
                                     bias=bqk[:, 1, j:j + 1]).then_inc(S["qk_e"], 1)

            def phi_hi(g, u, j):
                act.wait_ge(S["elu"], NQK * g + j + 1)
                nc.scalar.activation(ph[:, u, j, :], phi[:, u, j, :], ACT.Copy, scale=PHI).then_inc(S["ph"], 1)

            def prob_hi(n, r):
                act.wait_ge(S["sc"], 4 * n + r + 1)
                nc.scalar.copy(prh[:, r, :, :].rearrange("p x q -> p (x q)"),
                               prob[:, r, :, :].rearrange("p x q -> p (x q)")).then_inc(S["prh"], 1)

            def v_hi(g, u):
                act.wait_ge(S["v"], g + 1)
                nc.scalar.copy(vh[:, u, :, :, :].rearrange("p t h v -> p (t h v)"),
                               v1[:, u, :, :, :].rearrange("p t h v -> p (t h v)")).then_inc(S["vh"], 1)

            def out_copy(n):
                act.wait_ge(S["ot_p"], n + 1)
                nc.scalar.copy(ot[:, :], bank[3][:, 0:2 * P]).then_inc(S["ot"], 1)

            def prologue():
                rows_hi(0, 0)
                for j in range(NQK):
                    exponent(0, j)
                    phi_hi(0, 0, j)
                v_hi(0, 0)

            def batch(g, u, b, first, more, more2):
                n = 2 * g + b
                if b == 0 and more:
                    rows_hi(g + 1, 1 - u)
                prob_hi(n, 0)
                if b == 1 and more:
                    exponent(g + 1, 3)
                prob_hi(n, 1)
                if not first:
                    out_copy(n - 1)
                if more:
                    if b == 0:
                        exponent(g + 1, 0)
                    else:
                        phi_hi(g + 1, 1 - u, 3)
                prob_hi(n, 2)
                if b == 0 and more:
                    phi_hi(g + 1, 1 - u, 0)
                prob_hi(n, 3)
                if b == 1 and more:
                    v_hi(g + 1, 1 - u)
                if b == 0 and more:
                    exponent(g + 1, 1)
                    phi_hi(g + 1, 1 - u, 1)
                    exponent(g + 1, 2)
                    phi_hi(g + 1, 1 - u, 2)

            steps(act, prologue, batch, lambda: out_copy(BATCH - 1))

        @block.vector
        def _(dve):
            def normalise(g, u):
                after(dve, S["xt_p"], g - 1)
                for j in range(TPG):
                    ins = nc.vector.tensor_scalar(xn[:, u, j, :], h[:, dyn(g * TPG + j, 1), :],
                                                  mean[:, dyn(g * TPG + j, 1)], rstd[:, dyn(g * TPG + j, 1)],
                                                  ALU.subtract, ALU.mult)
                ins.then_inc(S["xn"], 1)

            def rows_lo(g, u):
                dve.wait_ge(S["xh"], g + 1)
                nc.vector.tensor_tensor(xl[:, u, :], bank[0][:, :], xh[:, u, :], ALU.subtract).then_inc(S["xl"], 1)

            def elu(g, u, j):
                dve.wait_ge(S["qk_e"], NQK * g + j + 1)
                nc.vector.scalar_tensor_tensor(phi[:, u, j, :], ebuf[:, j % 2, :], 1.0, xbuf[:, j % 2, :],
                                               ALU.min, ALU.max).then_inc(S["elu"], 1)

            def phi_lo(g, u, j):
                dve.wait_ge(S["ph"], NQK * g + j + 1)
                nc.vector.scalar_tensor_tensor(pl[:, u, j, :], phi[:, u, j, :], PHI, ph[:, u, j, :],
                                               ALU.mult, ALU.subtract).then_inc(S["pl"], 1)

            def add_bias(g, u):
                dve.wait_ge(S["v_p"], g + 1)
                nc.vector.scalar_tensor_tensor(v1[:, u, :, :, 0:E].rearrange("p t h e -> p (t h) e"),
                                               bank[0][:, :].rearrange("p (x e) -> p x e", e=E), 1.0 / W_SCALE,
                                               bv4[:, :].rearrange("p (x e) -> p x e", e=E),
                                               ALU.mult, ALU.add).then_inc(S["v"], 1)

            def v_lo(g, u):
                dve.wait_ge(S["vh"], g + 1)
                nc.vector.tensor_tensor(vl[:, u, :, :, :].rearrange("p t h v -> p (t h v)"),
                                        v1[:, u, :, :, :].rearrange("p t h v -> p (t h v)"),
                                        vh[:, u, :, :, :].rearrange("p t h v -> p (t h v)"),
                                        ALU.subtract).then_inc(S["vl"], 1)

            def mask(n, r):
                dve.wait_ge(S["sc_p"], 4 * n + r + 1)
                nc.vector.tensor_tensor(prob[:, r, :, :], bank[4 + r][:, :].rearrange("p (x q) -> p x q", x=4),
                                        tri4[:, r, :, :], ALU.mult).then_inc(S["sc"], 1)

            def fade_keys(n):
                dve.wait_ge(S["kt_p"], n + 1)
                nc.vector.tensor_tensor(ktok[:, :].rearrange("p (h e) -> p h e", h=H),
                                        bank[2][:, 0:2 * P].rearrange("p (h e) -> p h e", h=H),
                                        col[:, 2, :].rearrange("p (h o) -> p h o", o=1).broadcast_to([P, H, 2 * E]),
                                        ALU.mult).then_inc(S["kt"], 1)

            def mask_state(n):
                dve.wait_ge(S["st_p"], n + 1)
                nc.vector.tensor_tensor(state[:, :, :], bank[2][:, 0:2 * R * V].rearrange("p (i c) -> p i c", i=2),
                                        bdiag[:, :, :, :].rearrange("p i r v -> p i (r v)"),
                                        ALU.mult).then_inc(S["st"], 1)

            def divide(n):
                dve.wait_ge(S["pv_p"], n + 1)
                pv = bank[3][:, 0:2 * H * V].rearrange("p (t h v) -> p t h v", t=2, h=H)
                nc.vector.tensor_scalar(den[:, :, :], pv[:, :, :, E], PROB * LN_EPS, None, ALU.add).then_inc(S["den"], 1)
                dve.wait_ge(S["den"], 2 * n + 1)
                nc.vector.reciprocal(den[:, :, :], den[:, :, :]).then_inc(S["den"], 1)
                dve.wait_ge(S["den"], 2 * n + 2)
                nc.vector.tensor_tensor(on[:, :, :].rearrange("p t (h e) -> p t h e", h=H), pv[:, :, :, 0:E],
                                        den[:, :, :].rearrange("p t (h o) -> p t h o", o=1)
                                        .broadcast_to([P, 2, H, E]), ALU.mult).then_inc(S["on"], 1)

            def out_rows(n):
                dve.wait_ge(S["o_p"], n + 1)
                nc.vector.tensor_tensor(o_all[:, dyn(2 * n, 2), :], bank[3][:, 0:2 * D].rearrange("p (t d) -> p t d", t=2),
                                        rows[:, 1:2, :].broadcast_to([P, 2, D]), ALU.add).then_inc(S["o"], 1)

            def out_stats(n):
                dve.wait_ge(S["o"], n + 1)
                for j in range(2):
                    nc.vector.bn_stats(stats[:, dyn(2 * n + j, 1), :], o_all[:, dyn(2 * n + j, 1), :])

            def prologue():
                for g in range(2):
                    normalise(g, g)
                rows_lo(0, 0)
                for j in range(NQK):
                    elu(0, 0, j)
                    phi_lo(0, 0, j)
                add_bias(0, 0)
                v_lo(0, 0)

            def batch(g, u, b, first, more, more2):
                n = 2 * g + b
                fade_keys(n)
                if b == 0 and more:
                    rows_lo(g + 1, 1 - u)
                mask(n, 0)
                if b == 1 and more:
                    phi_lo(g + 1, 1 - u, 2)
                    elu(g + 1, 1 - u, 3)
                mask(n, 1)
                mask_state(n)
                if b == 0 and more:
                    elu(g + 1, 1 - u, 0)
                mask(n, 2)
                if b == 1 and more:
                    phi_lo(g + 1, 1 - u, 3)
                mask(n, 3)
                if not first:
                    out_rows(n - 1)
                if b == 1 and more:
                    add_bias(g + 1, 1 - u)
                if b == 0 and more:
                    elu(g + 1, 1 - u, 1)
                    phi_lo(g + 1, 1 - u, 0)
                    phi_lo(g + 1, 1 - u, 1)
                if not first:
                    out_stats(n - 1)
                if b == 1 and more:
                    v_lo(g + 1, 1 - u)
                divide(n)
                if b == 1 and more2:
                    normalise(g + 2, u)
                if b == 0 and more:
                    elu(g + 1, 1 - u, 2)

            def epilogue():
                out_rows(BATCH - 1)
                out_stats(BATCH - 1)

            steps(dve, prologue, batch, epilogue)

        @block.gpsimd
        def _(pool):
            def fade_queries(g, u, j):
                pool.wait_ge(S["elu"], NQK * g + j + 1)
                nc.gpsimd.tensor_tensor(qd[:, u, j, :, :],
                                        phi[:, u, j, :].rearrange("p (b s t) -> p b s t", b=2, s=2)[:, :, 1, :],
                                        fade[:, j:j + 1, 1:P + 1].broadcast_to([P, 2, P]), ALU.mult).then_inc(S["qd"], 1)

            def prob_lo(n, r):
                pool.wait_ge(S["prh"], 4 * n + r + 1)
                nc.gpsimd.tensor_tensor(prl[:, r, :, :].rearrange("p x q -> p (x q)"),
                                        prob[:, r, :, :].rearrange("p x q -> p (x q)"),
                                        prh[:, r, :, :].rearrange("p x q -> p (x q)"),
                                        ALU.subtract).then_inc(S["prl"], 1)

            def prologue():
                for j in range(2):
                    fade_queries(0, 0, j)

            def batch(g, u, b, first, more, more2):
                for r in range(R):
                    prob_lo(2 * g + b, r)
                if b == 0 and more:
                    for j in range(2):
                        fade_queries(g + 1, 1 - u, j)

            steps(pool, prologue, batch, lambda: None)

    layer_stats(nc, c, stats, mean, rstd, eps_t, s_ln, 1)
    s_ln = sem("s_a_ln")
    s_add = sem("s_a_add")
    s_nst = sem("s_a_newstats")
    with nc.Block() as block:
        @block.vector
        def _(dve):
            with dve.Fori(0, TILES // 4) as i:
                for u in range(4):
                    tl = 4 * i + u
                    nc.vector.scalar_tensor_tensor(off[:, u, :], o_all[:, dyn(tl, 1), :], mean[:, dyn(tl, 1)],
                                                   rows[:, 2, :], ALU.subtract, ALU.mult).then_inc(s_ln, 1)
                dve.wait_ge(s_add, 4 * i + 4)
                for u in range(4):
                    tl = 4 * i + u
                    dve.wait_ge(s_ln, tl + 1)
                    nc.vector.scalar_tensor_tensor(h[:, dyn(tl, 1), :], off[:, u, :], rstd[:, dyn(tl, 1)],
                                                   h[:, dyn(tl, 1), :], ALU.mult, ALU.add).then_inc(s_nst, 1)
                for u in range(4):
                    tl = 4 * i + u
                    dve.wait_ge(s_nst, tl + 1)
                    nc.vector.bn_stats(stats[:, dyn(tl, 1), :], h[:, dyn(tl, 1), :])

        @block.gpsimd
        def _(pool):
            with pool.Fori(0, TILES) as tl:
                nc.gpsimd.tensor_tensor(h[:, dyn(tl, 1), :], h[:, dyn(tl, 1), :], rows[:, 3:4, :],
                                        ALU.add).then_inc(s_add, 1)


def routing_phase(nc, c, t, h, mean, rstd, bank, ident, causal, pos, wrow, experts):
    def sb(name, shape, dt=F32):
        return c.enter_context(nc.sbuf_tensor(name, shape, dt))

    def sem(name):
        return c.enter_context(nc.semaphore(name))

    NL = GRP + EXPERTS
    SETS = 1 + GRP
    wr = sb("wr", [P, NL])
    br = sb("br", [P, NL])
    pr = sb("r_prob", [P, TILES, SETS, 4])
    rank = sb("r_rank", [P, TILES, SETS, 4])
    sel = sb("r_sel", [P, TILES, SETS, 4])
    one = sb("r_one", [P, TILES, SETS])
    top = sb("r_top", [P, 3, TILES, SETS])
    c_loop = ExitStack()
    xn = c_loop.enter_context(nc.sbuf_tensor("r_xn", [P, 2, TPG, D], F32))
    xt = c_loop.enter_context(nc.sbuf_tensor("r_xt", [P, 2, GT], F32))
    s_w = sem("s_r_w")
    s_xn, s_xtp, s_xt, s_lp, s_l = (sem("s_r_" + n) for n in ("xn", "xt_p", "xt", "logit_p", "logit"))

    with nc.Block() as block:
        @block.sync
        def _(sp):
            sp.dma_start(wr[:, :], t["wr"]).then_inc(s_w, 16)
            sp.dma_start(br[:, :], t["br"].partition_broadcast(P)).then_inc(s_w, 16)

        @block.vector
        def _(dve):
            dve.sem_inc(s_l, 2)
            dve.wait_ge(s_w, 32)

            def normalise(g, u):
                dve.wait_ge(s_xtp, g + 1)
                for j in range(TPG):
                    ins = nc.vector.tensor_scalar(xn[:, u, j, :], h[:, dyn(g * TPG + j, 1), :],
                                                  mean[:, dyn(g * TPG + j, 1)], rstd[:, dyn(g * TPG + j, 1)],
                                                  ALU.subtract, ALU.mult)
                ins.then_inc(s_xn, 1)

            def add_bias(g, u):
                dve.wait_ge(s_lp, g + 1 + 2)
                nc.vector.tensor_tensor(pr[:, dyn(g * TPG, TPG), :, :],
                                        bank[2 + u][:, 0:TPG * NL].rearrange("p (t s k) -> p t s k", t=TPG, k=4),
                                        br[:, :].rearrange("p (o s k) -> p o s k", o=1, k=4)
                                        .broadcast_to([P, TPG, SETS, 4]), ALU.add).then_inc(s_l, 1)

            run_ahead(dve, normalise, add_bias)

        @block.tensor
        def _(pe):
            pe.sem_inc(s_xtp, 2)
            pe.wait_ge(s_w, 32)

            def transpose(g, u):
                pe.wait_ge(s_xn, g + 1)
                pe.wait_ge(s_xt, g + 1)
                for j in range(TPG):
                    mm = nc.tensor.transpose(bank[u][:, j * P:(j + 1) * P], xn[:, u, j, :], ident[:, :])
                mm.then_inc(s_xtp, 1)

            def logits(g, u):
                pe.wait_ge(s_xt, g + 1 + 2)
                pe.wait_ge(s_l, g + 1)
                for j in range(TPG):
                    mm = nc.tensor.matmul(bank[2 + u][:, j * NL:(j + 1) * NL], xt[:, u, j * P:(j + 1) * P],
                                          wr[:, :], start=(j == 0), stop=True, skip_group_check=True)
                mm.then_inc(s_lp, 1)

            run_ahead(pe, transpose, logits, behind_first=True)

        @block.scalar
        def _(act):
            act.sem_inc(s_xt, 2)
            act.sem_inc(s_lp, 2)
            with act.Fori(0, GROUPS // 2) as i:
                for u in range(2):
                    g = 2 * i + u
                    act.wait_ge(s_xtp, g + 1 + 2)
                    act.wait_ge(s_lp, g + 1)
                    nc.scalar.copy(xt[:, u, :], bank[u][:, :]).then_inc(s_xt, 1)

    c_loop.close()
    tw = sb("r_tw", [P, TILES, EXPERTS])
    mem = sb("r_mem", [P, TILES, SETS, 4])
    gsel = sb("r_gsel", [P, 2, TILES, GRP])
    pair = sb("r_pair", [P, TILES, GRP, PAIRS])
    bk = sb("r_bk", [P, 3, TILES, BUCKETS])
    off = sb("r_off", [P, 2, TILES, BUCKETS])
    base = sb("r_base", [P, 4, BUCKETS])
    strict = sb("r_strict", [P, P])
    ones = sb("r_ones", [P, P])
    wab = sb("r_wab", [P, 3, TILES, GRP])
    posf = sb("r_posf", [P, 2, TILES])
    ends = sb("r_ends", [BUCKETS, 1])
    iota_s = sb("r_iota_s", [BUCKETS, SLOTS])
    delta = sb("r_delta", [BUCKETS, 2])
    s_cnt, s_io, s_te, s_tb, s_de = (sem("s_r_" + n) for n in ("count", "iota", "ends_p", "table_p", "delta"))
    s_v = sem("s_r_chain")
    s_e = sem("s_r_exp")
    with nc.Block() as block:
        @block.scalar
        def _(act):
            act.wait_ge(s_v, 2)
            nc.scalar.activation(pr[:, :, :, :], pr[:, :, :, :], ACT.Exp).then_inc(s_e, 1)

        @block.sync
        def _(sp):
            sp.dma_start(delta[:, :], t["delta"]).then_inc(s_de, 16)

        @block.gpsimd
        def _(pool):
            nc.gpsimd.iota(iota_s[:, :], pattern=[[1, SLOTS]], base=0, channel_multiplier=0,
                           allow_small_or_imprecise_dtypes=True).then_inc(s_io, 1)
            nc.gpsimd.memset(ones[:, :], 1.0).then_inc(s_io, 1)
            nc.gpsimd.tensor_tensor(strict[:, :], causal[:, :], ident[:, :], ALU.subtract).then_inc(s_io, 1)

        @block.tensor
        def _(pe):
            flat = bk[:, 2, :, :].rearrange("p t b -> p (t b)")
            pe.wait_ge(s_io, 3)
            pe.wait_ge(s_cnt, 1)
            for k in range(3):
                nc.tensor.matmul(bank[k][:, :], strict[:, :], flat[:, 512 * k:512 * k + 512], start=True, stop=True)
                mm = nc.tensor.matmul(bank[3 + k][:, :], ones[:, :], flat[:, 512 * k:512 * k + 512], start=True,
                                      stop=True)
            mm.then_inc(s_cnt, 1)
            pe.wait_ge(s_cnt, 3)
            nc.tensor.transpose(bank[6][0:BUCKETS, 0:P], base[:, 1, :], ident[:, :]).then_inc(s_te, 1)
            pe.wait_ge(s_cnt, 4)
            pe.wait_ge(s_de, 16)
            for k in range(2):
                mm = nc.tensor.matmul(bank[7][0:1, k * SLOTS:(k + 1) * SLOTS], delta[:, k:k + 1], iota_s[:, :],
                                      start=True, stop=True)
            mm.then_inc(s_tb, 1)

        @block.vector
        def _(dve):
            count = [0]

            def step(ins):
                count[0] += 1
                ins.then_inc(s_v, 1)
                dve.wait_ge(s_v, count[0])

            def over4(a):
                return a.rearrange("p t (s o) -> p t s o", o=1).broadcast_to([P, TILES, SETS, 4])

            p4, r4, s4 = pr[:, :, :, :], rank[:, :, :, :], sel[:, :, :, :]
            m1, m2, keep = (top[:, k, :, :] for k in range(3))
            step(nc.vector.tensor_reduce(m1, p4, AX.X, ALU.max))
            step(nc.vector.tensor_tensor(p4, p4, over4(m1), ALU.subtract))
            dve.wait_ge(s_e, 1)
            step(nc.vector.tensor_reduce(m1, p4, AX.X, ALU.add))
            step(nc.vector.reciprocal(m1, m1))
            step(nc.vector.tensor_tensor(p4, p4, over4(m1), ALU.mult))
            for k in range(4):
                step(nc.vector.memset(rank[:, :, :, k], float(3 - k)))
            for a in range(4):
                for b in range(a + 1, 4):
                    step(nc.vector.tensor_tensor(one[:, :, :], pr[:, :, :, a], pr[:, :, :, b], ALU.is_ge))
                    step(nc.vector.tensor_tensor(rank[:, :, :, b], rank[:, :, :, b], one[:, :, :], ALU.add))
                    step(nc.vector.tensor_tensor(rank[:, :, :, a], rank[:, :, :, a], one[:, :, :], ALU.subtract))
            step(nc.vector.tensor_scalar(mem[:, :, :, :], r4, 1.0, None, ALU.is_le))
            for k in range(2):
                step(nc.vector.tensor_scalar(gsel[:, k, :, :], rank[:, :, 0, :], float(k), None, ALU.is_equal))
            step(nc.vector.scalar_tensor_tensor(s4.rearrange("p t s k -> p (t s k)"), r4.rearrange("p t s k -> p (t s k)"),
                                                0.0, p4.rearrange("p t s k -> p (t s k)"), ALU.is_equal, ALU.mult))
            step(nc.vector.tensor_reduce(m1, s4, AX.X, ALU.add))
            step(nc.vector.scalar_tensor_tensor(r4.rearrange("p t s k -> p (t s k)"), r4.rearrange("p t s k -> p (t s k)"),
                                                1.0, p4.rearrange("p t s k -> p (t s k)"), ALU.is_equal, ALU.mult))
            step(nc.vector.tensor_reduce(m2, r4, AX.X, ALU.add))
            step(nc.vector.tensor_tensor(keep, m1, m2, ALU.add))
            step(nc.vector.tensor_scalar(keep, keep, TOP_P, None, ALU.is_le))
            step(nc.vector.tensor_tensor(m2, m2, keep, ALU.mult))
            step(nc.vector.tensor_tensor(r4, r4, over4(keep), ALU.mult))
            step(nc.vector.tensor_tensor(r4, r4, s4, ALU.add))
            step(nc.vector.tensor_tensor(m1, m1, m2, ALU.add))
            step(nc.vector.tensor_scalar(m1, m1, 1e-9, None, ALU.add))
            step(nc.vector.reciprocal(m1, m1))
            step(nc.vector.tensor_tensor(r4, r4, over4(m1), ALU.mult))
            step(nc.vector.tensor_tensor(tw[:, :, :].rearrange("p t (g k) -> p t g k", k=4), rank[:, :, 1:SETS, :],
                                         rank[:, :, 0, :].rearrange("p t (g o) -> p t g o", o=1)
                                         .broadcast_to([P, TILES, GRP, 4]), ALU.mult))
            step(nc.vector.tensor_scalar(tw[:, :, :], tw[:, :, :], GRP ** -0.5, None, ALU.mult))
            n = 0
            for a in range(4):
                for b in range(a + 1, 4):
                    step(nc.vector.tensor_tensor(pair[:, :, :, n], mem[:, :, 1:SETS, a], mem[:, :, 1:SETS, b], ALU.mult))
                    n += 1
            for k in range(2):
                step(nc.vector.tensor_tensor(bk[:, k, :, :].rearrange("p t (g m) -> p t g m", g=GRP), pair[:, :, :, :],
                                             gsel[:, k, :, :].rearrange("p t (g o) -> p t g o", o=1)
                                             .broadcast_to([P, TILES, GRP, PAIRS]), ALU.mult))
            step(nc.vector.tensor_tensor(bk[:, 2, :, :], bk[:, 0, :, :], bk[:, 1, :, :], ALU.add))
            dve.sem_inc(s_cnt, 1)
            w4 = tw[:, :, :].rearrange("p t (g k) -> p t g k", k=4)
            out4, wsum = mem, wab[:, 2, :, :]
            step(nc.vector.tensor_scalar(out4[:, :, :, :], mem[:, :, :, :], -1.0, 1.0, ALU.mult, ALU.add))
            for k, (x, y, z) in enumerate(((0, 1, 2), (3, 2, 1))):
                wk = wab[:, k, :, :]
                step(nc.vector.tensor_tensor(wsum, w4[:, :, :, z], out4[:, :, 1:SETS, y], ALU.mult))
                step(nc.vector.tensor_tensor(wsum, wsum, w4[:, :, :, y], ALU.add))
                step(nc.vector.tensor_tensor(wsum, wsum, out4[:, :, 1:SETS, x], ALU.mult))
                step(nc.vector.tensor_tensor(wk, wsum, w4[:, :, :, x], ALU.add))
            for ch in range(2):
                for k in range(2):
                    step(nc.vector.scalar_tensor_tensor(wsum.rearrange("p t g -> p (t g)"),
                                                        wab[:, k, :, :].rearrange("p t g -> p (t g)"), W_HID,
                                                        gsel[:, ch, :, :].rearrange("p t g -> p (t g)"),
                                                        ALU.mult, ALU.mult))
                    step(nc.vector.tensor_reduce(wrow[:, :, ch, k], wsum, AX.X, ALU.add))
            dve.wait_ge(s_cnt, 2)
            for k in range(3):
                step(nc.vector.tensor_copy(off[:, 0, :, :].rearrange("p t b -> p (t b)")[:, 512 * k:512 * k + 512],
                                           bank[3 + k][:, :]))
            a, b, n = 0, 1, 1
            while n < TILES:
                step(nc.vector.tensor_copy(off[:, b, 0:n, :], off[:, a, 0:n, :]))
                step(nc.vector.tensor_tensor(off[:, b, n:TILES, :], off[:, a, n:TILES, :], off[:, a, 0:TILES - n, :],
                                             ALU.add))
                a, b, n = b, a, 2 * n
            total = off[:, a, TILES - 1, :]
            step(nc.vector.tensor_scalar(base[:, 0, :], total, 1.0 / P, 0.5 - 0.5 / P, ALU.mult, ALU.add))
            step(nc.vector.tensor_scalar(base[:, 0, :], base[:, 0, :], ROUND, ROUND, ALU.add, ALU.subtract))
            step(nc.vector.tensor_copy(base[:, 1, :], base[:, 0, :]))
            for m in range(1, BUCKETS):
                step(nc.vector.tensor_tensor(base[:, 1, m:m + 1], base[:, 1, m - 1:m], base[:, 0, m:m + 1], ALU.add))
            dve.sem_inc(s_cnt, 1)
            step(nc.vector.tensor_tensor(base[:, 2, :], base[:, 1, :], base[:, 0, :], ALU.subtract))
            step(nc.vector.tensor_scalar(base[:, 2, :], base[:, 2, :], float(P), None, ALU.mult))
            step(nc.vector.memset(off[:, b, 0, :], 0.0))
            step(nc.vector.tensor_copy(off[:, b, 1:TILES, :], off[:, a, 0:TILES - 1, :]))
            fl = off[:, b, :, :].rearrange("p t b -> p (t b)")
            for k in range(3):
                step(nc.vector.tensor_tensor(fl[:, 512 * k:512 * k + 512], bank[k][:, :], fl[:, 512 * k:512 * k + 512],
                                             ALU.add))
            step(nc.vector.tensor_tensor(off[:, b, :, :], off[:, b, :, :],
                                         base[:, 2:3, :].broadcast_to([P, TILES, BUCKETS]), ALU.add))
            for ch in range(2):
                step(nc.vector.tensor_tensor(off[:, a, :, :], off[:, b, :, :], bk[:, ch, :, :], ALU.mult))
                step(nc.vector.tensor_reduce(posf[:, ch, :], off[:, a, :, :], AX.X, ALU.add))
                step(nc.vector.tensor_copy(pos[:, :, ch], posf[:, ch, :]))
            dve.wait_ge(s_te, 1)
            step(nc.vector.tensor_copy(ends[:, :], bank[6][0:BUCKETS, 0:1]))
            dve.wait_ge(s_io, 3)
            step(nc.vector.tensor_scalar(iota_s[:, :], iota_s[:, :], ends[:, 0:1], None, ALU.is_ge))
            dve.sem_inc(s_cnt, 1)
            dve.wait_ge(s_tb, 1)
            for k in range(2):
                step(nc.vector.tensor_scalar(experts[:, :, k], bank[7][0:1, k * SLOTS:(k + 1) * SLOTS], float(k), None,
                                             ALU.add))


def sorted_ffn_phase(nc, c, t, h, mean, rstd, bank, ident, pos, wrow, experts, x_sorted, y_sorted, s_io, s_rows,
                     s_issue):
    def sb(name, shape, dt=F32):
        return c.enter_context(nc.sbuf_tensor(name, shape, dt))

    def sem(name):
        return c.enter_context(nc.semaphore(name))

    CH = HID // P
    MATS = 3
    w1s, w3s = (sb(n, [P, EXPERTS, 2, HID], F16) for n in ("w1s", "w3s"))
    w2s = sb("w2s", [P, EXPERTS, CH, 2, D], F16)
    row = sb("g_row", [P, TPG, 2, ROW])
    idx = sb("g_idx", [P, TPG, 2], I32)
    c_load = ExitStack()
    stage = c_load.enter_context(nc.sbuf_tensor("w_stage", [P, 2, MATS, HID], F32))

    s_ld = [sem(f"s_g_wload{u}") for u in range(2)]
    s_whi, s_wlo = sem("s_g_w_hi"), sem("s_g_w_lo")
    s_row, s_copy, s_idx = sem("s_g_row"), sem("s_g_copy"), sem("s_g_idx")
    s_sc = s_rows
    s_pd = sem("s_g_pad")
    def hi_lo(e, u, k):
        m = stage[:, u, k, :]
        if k < 2:
            w = (w1s, w3s)[k]
            return w[:, dyn(e, 1), 0, :], w[:, dyn(e, 1), 1, :], m
        w = w2s[:, dyn(e, 1), :, :, :].rearrange("p e c t d -> p (e c) t d")
        return w[:, :, 0, :], w[:, :, 1, :], m.rearrange("p (c d) -> p c d", c=CH)

    with nc.Block() as block:
        @block.sync
        def _(sp):
            with sp.Fori(0, EXPERTS // 2) as i:
                for u in range(2):
                    e = 2 * i + u
                    sp.wait_ge(s_wlo, e + 1)
                    for k, n in enumerate(("w1", "w3", "w2")):
                        src = t[n][dyn(e, 1), :, :].rearrange("e (c p) d -> p (e c) d", p=P)
                        sp.dma_start(stage[:, u, k, :].rearrange("p (c d) -> p c d", c=src.shape[1]), src)\
                            .then_inc(s_ld[u], 16)

        @block.vector
        def _(dve):
            dve.sem_inc(s_wlo, 2)
            dve.wait_ge(s_pd, 1)

            def rows(g, first=False):
                for j in range(TPG):
                    tl = g * TPG + j
                    if not first:
                        dve.wait_ge(s_sc[j], 32 * g)
                    nc.vector.tensor_scalar(row[:, j, 0, 0:D], h[:, dyn(tl, 1), :], mean[:, dyn(tl, 1)],
                                            rstd[:, dyn(tl, 1)], ALU.subtract, ALU.mult).then_inc(s_row, 1)
                    nc.vector.tensor_copy(row[:, j, :, D:D + 2], wrow[:, dyn(tl, 1), :, :]
                                          .rearrange("p t a b -> p (t a) b")).then_inc(s_idx, 1)
                    nc.vector.tensor_copy(idx[:, j, :], pos[:, dyn(tl, 1), :]
                                          .rearrange("p t a -> p (t a)")).then_inc(s_idx, 1)

            def weights_lo(e, u):
                for k in range(MATS):
                    hi, lo, m = hi_lo(e, u, k)
                    dve.wait_ge(s_whi, MATS * e + k + 1)
                    ins = nc.vector.scalar_tensor_tensor(lo, m, W_SCALE, hi, ALU.mult, ALU.subtract)
                ins.then_inc(s_wlo, 1)

            for g in range(2):
                rows(g, first=g == 0)
                weights_lo(g, g)
            with dve.Fori(1, GROUPS // 2) as i:
                for u in range(2):
                    rows(2 * i + u)
                    weights_lo(2 * i + u, u)

        @block.scalar
        def _(act):
            with act.Fori(0, GROUPS // 2) as i:
                for u in range(2):
                    g = 2 * i + u
                    for j in range(TPG):
                        act.wait_ge(s_row, g * TPG + j + 1)
                        nc.scalar.copy(row[:, j, 1, 0:D], row[:, j, 0, 0:D]).then_inc(s_copy, 1)
                    act.wait_ge(s_ld[u], 16 * MATS * (i + 1))
                    for k in range(MATS):
                        hi, _, m = hi_lo(g, u, k)
                        nc.scalar.activation(hi, m, ACT.Copy, scale=W_SCALE).then_inc(s_whi, 1)

        @block.gpsimd
        def _(pool):
            nc.gpsimd.memset(row[:, :, :, D:ROW], 0.0).then_inc(s_pd, 1)
            with pool.Fori(0, GROUPS) as g:
                for j in range(TPG):
                    pool.wait_ge(s_copy, g * TPG + j + 1)
                    pool.wait_ge(s_idx, 2 * (g * TPG + j + 1))
                    pool.sem_inc(s_issue, 1)
                    for k in range(2):
                        nc.gpsimd.indirect_dma_start(
                            out=x_sorted, out_offset=bass.IndirectOffsetOnAxis(ap=idx[:, j, k:k + 1].bitcast(U32), axis=0),
                            in_=row[:, j, k, :], in_offset=None).then_inc(s_sc[j], 16)
            for j in range(TPG):
                pool.wait_ge(s_sc[j], 32 * GROUPS)

    c_load.close()
    SPT = 4
    NU = 2 * SPT
    TURNS = SLOTS // SPT
    xs = sb("g_xs", [P, SPT, ROW])
    xh = sb("g_xh", [P, 2, P], F16)
    xl = sb("g_xl", [P, 2, P], F16)
    gate = sb("g_gate", [P, 2, HID])
    hid = sb("g_hid", [P, 2, HID])
    hh = sb("g_hh", [P, 2, CH, P], F16)
    hl = sb("g_hl", [P, 2, CH, P], F16)
    yb = sb("g_yb", [P, 2, D])
    ys = sb("g_ys", [P, SPT, D])
    S = {n: sem("s_g_" + n) for n in ("xt_p", "xh", "xl", "up", "gate", "hid", "ht_p", "hh", "hl", "y_p", "yb", "ys")}
    s_xs, BASE = s_io, 16
    s_yo = [sem(f"s_g_yout{u}") for u in range(SPT)]
    x_t = x_sorted.rearrange("(s p) d -> s p d", p=P)
    y_t = y_sorted.rearrange("(s p) d -> s p d", p=P)

    with nc.Block() as block:
        @block.sync
        def _(sp):
            def load(i, u, first=False):
                if not first:
                    sp.wait_ge(S["hid"], NU * (i - 1) + 2 * u + 2)
                sp.dma_start(xs[:, u, :], x_t[dyn(SPT * i + u, 1), :, :].rearrange("s p d -> p (s d)"))\
                    .then_inc(s_xs[u], 16)

            def store(i, u):
                sp.wait_ge(S["ys"], SPT * i + u + 1)
                sp.dma_start(y_t[dyn(SPT * i + u, 1), :, :].rearrange("s p d -> p (s d)"), ys[:, u, :])\
                    .then_inc(s_yo[u], 16)

            for u in range(SPT):
                load(0, u, first=True)
            with sp.Fori(1, TURNS) as i:
                for u in range(SPT):
                    load(i, u)
                    store(i - 1, u)
            for u in range(SPT):
                store(TURNS - 1, u)
            for u in range(SPT):
                sp.wait_ge(s_yo[u], 16 * TURNS)

        @block.tensor
        def _(pe):
            def transpose_rows(i, u):
                pe.wait_ge(s_xs[u], BASE + 16 * i + 16)
                nc.tensor.transpose(bank[0][:, 0:P], xs[:, u, 0:D], ident[:, :]).then_inc(S["xt_p"], 1)

            def expert(i, u, k):
                return pe.value_load(experts[0:1, dyn(SPT * i + u, 1), k], min_val=0, max_val=EXPERTS - 1)

            def up(i, u, k, e):
                if k == 0:
                    pe.wait_ge(S["xl"], SPT * i + u + 1)
                for w, b in ((w1s, 1 + k), (w3s, 3 + k)):
                    hi, lo = w[:, dyn(e, 1), 0, :], w[:, dyn(e, 1), 1, :]
                    nc.tensor.matmul(bank[b][:, :], xh[:, u % 2, :], hi, start=True, stop=False)
                    nc.tensor.matmul(bank[b][:, :], xl[:, u % 2, :], hi, start=False, stop=False)
                    mm = nc.tensor.matmul(bank[b][:, :], xh[:, u % 2, :], lo, start=False, stop=True)
                mm.then_inc(S["up"], 1)

            def transpose_hidden(i, u, k):
                v = 2 * (SPT * i + u) + k
                pe.wait_ge(S["hid"], v + 1)
                for m in range(CH):
                    mm = nc.tensor.transpose(bank[5 + k][:, m * P:(m + 1) * P], hid[:, k, m * P:(m + 1) * P],
                                             ident[:, :])
                mm.then_inc(S["ht_p"], 1)

            def down(i, u, k, e, first=False):
                s = SPT * i + u
                pe.wait_ge(S["hl"], 2 * s + k + 1)
                if k == 0 and not (first and u == 0):
                    pe.wait_ge(S["ys"], s)
                y = bank[7][:, 0:2 * D]
                for m in range(CH):
                    both = w2s[:, dyn(e, 1), m, :, :].rearrange("p e t d -> p (e t d)")
                    hi = w2s[:, dyn(e, 1), m, 0, :]
                    start, stop = k == 0 and m == 0, k == 1 and m == CH - 1
                    nc.tensor.matmul(y, hh[:, k, m, :], both, start=start, stop=False)
                    mm = nc.tensor.matmul(y[:, 0:D], hl[:, k, m, :], hi, start=False, stop=stop)
                mm.then_inc(S["y_p"], 1)

            def turn(i, first=False, last=False):
                if first:
                    transpose_rows(0, 0)
                es = {}
                for v in range(NU):
                    es[v] = expert(i, v // 2, v % 2)
                    up(i, v // 2, v % 2, es[v])
                    if v % 2 == 0 and v + 2 < NU:
                        transpose_rows(i, v // 2 + 1)
                    if v + 2 == NU and not last:
                        transpose_rows(i + 1, 0)
                    if not (first and v == 0):
                        w = (v - 1) % NU
                        transpose_hidden(i if v >= 1 else i - 1, w // 2, w % 2)
                    if v >= 2:
                        down(i, v // 2 - 1, v % 2, es[v - 2], first)
                    elif not first:
                        down(i - 1, SPT - 1, v, expert(i - 1, SPT - 1, v))

            turn(0, first=True)
            with pe.Fori(1, TURNS - 1) as i:
                turn(i)
            turn(TURNS - 1, last=True)
            transpose_hidden(TURNS - 1, SPT - 1, 1)
            for k in range(2):
                down(TURNS - 1, SPT - 1, k, expert(TURNS - 1, SPT - 1, k))

        @block.scalar
        def _(act):
            def split_rows(s, u):
                act.wait_ge(S["xt_p"], s + 1)
                nc.scalar.copy(xh[:, u % 2, :], bank[0][:, 0:P]).then_inc(S["xh"], 1)

            def silu(s, k):
                act.wait_ge(S["up"], 2 * s + k + 1)
                nc.scalar.activation(gate[:, k, :], bank[1 + k][:, :], ACT.Silu, scale=1.0 / W_SCALE)\
                    .then_inc(S["gate"], 1)

            def split_hidden(s, k):
                act.wait_ge(S["ht_p"], 2 * s + k + 1)
                nc.scalar.copy(hh[:, k, :, :].rearrange("p c n -> p (c n)"), bank[5 + k][:, :]).then_inc(S["hh"], 1)

            def rows_lo(s, u):
                act.wait_ge(S["y_p"], 2 * s + 2)
                nc.scalar.activation(yb[:, u % 2, :], bank[7][:, D:2 * D], ACT.Copy,
                                     scale=1.0 / (W_SCALE * W_SCALE * W_HID)).then_inc(S["yb"], 1)

            def turn(i, first=False, last=False):
                if first:
                    split_rows(0, 0)
                for v in range(NU):
                    u, k = v // 2, v % 2
                    silu(SPT * i + u, k)
                    if v % 2 == 0 and not (last and v + 2 == NU):
                        split_rows(SPT * i + u + 1, u + 1)
                    if not (first and v == 0):
                        w = (v - 1) % NU
                        split_hidden(SPT * (i if v >= 1 else i - 1) + w // 2, w % 2)
                    if v % 2 == 1 and not (first and v == 1):
                        w = (v // 2 - 1) % SPT
                        rows_lo(SPT * (i if v > 1 else i - 1) + w, w)

            turn(0, first=True)
            with act.Fori(1, TURNS - 1) as i:
                turn(i)
            turn(TURNS - 1, last=True)
            split_hidden(SLOTS - 1, 1)
            rows_lo(SLOTS - 1, SPT - 1)

        @block.vector
        def _(dve):
            def rest_rows(s, u):
                dve.wait_ge(S["xh"], s + 1)
                nc.vector.tensor_tensor(xl[:, u % 2, :], bank[0][:, 0:P], xh[:, u % 2, :], ALU.subtract).then_inc(S["xl"], 1)

            def hidden(s, u, k):
                dve.wait_ge(S["gate"], 2 * s + k + 1)
                nc.vector.scalar_tensor_tensor(hid[:, k, :], bank[3 + k][:, :], xs[:, u, D + k:D + k + 1], gate[:, k, :],
                                               ALU.mult, ALU.mult).then_inc(S["hid"], 1)

            def rest_hidden(s, k):
                dve.wait_ge(S["hh"], 2 * s + k + 1)
                nc.vector.tensor_tensor(hl[:, k, :, :].rearrange("p c n -> p (c n)"), bank[5 + k][:, :],
                                        hh[:, k, :, :].rearrange("p c n -> p (c n)"), ALU.subtract).then_inc(S["hl"], 1)

            def rows_out(i, u, first=False):
                dve.wait_ge(S["yb"], SPT * i + u + 1)
                if not first:
                    dve.wait_ge(s_yo[u], 16 * i)
                nc.vector.scalar_tensor_tensor(ys[:, u, :], bank[7][:, 0:D],
                                               1.0 / (W_SCALE * W_SCALE * W_HID), yb[:, u % 2, :],
                                               ALU.mult, ALU.add).then_inc(S["ys"], 1)

            def turn(i, first=False, last=False, second=False):
                if first:
                    rest_rows(0, 0)
                for v in range(NU):
                    u, k = v // 2, v % 2
                    if v % 2 == 0 and v >= 4:
                        rows_out(i, v // 2 - 2, first)
                    elif v % 2 == 0 and not first:
                        rows_out(i - 1, v // 2 - 2 + SPT, second)
                    hidden(SPT * i + u, u, k)
                    if v % 2 == 0 and not (last and v + 2 == NU):
                        rest_rows(SPT * i + u + 1, u + 1)
                    if not (first and v == 0):
                        w = (v - 1) % NU
                        rest_hidden(SPT * (i if v >= 1 else i - 1) + w // 2, w % 2)

            turn(0, first=True)
            turn(1, second=True)
            with dve.Fori(2, TURNS - 1) as i:
                turn(i)
            turn(TURNS - 1, last=True)
            rows_out(TURNS - 1, SPT - 2)
            rest_hidden(SLOTS - 1, 1)
            rows_out(TURNS - 1, SPT - 1)


def slice_attention_phase(nc, c, t, h, stats, mean, rstd, bank, ident, eps_t, s_ln, turn, pos, y_sorted, s_rows,
                          s_issue):
    def sb(name, shape, dt=F32):
        return c.enter_context(nc.sbuf_tensor(name, shape, dt))

    def sem(name):
        return c.enter_context(nc.semaphore(name))

    H, DH, M = HEADS1, DH1, SLICES
    HM = H * M
    NB = OCTET
    OCT = BATCH // NB
    wx = sb("c_wx", [DH, H, D])
    wsl = sb("c_wsl", [DH, M])
    bx = sb("c_bx", [DH, H])
    bxr = sb("c_bxr", [DH, H, P])
    bsl = sb("c_bsl", [P, M])
    temp = sb("c_temp", [P, 2, H])
    wqkv = sb("c_wqkv", [DH, 3, DH])
    wot = sb("c_wot", [DH, H, D])
    wfx = sb("c_wfx", [P, H, DH])
    bfx = sb("c_bfx", [1, H, DH])
    bo = sb("c_bo", [P, 1, D])
    wl = sb("c_wl", [P, HM])
    folds = sb("c_folds", [DH, DH + H * D])
    wl_h, wl_l = (sb("c_wl" + n, [P, HM], F16) for n in ("h", "l"))
    folds_h, folds_l = (sb("c_folds" + n, [DH, DH + H * D], F16) for n in ("h", "l"))
    wfx_h, wfx_l = (sb("c_wfx" + n, [P, H, DH], F16) for n in ("h", "l"))
    bl = sb("c_bl", [P, 1, HM])
    off_block = sb("c_off", [P, 4, P])

    xn1 = sb("c_xn1", [P, 2, 2, D + 1])
    xh = sb("c_xh", [P, SEQ], F16)
    xl = sb("c_xl", [P, SEQ], F16)
    lg = sb("c_lg", [P, 2 * H, M])
    mx = sb("c_mx", [P, 2 * H])
    sm = sb("c_sm", [P, 2 * H])
    w = sb("c_w", [P, NB, 2, HM])
    dn = sb("c_dn", [P, 2])
    xs = sb("c_xs", [P, 2, D + 1])
    wt = sb("c_wt", [P, NB, 2, SEQ])
    xsth, xstl = (sb("c_xst" + n, [P, NB, H, M], F16) for n in ("h", "l"))
    rt = sb("c_rt", [1, NB, H, M])
    tth, ttl = (sb("c_tt" + n, [DH, NB, H, M], F16) for n in ("h", "l"))
    uth, utl = (sb("c_ut" + n, [DH, NB, H, M], F16) for n in ("h", "l"))
    at = sb("c_at", [P, 4, P])
    amx = sb("c_amx", [P, 4])
    asm = sb("c_asm", [P, 4])
    att = sb("c_att", [P, 4, P])
    vo = sb("c_vo", [P, 4, P])
    os_ = sb("c_os", [P, 4, D])

    idx = sb("c_idx", [P, 2, 2, 2], I32)
    yg = sb("c_yg", [P, 2, 2, 2, D])
    ln_tmp = sb("c_ln_tmp", [P, 3, 2 * NB])
    s_gi, s_ga, s_gb, s_gs = (sem("s_c_" + n) for n in ("gidx", "gsum", "gadd", "gstats"))

    def gather(pool, n, k):
        nc.gpsimd.tensor_copy(idx[:, k % 2, :, :].rearrange("p a c -> p (a c)"),
                              pos[:, dyn(2 * n, 2), :].rearrange("p a c -> p (a c)")).then_inc(s_gi, 1)
        pool.wait_ge(s_gi, n + 1)
        if not isinstance(n, int) or n >= 2:
            pool.wait_ge(s_ga, n - 1)
        pool.sem_inc(s_issue, 1)
        for a in range(2):
            for ch in range(2):
                nc.gpsimd.indirect_dma_start(
                    out=yg[:, k % 2, a, ch, :], out_offset=None, in_=y_sorted,
                    in_offset=bass.IndirectOffsetOnAxis(ap=idx[:, k % 2, a, ch:ch + 1].bitcast(U32), axis=0))\
                    .then_inc(s_rows[2 * (k % 2) + a], 16)

    def add_rows(pool, q, k):
        n = NB * q + k
        for a in range(2):
            pool.wait_ge(s_rows[2 * (k % 2) + a], 32 * GROUPS + 32 * (NB // 2 * q + k // 2 + 1))
        both = yg[:, k % 2, :, :, :]
        nc.gpsimd.tensor_tensor(both[:, :, 0, :], both[:, :, 0, :], both[:, :, 1, :], ALU.add).then_inc(s_ga, 1)
        pool.wait_ge(s_ga, n + 1)
        h2 = h[:, dyn(2 * n, 2), :]
        nc.gpsimd.tensor_tensor(h2, h2, both[:, :, 0, :], ALU.add).then_inc(s_gb, 1)

    def added_stats(dve, n):
        dve.wait_ge(s_gb, n + 1)
        for a in range(2):
            ins = nc.vector.bn_stats(stats[:, dyn(2 * n + a, 1), :], h[:, dyn(2 * n + a, 1), :])
        ins.then_inc(s_gs, 1)

    s_w, s_m, s_k, s_f, s_hi = (sem("s_c_" + n) for n in ("weights", "mask", "setup", "fold", "halves"))
    FOLD = 16.0
    halves = ((wl[:, :], wl_h[:, :], wl_l[:, :], FOLD), (folds[:, :], folds_h[:, :], folds_l[:, :], FOLD),
              (wfx[:, :, :], wfx_h[:, :, :], wfx_l[:, :, :], W_SCALE))
    with nc.Block() as block:
        @block.sync
        def _(sp):
            for dst, name in ((wx[:, :, :], "wx"), (wsl[:, :], "wsl"), (bx[:, :], "bx"), (wqkv[:, :, :], "wqkv1"),
                              (wot[:, :, :], "wot"), (wfx[:, :, :], "wfx"), (bfx[:, :, :], "bfx")):
                sp.dma_start(dst, t[name]).then_inc(s_w, 16)
            sp.dma_start(bsl[:, :], t["bsl"].partition_broadcast(P)).then_inc(s_w, 16)
            sp.dma_start(temp[:, 0, :], t["temp"].partition_broadcast(P)).then_inc(s_w, 16)
            sp.dma_start(bo[:, 0, :], t["bo1"].partition_broadcast(P)).then_inc(s_w, 16)

        @block.gpsimd
        def _(pool):
            nc.gpsimd.memset(off_block[:, :, :], -1e30).then_inc(s_m, 1)
            nc.gpsimd.memset(xn1[:, :, :, :], 1.0).then_inc(s_m, 1)
            pool.wait_ge(s_m, 2)
            for r in range(4):
                nc.gpsimd.memset(off_block[32 * r:32 * r + 32, :, 32 * r:32 * r + 32], 0.0).then_inc(s_m, 1)
            pool.wait_ge(s_m, 6)
            for k in range(NB):
                gather(pool, k, k)
                if k >= 1:
                    add_rows(pool, 0, k - 1)
            add_rows(pool, 0, NB - 1)

        @block.vector
        def _(dve):
            dve.wait_ge(s_w, 160)
            nc.vector.tensor_copy(bxr[:, :, :], bx[:, :].rearrange("p (h o) -> p h o", o=1)
                                  .broadcast_to([DH, H, P])).then_inc(s_k, 1)
            nc.vector.reciprocal(temp[:, 1, :], temp[:, 0, :]).then_inc(s_k, 1)
            dve.wait_ge(s_k, 2)
            inv = temp[:, 1, :].rearrange("p (h o) -> p h o", o=1).broadcast_to([P, H, M])
            dve.wait_ge(s_f, 1)
            nc.vector.tensor_tensor(wl[:, :].rearrange("p (h m) -> p h m", h=H),
                                    bank[0][:, 0:HM].rearrange("p (h m) -> p h m", h=H), inv, ALU.mult).then_inc(s_k, 1)
            nc.vector.tensor_tensor(bl[:, 0, :].rearrange("p (h m) -> p h m", h=H),
                                    bank[1][:, 0:HM].rearrange("p (h m) -> p h m", h=H),
                                    bsl[:, :].rearrange("p (o m) -> p o m", o=1).broadcast_to([P, H, M]),
                                    ALU.add).then_inc(s_k, 1)
            dve.wait_ge(s_k, 4)
            nc.vector.tensor_tensor(bl[:, 0, :].rearrange("p (h m) -> p h m", h=H),
                                    bl[:, 0, :].rearrange("p (h m) -> p h m", h=H), inv, ALU.mult).then_inc(s_k, 1)
            nc.vector.tensor_copy(folds[:, 0:DH], bank[2][0:DH, 0:DH]).then_inc(s_k, 1)
            for k in range(2):
                nc.vector.tensor_copy(folds[:, DH + 4 * k * D:DH + 4 * (k + 1) * D], bank[3 + k][0:DH, :]).then_inc(s_k, 1)
            nc.vector.tensor_scalar(bfx[:, :, :], bfx[:, :, :], W_SCALE, None, ALU.mult).then_inc(s_k, 1)
            dve.wait_ge(s_hi, 3)
            for full, hi, lo, scale in halves:
                nc.vector.scalar_tensor_tensor(lo, full, scale, hi, ALU.mult, ALU.subtract).then_inc(s_k, 1)
            for n in range(NB):
                added_stats(dve, n)

        @block.scalar
        def _(act):
            act.wait_ge(s_k, 9)
            for full, hi, lo, scale in halves:
                nc.scalar.activation(hi, full, ACT.Copy, scale=scale).then_inc(s_hi, 1)

        @block.tensor
        def _(pe):
            pe.wait_ge(s_w, 160)
            pe.wait_ge(s_k, 1)
            for hd in range(H):
                nc.tensor.matmul(bank[0][:, hd * M:(hd + 1) * M], wx[:, hd, :], wsl[:, :], start=True, stop=True)
                nc.tensor.matmul(bank[1][:, hd * M:(hd + 1) * M], bxr[:, hd, :], wsl[:, :], start=True, stop=True)
            nc.tensor.matmul(bank[2][0:DH, 0:DH], wqkv[:, 0, :], wqkv[:, 1, :], start=True, stop=True)
            for k in range(2):
                mm = nc.tensor.matmul(bank[3 + k][0:DH, :], wqkv[:, 2, :],
                                      wot[:, 4 * k:4 * k + 4, :].rearrange("p h d -> p (h d)"), start=True, stop=True)
            mm.then_inc(s_f, 1)

    layer_stats(nc, c, stats, mean, rstd, eps_t, s_ln, turn, tiles=2 * NB)

    names = ("xn", "xt_p", "xh", "xl", "lg_p", "sm1", "chain", "exp", "w", "xs_p", "xs", "xst_p", "xst", "xstl",
             "wt_p", "wt", "tt_p", "tt", "ttl", "ut_p", "ut", "utl", "al_p", "a1", "aexp", "vo_p", "vo", "att_p", "att",
             "asum", "o_p", "o", "bo", "y_p", "y")
    S = {n: sem("s_c_" + n) for n in names}
    NP = NB // 2

    def after(eng, sem, count):
        if not isinstance(count, int) or count > 0:
            eng.wait_ge(sem, count)

    def steps(eng, begin, end, attend, rows, finish, turn_over):
        def octet(q, now, past):
            for k in range(NB + 1):
                if past and k < NB:
                    attend(q - 1, k // 2, k % 2)
                begin(q, k, now and k < NB, past and k < NB, now and k >= 1)
                if past and (k % 2 == 1 and k >= 3 or k == NB):
                    rows(q - 1, (k - 3) // 2 if k < NB else NP - 1)
                if now and k >= 1:
                    end(q, k - 1)
                if past and k < NB:
                    finish(q - 1, k // 2, k % 2)
            if now:
                turn_over(q)

        octet(0, True, False)
        with eng.Fori(1, OCT - 1) as q:
            octet(q, True, True)
        octet(OCT - 1, True, True)
        octet(OCT, False, True)

    with nc.Block() as block:
        @block.tensor
        def _(pe):
            def three(to, pairs):
                (ah, al), (bh, bl_) = pairs
                nc.tensor.matmul(to, ah, bh, start=True, stop=False)
                nc.tensor.matmul(to, ah, bl_, start=False, stop=False)
                return nc.tensor.matmul(to, al, bh, start=False, stop=True)

            def attend(q, p, part):
                n = q * NP + p
                if part == 0:
                    if p == 0:
                        pe.wait_ge(S["utl"], NP * (q + 1))
                    for u in range(4):
                        b, i = 2 * p + u // 2, u % 2
                        hs = slice(4 * i, 4 * i + 4)
                        uu, tt = (tuple(a[:, b, hs, :].rearrange("p h m -> p (h m)") for a in x)
                                  for x in ((uth, utl), (tth, ttl)))
                        mm = three(bank[4][:, u * P:(u + 1) * P], (uu, tt))
                    mm.then_inc(S["al_p"], 1)
                else:
                    pe.wait_ge(S["aexp"], n + 1)
                    for u in range(4):
                        mm = nc.tensor.transpose(bank[6][:, u * P:(u + 1) * P], at[:, u, :], ident[:, :])
                    mm.then_inc(S["att_p"], 1)

            def values(p, us):
                for u in us:
                    b, i = 2 * p + u // 2, u % 2
                    for r in range(4):
                        hd = 4 * i + r
                        at_w = slice(DH + hd * D, DH + (hd + 1) * D)
                        mm = three(bank[5][32 * r:32 * r + 32, u * P:(u + 1) * P],
                                   ((tth[:, b, hd, :], ttl[:, b, hd, :]), (folds_h[:, at_w], folds_l[:, at_w])))
                mm.then_inc(S["vo_p"], 1)

            def begin(q, k, now, past, ending):
                n = q * NB + k
                even = past and k % 2 == 0
                if now:
                    pe.wait_ge(S["xn"], n + 1)
                    for j in range(2):
                        mm = nc.tensor.transpose(bank[0][:, j * P:(j + 1) * P], xn1[:, k % 2, j, 0:D], ident[:, :])
                    mm.then_inc(S["xt_p"], 1)
                if even:
                    values(k // 2, (0, 1))
                if ending:
                    pe.wait_ge(S["w"], n)
                    after(pe, S["xstl"], n - 1)
                    for i in range(2):
                        for j in range(2):
                            mm = nc.tensor.matmul(bank[3][:, i * (D + 1):(i + 1) * (D + 1)],
                                                  w[:, k - 1, j, i * P:(i + 1) * P], xn1[:, (k - 1) % 2, j, :],
                                                  start=(i == 0 and j == 0), stop=(j == 1), skip_group_check=True)
                    mm.then_inc(S["xs_p"], 1)
                if now:
                    pe.wait_ge(S["xl"], n + 1)
                    for j in range(2):
                        at_x = slice(j * P, (j + 1) * P)
                        mm = three(bank[1][:, j * HM:(j + 1) * HM],
                                   ((xh[:, at_x], xl[:, at_x]), (wl_h[:, :], wl_l[:, :])))
                    mm.then_inc(S["lg_p"], 1)
                if even:
                    values(k // 2, (2, 3))

            def finish(q, p, part):
                if part == 1:
                    n = q * NP + p
                    pe.wait_ge(S["att"], n + 1)
                    pe.wait_ge(S["vo"], n + 1)
                    for u in range(4):
                        mm = nc.tensor.matmul(bank[6][:, u * D:(u + 1) * D], att[:, u, :], vo[:, u, :],
                                              start=True, stop=True)
                    mm.then_inc(S["o_p"], 1)

            def rows(q, p):
                n = q * NP + p
                pe.wait_ge(S["o"], n + 1)
                after(pe, S["y"], n)
                for u in range(4):
                    b, j = u // 2, u % 2
                    for i in range(2):
                        mm = nc.tensor.matmul(bank[7][:, u * D:(u + 1) * D],
                                              wt[:, 2 * p + b, i, j * P:(j + 1) * P], os_[:, 2 * b + i, :],
                                              start=(u == 0 and i == 0), stop=(i == 1), skip_group_check=True)
                mm.then_inc(S["y_p"], 1)

            def end(q, k):
                pe.wait_ge(S["xs"], q * NB + k + 1)
                for i in range(2):
                    nc.tensor.transpose(bank[3][:, i * P:(i + 1) * P], xs[:, i, 0:D], ident[:, :])
                    mm = nc.tensor.transpose(bank[3][0:1, 2 * P + i * P:2 * P + (i + 1) * P], xs[:, i, D:D + 1],
                                             ident[:, :])
                mm.then_inc(S["xst_p"], 1)

            def turn_over(q):
                pe.wait_ge(S["xstl"], q * NB + NB)
                for k in range(NB):
                    after(pe, S["ttl"], q * H + k - 1 if k >= 2 else 0)
                    to = bank[k % 2][0:DH, 0:NB * M]
                    nc.tensor.matmul(to, wfx_h[:, k, :], xsth[:, :, k, :], start=True, stop=False)
                    nc.tensor.matmul(to, wfx_h[:, k, :], xstl[:, :, k, :], start=False, stop=False)
                    nc.tensor.matmul(to, wfx_l[:, k, :], xsth[:, :, k, :], start=False, stop=False)
                    nc.tensor.matmul(to, bfx[0:1, k, :], rt[0:1, :, k, :], start=False, stop=True).then_inc(S["tt_p"], 1)
                    after(pe, S["wt"], q * NB + k - 1 if k >= 2 else 0)
                    for i in range(2):
                        for j in range(2):
                            mm = nc.tensor.transpose(bank[2 + 2 * (k % 2)][:, i * SEQ + j * P:i * SEQ + (j + 1) * P],
                                                     w[:, k, j, i * P:(i + 1) * P], ident[:, :])
                    mm.then_inc(S["wt_p"], 1)
                pe.wait_ge(S["ttl"], q * H + H)
                for k in range(NP):
                    after(pe, S["utl"], q * NP + k - 1 if k >= 2 else 0)
                    tt = (a[:, 2 * k:2 * k + 2, :, :].rearrange("p b h m -> p (b h m)") for a in (tth, ttl))
                    three(bank[k % 2][:, :], ((folds_h[:, 0:2 * DH], folds_l[:, 0:2 * DH]), tt)).then_inc(S["ut_p"], 1)
                pe.wait_ge(S["wt"], q * NB + NB)

            steps(pe, begin, end, attend, rows, finish, turn_over)

        @block.scalar
        def _(act):
            def attend(q, p, part):
                n = q * NP + p
                if part == 1:
                    act.wait_ge(S["att_p"], n + 1)
                    nc.scalar.copy(att[:, :, :].rearrange("p u c -> p (u c)"), bank[6][:, :]).then_inc(S["att"], 1)

            def begin(q, k, now, past, ending):
                n = q * NB + k
                if now:
                    act.wait_ge(S["xt_p"], n + 1)
                    nc.scalar.copy(xh[:, :], bank[0][:, 0:SEQ]).then_inc(S["xh"], 1)
                if past and k % 2 == 0:
                    act.wait_ge(S["a1"], (q - 1) * NP + k // 2 + 1)
                    nc.scalar.activation(at[:, :, :], at[:, :, :], ACT.Exp).then_inc(S["aexp"], 1)

            def end(q, k):
                n = q * NB + k
                act.wait_ge(S["xst_p"], n + 1)
                nc.scalar.copy(xsth[:, k, :, :].rearrange("p h m -> p (h m)"), bank[3][:, 0:HM]).then_inc(S["xst"], 1)
                nc.scalar.copy(rt[0:1, k, :, :].rearrange("p h m -> p (h m)"), bank[3][0:1, HM:2 * HM])\
                    .then_inc(S["xst"], 1)
                if k + 1 < NB:
                    exp(q, k + 1)

            def finish(q, p, part):
                if part == 0:
                    act.wait_ge(S["vo_p"], 2 * (q * NP + p) + 2)
                    nc.scalar.activation(vo[:, :, :].rearrange("p u c -> p (u c)"), bank[5][:, :], ACT.Copy,
                                         scale=1.0 / FOLD).then_inc(S["vo"], 1)

            def exp(q, k):
                act.wait_ge(S["sm1"], q * NB + k + 1)
                nc.scalar.activation(lg[:, :, :], lg[:, :, :], ACT.Exp).then_inc(S["exp"], 1)

            def begin_all(q, k, now, past, ending):
                begin(q, k, now, past, ending)
                if k == 0 and now:
                    exp(q, 0)

            def turn_over(q):
                for k in range(NB):
                    act.wait_ge(S["tt_p"], q * H + k + 1)
                    nc.scalar.activation(tth[:, :, k, :], bank[k % 2][0:DH, 0:NB * M].rearrange("p (b m) -> p b m", b=NB),
                                         ACT.Copy, scale=1.0 / W_SCALE).then_inc(S["tt"], 1)
                    act.wait_ge(S["wt_p"], q * NB + k + 1)
                    nc.scalar.copy(wt[:, k, :, :].rearrange("p i s -> p (i s)"), bank[2 + 2 * (k % 2)][:, :])\
                        .then_inc(S["wt"], 1)
                for k in range(NP):
                    act.wait_ge(S["ut_p"], q * NP + k + 1)
                    nc.scalar.activation(uth[:, 2 * k:2 * k + 2, :, :].rearrange("p b h m -> p (b h m)"),
                                         bank[k % 2][0:DH, :], ACT.Copy, scale=1.0 / FOLD).then_inc(S["ut"], 1)
                if not isinstance(q, int) or q < OCT - 1:
                    stats_scalar(nc, act, ln_tmp, eps_t, s_ln, turn + 1 + q)

            steps(act, begin_all, end, attend, lambda q, p: None, finish, turn_over)

        @block.gpsimd
        def _(pool):
            def octet(q, more):
                for k in range(NB):
                    if more:
                        gather(pool, NB * (q + 1) + k, k)
                        if k >= 1:
                            add_rows(pool, q + 1, k - 1)
                    h2 = h[:, dyn((q * NB + k) * 2, 2), :]
                    pool.wait_ge(S["xn"], q * NB + k + 1)
                    nc.gpsimd.tensor_tensor(h2, h2, bo[:, :, :].broadcast_to([P, 2, D]), ALU.add).then_inc(S["bo"], 1)
                if more:
                    add_rows(pool, q + 1, NB - 1)

            octet(0, True)
            with pool.Fori(1, OCT - 1) as q:
                octet(q, True)
            octet(OCT - 1, False)

        @block.vector
        def _(dve):
            def chained(ins, count):
                ins.then_inc(S["chain"], 1)
                dve.wait_ge(S["chain"], count)

            def normalise(q, k):
                n = q * NB + k
                for j in range(2):
                    tl = n * 2 + j
                    ins = nc.vector.tensor_scalar(xn1[:, k % 2, j, 0:D], h[:, dyn(tl, 1), :], mean[:, dyn(tl, 1)],
                                                  rstd[:, dyn(tl, 1)], ALU.subtract, ALU.mult)
                ins.then_inc(S["xn"], 1)

            def softmax_sum(q, k):
                n = q * NB + k
                dve.wait_ge(S["exp"], n + 1)
                chained(nc.vector.tensor_reduce(sm[:, :], lg[:, :, :], AX.X, ALU.add), 6 * n + 3)
                chained(nc.vector.reciprocal(sm[:, :], sm[:, :]), 6 * n + 4)
                nc.vector.tensor_tensor(w[:, k, :, :].rearrange("p t (h m) -> p (t h) m", h=H), lg[:, :, :],
                                        sm[:, :].rearrange("p (g o) -> p g o", o=1)
                                        .broadcast_to([P, 2 * H, M]), ALU.mult).then_inc(S["w"], 1)

            def softmax_max(q, k):
                n = q * NB + k
                dve.wait_ge(S["lg_p"], n + 1)
                chained(nc.vector.scalar_tensor_tensor(lg[:, :, :].rearrange("p (t h) m -> p t (h m)", t=2),
                                                       bank[1][:, :].rearrange("p (t c) -> p t c", t=2), 1.0 / FOLD,
                                                       bl[:, :, :].broadcast_to([P, 2, HM]), ALU.mult, ALU.add),
                        6 * n + 1)
                chained(nc.vector.tensor_reduce(mx[:, :], lg[:, :, :], AX.X, ALU.max), 6 * n + 2)
                nc.vector.tensor_tensor(lg[:, :, :], lg[:, :, :], mx[:, :].rearrange("p (g o) -> p g o", o=1)
                                        .broadcast_to([P, 2 * H, M]), ALU.subtract).then_inc(S["sm1"], 1)

            def rows_lo(q, k):
                dve.wait_ge(S["xh"], q * NB + k + 1)
                nc.vector.tensor_tensor(xl[:, :], bank[0][:, 0:SEQ], xh[:, :], ALU.subtract).then_inc(S["xl"], 1)

            def scale_slices(q, k):
                n = q * NB + k
                dve.wait_ge(S["xs_p"], n + 1)
                xp = bank[3][:, 0:2 * (D + 1)].rearrange("p (i d) -> p i d", i=2)
                chained(nc.vector.tensor_scalar(dn[:, :], xp[:, :, D], LN_EPS, None, ALU.add), 6 * n + 5)
                chained(nc.vector.reciprocal(dn[:, :], dn[:, :]), 6 * n + 6)
                nc.vector.tensor_tensor(xs[:, :, :], xp, dn[:, :].rearrange("p (i o) -> p i o", o=1)
                                        .broadcast_to([P, 2, D + 1]), ALU.mult).then_inc(S["xs"], 1)

            def slices_lo(q, k):
                dve.wait_ge(S["xst"], 2 * (q * NB + k) + 2)
                nc.vector.tensor_tensor(xstl[:, k, :, :].rearrange("p h m -> p (h m)"), bank[3][:, 0:HM],
                                        xsth[:, k, :, :].rearrange("p h m -> p (h m)"), ALU.subtract)\
                    .then_inc(S["xstl"], 1)

            def attend_scores(q, p):
                n = q * NP + p
                dve.wait_ge(S["al_p"], n + 1)
                nc.vector.scalar_tensor_tensor(at[:, :, :].rearrange("p u c -> p (u c)"), bank[4][:, :], DH ** -0.5,
                                               off_block[:, :, :].rearrange("p u c -> p (u c)"),
                                               ALU.mult, ALU.add).then_inc(S["asum"], 1)
                dve.wait_ge(S["asum"], 4 * n + 1)
                nc.vector.tensor_reduce(amx[:, :], at[:, :, :], AX.X, ALU.max).then_inc(S["asum"], 1)
                dve.wait_ge(S["asum"], 4 * n + 2)
                nc.vector.tensor_tensor(at[:, :, :], at[:, :, :], amx[:, :].rearrange("p (u o) -> p u o", o=1)
                                        .broadcast_to([P, 4, P]), ALU.subtract).then_inc(S["a1"], 1)

            def attend_sums(q, p):
                n = q * NP + p
                dve.wait_ge(S["aexp"], n + 1)
                nc.vector.tensor_reduce(asm[:, :], at[:, :, :], AX.X, ALU.add).then_inc(S["asum"], 1)
                dve.wait_ge(S["asum"], 4 * n + 3)
                nc.vector.reciprocal(asm[:, :], asm[:, :]).then_inc(S["asum"], 1)

            def attend_out(q, p):
                n = q * NP + p
                dve.wait_ge(S["o_p"], n + 1)
                dve.wait_ge(S["asum"], 4 * n + 4)
                nc.vector.tensor_tensor(os_[:, :, :], bank[6][:, :].rearrange("p (u c) -> p u c", u=4),
                                        asm[:, :].rearrange("p (u o) -> p u o", o=1).broadcast_to([P, 4, D]),
                                        ALU.mult).then_inc(S["o"], 1)

            def rows(q, p):
                n = q * NP + p
                dve.wait_ge(S["y_p"], n + 1)
                dve.wait_ge(S["bo"], 2 * n + 2)
                h4 = h[:, dyn(4 * n, 4), :]
                nc.vector.tensor_tensor(h4, bank[7][:, :].rearrange("p (u d) -> p u d", u=4), h4, ALU.add)\
                    .then_inc(S["y"], 1)

            def row_stats(q, p):
                n = q * NP + p
                dve.wait_ge(S["y"], n + 1)
                for j in range(4):
                    nc.vector.bn_stats(stats[:, dyn(4 * n + j, 1), :], h[:, dyn(4 * n + j, 1), :])

            def octet(q, now, past, more=False):
                for k in range(NB + 1):
                    if now and k == 0:
                        normalise(q, 0)
                    if now and k >= 1:
                        softmax_sum(q, k - 1)
                    if now and k < NB:
                        rows_lo(q, k)
                    if past and k < NB:
                        (attend_scores if k % 2 == 0 else attend_sums)(q - 1, k // 2)
                    if now and k >= 1:
                        scale_slices(q, k - 1)
                    if now and k < NB:
                        softmax_max(q, k)
                    if now and k >= 1:
                        slices_lo(q, k - 1)
                    if now and k + 1 < NB:
                        normalise(q, k + 1)
                    if past and (k % 2 == 1 and k >= 3 or k == NB):
                        rows(q - 1, (k - 3) // 2 if k < NB else NP - 1)
                    if past and k < NB and k % 2 == 1:
                        attend_out(q - 1, k // 2)
                    if past and (k % 2 == 0 and k >= 4):
                        row_stats(q - 1, k // 2 - 2)
                    if past and k == NB:
                        row_stats(q - 1, NP - 1)
                    if more and k >= 2:
                        added_stats(dve, NB * (q + 1) + k - 2)
                if now:
                    for k in range(NB):
                        dve.wait_ge(S["tt"], q * H + k + 1)
                        nc.vector.scalar_tensor_tensor(
                            ttl[:, :, k, :], bank[k % 2][0:DH, 0:NB * M].rearrange("p (b m) -> p b m", b=NB),
                            1.0 / W_SCALE, tth[:, :, k, :], ALU.mult, ALU.subtract).then_inc(S["ttl"], 1)
                    for k in range(NP):
                        dve.wait_ge(S["ut"], q * NP + k + 1)
                        nc.vector.scalar_tensor_tensor(
                            utl[:, 2 * k:2 * k + 2, :, :].rearrange("p b h m -> p (b h m)"), bank[k % 2][0:DH, :],
                            1.0 / FOLD, uth[:, 2 * k:2 * k + 2, :, :].rearrange("p b h m -> p (b h m)"),
                            ALU.mult, ALU.subtract).then_inc(S["utl"], 1)
                if more:
                    added_stats(dve, NB * (q + 1) + NB - 1)
                    dve.wait_ge(s_gs, NB * (q + 2))
                    stats_vector(nc, dve, stats, mean, rstd, ln_tmp, s_ln, turn + 1 + q, dyn(2 * NB * (q + 1), 2 * NB))
                    dve.wait_ge(s_ln[0], 7 * (turn + 2 + q))

            octet(0, True, False, True)
            with dve.Fori(1, OCT - 1) as q:
                octet(q, True, True, True)
            octet(OCT - 1, True, True)
            octet(OCT, False, True)


def expert_choice_phase(nc, c, t, h, mean, rstd, bank, ident, out):
    def sb(name, shape, dt=F32):
        return c.enter_context(nc.sbuf_tensor(name, shape, dt))

    def sem(name):
        return c.enter_context(nc.semaphore(name))

    E = GATES
    CAP = SEQ // E
    HB = P // E
    wg = sb("d_wg", [P, E])
    we = sb("d_we", [P, E, D])
    weh = sb("d_weh", [P, E, D], F16)
    wel = sb("d_wel", [P, E, D], F16)
    xh = sb("d_xh", [P, TILES, P], F16)
    xl = sb("d_xl", [P, TILES, P], F16)
    ones = sb("d_ones", [P, P])
    xn = sb("d_xn", [P, 2, TPG, D])
    xt = sb("d_xt", [P, 2, GT])
    gate_h = sb("d_gate", [P, 2, BATCH, E])
    gate = gate_h[:, :, :, :].rearrange("p n b e -> p (n b) e")
    rsum = sb("d_rsum", [P, TILES])
    csum = sb("d_csum", [P, BATCH, E])
    gt = sb("d_gt", [P, 2, SEQ])
    wk = sb("d_wk", [P, 2, 2, SEQ])
    top8 = sb("d_top8", [P, 2, 8])
    alive = sb("d_alive", [P, 2, TILES])
    s_w, s_one, s_wh, s_xh, s_xl = (sem("s_d_" + n) for n in ("w", "one", "weights_hi", "xh", "xl"))
    s_xn, s_xtp, s_xt, s_lp, s_l = (sem("s_d_" + n) for n in ("xn", "xt_p", "xt", "logit_p", "logit"))

    with nc.Block() as block:
        @block.sync
        def _(sp):
            sp.dma_start(wg[:, :], t["wg"]).then_inc(s_w, 16)
            sp.dma_start(we[:, :, :], t["we"]).then_inc(s_w, 16)

        @block.gpsimd
        def _(pool):
            nc.gpsimd.memset(ones[:, :], 1.0).then_inc(s_one, 1)

        @block.vector
        def _(dve):
            dve.sem_inc(s_l, 2)
            dve.sem_inc(s_xl, 2)
            dve.wait_ge(s_wh, 1)
            nc.vector.scalar_tensor_tensor(wel[:, :, :], we[:, :, :], W_SCALE, weh[:, :, :], ALU.mult, ALU.subtract)

            def normalise(g, u):
                dve.wait_ge(s_xtp, g + 1)
                for j in range(TPG):
                    ins = nc.vector.tensor_scalar(xn[:, u, j, :], h[:, dyn(g * TPG + j, 1), :],
                                                  mean[:, dyn(g * TPG + j, 1)], rstd[:, dyn(g * TPG + j, 1)],
                                                  ALU.subtract, ALU.mult)
                ins.then_inc(s_xn, 1)

            def clip(g, u):
                dve.wait_ge(s_xh, g + 1)
                nc.vector.tensor_tensor(xl[:, dyn(g * TPG, TPG), :], xt[:, u, :].rearrange("p (j t) -> p j t", j=TPG),
                                        xh[:, dyn(g * TPG, TPG), :], ALU.subtract).then_inc(s_xl, 1)
                dve.wait_ge(s_lp, g + 1 + 2)
                nc.vector.tensor_scalar(gate_h[:, :, dyn(2 * g, 2), :],
                                        bank[2 + u][:, 0:TPG * E].rearrange("p (b n e) -> p n b e", b=2, n=2),
                                        GATE_EPS, None, ALU.max).then_inc(s_l, 1)

            run_ahead(dve, normalise, clip)

        @block.tensor
        def _(pe):
            pe.sem_inc(s_xtp, 2)
            pe.sem_inc(s_lp, 2)
            pe.wait_ge(s_w, 32)

            def transpose(g, u):
                pe.wait_ge(s_xn, g + 1)
                pe.wait_ge(s_xt, g + 1)
                for j in range(TPG):
                    mm = nc.tensor.transpose(bank[u][:, j * P:(j + 1) * P], xn[:, u, j, :], ident[:, :])
                mm.then_inc(s_xtp, 1)

            def logits(g, u):
                pe.wait_ge(s_xt, g + 1 + 2)
                pe.wait_ge(s_l, g + 1)
                for j in range(TPG):
                    mm = nc.tensor.matmul(bank[2 + u][:, j * E:(j + 1) * E], xt[:, u, j * P:(j + 1) * P],
                                          wg[:, :], start=True, stop=True)
                mm.then_inc(s_lp, 1)

            run_ahead(pe, transpose, logits, behind_first=True)

        @block.scalar
        def _(act):
            act.sem_inc(s_xt, 2)
            act.wait_ge(s_w, 32)
            nc.scalar.activation(weh[:, :, :], we[:, :, :], ACT.Copy, scale=W_SCALE).then_inc(s_wh, 1)
            with act.Fori(0, GROUPS // 2) as i:
                for u in range(2):
                    g = 2 * i + u
                    act.wait_ge(s_xtp, g + 1 + 2)
                    act.wait_ge(s_lp, g + 1)
                    act.wait_ge(s_xl, g + 1)
                    nc.scalar.copy(xt[:, u, :], bank[u][:, :]).then_inc(s_xt, 1)
                    act.wait_ge(s_xt, g + 1 + 2)
                    nc.scalar.copy(xh[:, dyn(g * TPG, TPG), :].rearrange("p j t -> p (j t)"), xt[:, u, :]).then_inc(s_xh, 1)

    s_v, s_cp, s_gp, s_bp = sem("s_d_chain"), sem("s_d_col_p"), sem("s_d_gt_p"), sem("s_d_back_p")
    with nc.Block() as block:
        @block.vector
        def _(dve):
            count = [0]

            def step(ins):
                count[0] += 1
                ins.then_inc(s_v, 1)
                dve.wait_ge(s_v, count[0])

            for it in range(SINKHORN):
                dve.wait_ge(s_cp, it + 1)
                step(nc.vector.reciprocal(csum[:, :, :], bank[0][:, 0:BATCH * E].rearrange("p (b e) -> p b e", e=E)))
                step(nc.vector.tensor_tensor(gate_h[:, :, :, :].rearrange("p n b e -> p n (b e)"),
                                             gate_h[:, :, :, :].rearrange("p n b e -> p n (b e)"),
                                             csum[:, :, :].rearrange("p (o b) e -> p o (b e)", o=1)
                                             .broadcast_to([P, 2, BATCH * E]), ALU.mult))
                step(nc.vector.tensor_reduce(rsum[:, :], gate[:, :, :], AX.X, ALU.add))
                step(nc.vector.reciprocal(rsum[:, :], rsum[:, :]))
                step(nc.vector.tensor_tensor(gate[:, :, :], gate[:, :, :],
                                             rsum[:, :].rearrange("p (t o) -> p t o", o=1)
                                             .broadcast_to([P, TILES, E]), ALU.mult))
            dve.wait_ge(s_gp, 1)
            step(nc.vector.tensor_copy(gt[:, :, :].rearrange("p m n -> p (m n)"), bank[1][:, :]))
            for m in range(2):
                src = gt[:, m, :]
                for r in range(CAP // 8):
                    dst = wk[:, m, r % 2, :]
                    step(nc.vector.max(top8[:, m, :], src))
                    step(nc.vector.match_replace(dst, top8[:, m, :], src, -1.0))
                    src = dst
                step(nc.vector.scalar_tensor_tensor(gt[:, m, :], src, 0.0, gt[:, m, :], ALU.is_lt, ALU.mult))
            dve.wait_ge(s_bp, 1)
            for m in range(2):
                for n in range(2):
                    step(nc.vector.tensor_copy(
                        gate_h[:, n, HB * m:HB * (m + 1), :],
                        bank[2][:, (2 * m + n) * P:(2 * m + n + 1) * P].rearrange("p (b e) -> p b e", e=E)))
            step(nc.vector.memset(alive[:, 0, :], 1.0))
            for e in range(E - 1, -1, -1):
                a, b = (E - 1 - e) % 2, (E - e) % 2
                step(nc.vector.scalar_tensor_tensor(alive[:, b, :], gate[:, :, e], 0.0, alive[:, a, :],
                                                    ALU.is_equal, ALU.mult))
                step(nc.vector.tensor_tensor(gate[:, :, e], gate[:, :, e], alive[:, a, :], ALU.mult))

        @block.tensor
        def _(pe):
            pe.wait_ge(s_one, 1)
            for it in range(SINKHORN):
                if it:
                    pe.wait_ge(s_v, 5 * it)
                for n in range(2):
                    mm = nc.tensor.matmul(bank[0][:, 0:BATCH * E], ones[:, :],
                                          gate_h[:, n, :, :].rearrange("p b e -> p (b e)"), start=(n == 0), stop=(n == 1))
                mm.then_inc(s_cp, 1)
            pe.wait_ge(s_v, 5 * SINKHORN)
            for m in range(2):
                for n in range(2):
                    mm = nc.tensor.transpose(bank[1][:, (2 * m + n) * P:(2 * m + n + 1) * P],
                                             gate_h[:, n, HB * m:HB * (m + 1), :].rearrange("p b e -> p (b e)"), ident[:, :])
            mm.then_inc(s_gp, 1)
            pe.wait_ge(s_v, 5 * SINKHORN + 1 + 2 * (2 * (CAP // 8) + 1))
            for m in range(2):
                for n in range(2):
                    mm = nc.tensor.transpose(bank[2][:, (2 * m + n) * P:(2 * m + n + 1) * P],
                                             gt[:, m, n * P:(n + 1) * P], ident[:, :])
            mm.then_inc(s_bp, 1)

    pair_gate = sb("d_pair_gate", [P, 2, 2, E])
    side = sb("d_side", [P, 2, 2, 2, D])
    s_yp, s_pg, s_add = (sem("s_e_" + n) for n in ("y_p", "gates", "add"))
    s_side, SIDE0, s_sum, SUM0 = s_xh, GROUPS, s_xl, GROUPS + 2
    s_out, PARTS = sem("s_out"), 4
    EV = E - 2
    PAIR_ADDS = 2 * EV
    with nc.Block() as block:
        @block.sync
        def _(sp):
            rows = out.rearrange("(t p) d -> p t d", p=P)
            for q in range(PARTS):
                pairs, tiles = BATCH // PARTS, TILES // PARTS
                sp.wait_ge(s_sum, SUM0 + 2 * pairs * (q + 1))
                at = slice(q * tiles, (q + 1) * tiles)
                sp.dma_start(rows[:, at, :], h[:, at, :]).then_inc(s_out, 16)
            sp.wait_ge(s_out, 16 * PARTS)

        @block.vector
        def _(dve):
            def pair(m, u):
                dve.wait_ge(s_yp, m + 1)
                nc.vector.tensor_scalar(pair_gate[:, u, :, :],
                                        gate_h[:, :, dyn(m, 1), :].rearrange("p n b e -> p n (b e)"),
                                        1.0 / W_SCALE, None, ALU.mult).then_inc(s_pg, 1)
                dve.wait_ge(s_pg, m + 1)
                for e in range(EV):
                    if e == 4:
                        dve.wait_ge(s_side, SIDE0 + m + 1)
                    for n in range(2):
                        count = PAIR_ADDS * m + 2 * e + n
                        if e:
                            dve.wait_ge(s_add, count - 1)
                        y = bank[4 * u + 2 * n + e // 4][:, (e % 4) * D:(e % 4 + 1) * D]
                        row = h[:, dyn(2 * m + n, 1), :]
                        nc.vector.scalar_tensor_tensor(row, y, pair_gate[:, u, n, e:e + 1], row,
                                                       ALU.mult, ALU.add).then_inc(s_add, 1)

            with dve.Fori(0, BATCH // 2) as i:
                for u in range(2):
                    pair(2 * i + u, u)

        @block.scalar
        def _(act):
            def pair(m, u, first=False):
                act.wait_ge(s_yp, m + 1)
                act.wait_ge(s_pg, m + 1)
                if not first:
                    act.wait_ge(s_sum, SUM0 + 2 * (m - 1))
                for n in range(2):
                    for e in range(EV, E):
                        y = bank[4 * u + 2 * n + e // 4][:, (e % 4) * D:(e % 4 + 1) * D]
                        ins = nc.scalar.activation(side[:, u, n, e - EV, :], y, ACT.Identity,
                                                   scale=pair_gate[:, u, n, e:e + 1])
                ins.then_inc(s_side, 1)

            for m in range(2):
                pair(m, m, first=True)
            with act.Fori(1, BATCH // 2) as i:
                for u in range(2):
                    pair(2 * i + u, u)

        @block.gpsimd
        def _(pool):
            with pool.Fori(0, BATCH // 2) as i:
                for u in range(2):
                    m = 2 * i + u
                    pool.wait_ge(s_side, SIDE0 + m + 1)
                    nc.gpsimd.tensor_tensor(side[:, u, :, 0, :], side[:, u, :, 0, :], side[:, u, :, 1, :],
                                            ALU.add).then_inc(s_sum, 1)
                    pool.wait_ge(s_sum, SUM0 + 2 * m + 1)
                    pool.wait_ge(s_add, PAIR_ADDS * (m + 1))
                    h2 = h[:, dyn(2 * m, 2), :]
                    nc.gpsimd.tensor_tensor(h2, h2, side[:, u, :, 0, :], ALU.add).then_inc(s_sum, 1)

        @block.tensor
        def _(pe):
            def pair(m, u, first=False):
                if not first:
                    pe.wait_ge(s_add, PAIR_ADDS * (m - 1))
                    pe.wait_ge(s_side, SIDE0 + m - 1)
                for n in range(2):
                    hi, lo = xh[:, dyn(2 * m + n, 1), :], xl[:, dyn(2 * m + n, 1), :]
                    hi, lo = (a.rearrange("p o t -> p (o t)") for a in (hi, lo))
                    for k in range(2):
                        y = bank[4 * u + 2 * n + k][:, :]
                        wh, wl = (a[:, 4 * k:4 * k + 4, :].rearrange("p e d -> p (e d)") for a in (weh, wel))
                        nc.tensor.matmul(y, hi, wh, start=True, stop=False)
                        nc.tensor.matmul(y, hi, wl, start=False, stop=False)
                        mm = nc.tensor.matmul(y, lo, wh, start=False, stop=True)
                mm.then_inc(s_yp, 1)

            for m in range(2):
                pair(m, m, first=True)
            with pe.Fori(1, BATCH // 2) as i:
                for u in range(2):
                    pair(2 * i + u, u)


def kernel(**inputs):
    import numpy as np
    import concourse.bacc as bacc
    from concourse.bass_utils import run_bass_kernel_spmd as run

    nc = bacc.Bacc("TRN2", target_bir_lowering=False, num_devices=1)
    arrays, t = {}, {}

    def give(name, a):
        a = np.ascontiguousarray(a)
        arrays[f"in_{name}"] = a
        t[name] = nc.dram_tensor(f"in_{name}", a.shape, mybir.dt.from_np(a.dtype), kind="ExternalInput").ap()

    x = {k: np.asarray(v) for k, v in inputs.items()}
    give("x", x["x"])
    give("emb", x["L0_tok_emb_weight"])
    give("conv", x["L0_tok_conv_weight"].reshape(D, 2).T)
    wqkv, bqkv = x["L0_attn_Wqkv"], x["L0_attn_bqkv"]
    wqk = np.zeros((D, 4, 4, 32), wqkv.dtype)
    bqk = np.zeros((4, 32, 4), bqkv.dtype)
    lam = np.zeros((4, 32, 2), bqkv.dtype)
    for j in range(4):
        for r in range(4):
            at = (j // 2) * D + (4 * (j % 2) + r) * E0
            wqk[:, j, r, :E0] = wqkv[:, at:at + E0]
            bqk[r, :E0, j] = bqkv[at:at + E0]
            if j < 2:
                lam[r, :E0, j] = x["L0_attn_decay_logits"][4 * j + r]
    give("wqk", wqk.reshape(D, 4, P))
    give("bqk", bqk.reshape(P, 4))
    give("lam", lam.reshape(P, 2))
    give("wv", wqkv[:, 2 * D:])
    give("logits", x["L0_attn_decay_logits"])
    give("wo", x["L0_attn_Wout"])
    give("rows0", np.stack([bqkv[2 * D:], x["L0_attn_bout"], x["L0_attn_ln_gamma"], x["L0_attn_ln_beta"]]))
    give("wr", np.concatenate([x["L0_ffn_Wr"], x["L0_ffn_Wgate"].transpose(1, 0, 2).reshape(D, EXPERTS)], axis=1))
    give("br", np.concatenate([x["L0_ffn_br"], x["L0_ffn_bgate"].reshape(-1)]))
    of = np.array([(4 * g + a, 4 * g + b) for g in range(GRP) for a in range(4) for b in range(a + 1, 4)])
    give("delta", np.concatenate([np.diff(of, axis=0), [[0, 0]]]).astype(np.float32))
    for k in ("w1", "w3", "w2"):
        give(k, x["L0_ffn_" + k.upper()])
    give("wx", x["L1_attn_Wx"].reshape(HEADS1, DH1, D).transpose(1, 0, 2))
    give("bx", x["L1_attn_bx"].reshape(HEADS1, DH1).T)
    give("wsl", x["L1_attn_Wslice"].T)
    give("bsl", x["L1_attn_bslice"])
    give("temp", x["L1_attn_temperature"].reshape(HEADS1))
    give("wqkv1", np.stack([x["L1_attn_Wq"], x["L1_attn_Wk"], x["L1_attn_Wv"]], axis=1))
    give("wot", x["L1_attn_Wout"].T.reshape(HEADS1, DH1, D).transpose(1, 0, 2))
    give("wfx", x["L1_attn_Wfx"].T.reshape(D, HEADS1, DH1))
    give("bfx", x["L1_attn_bfx"].reshape(1, HEADS1, DH1))
    give("bo1", x["L1_attn_bout"])
    give("wg", x["L1_ffn_gate_weight"][0])
    give("we", x["L1_ffn_experts"].transpose(1, 0, 2))
    out = nc.dram_tensor("out_0_dram", (BATCH * SEQ, D), F32, kind="ExternalOutput").ap()
    tower(nc, t, out)
    r = run(nc, [arrays], core_ids=[0])
    return r.results[0]["out_0_dram"].reshape(BATCH, SEQ, D)
```
